# Optimizing a Trainium2 kernel written in Bass

```python
import numpy as np
import jax
import jax.numpy as jnp

def _softmax(x, axis=-1):
    return jax.nn.softmax(x, axis=axis)

def _gelu(x):
    return jax.nn.gelu(x, approximate=True)

def _silu(x):
    return jax.nn.silu(x)

def _sigmoid(x):
    return jax.nn.sigmoid(x)

def _layernorm(x, axis=-1, eps=1e-05):
    m = jnp.mean(x, axis=axis, keepdims=True)
    v = jnp.var(x, axis=axis, keepdims=True)
    return (x - m) / jnp.sqrt(v + eps)

def _scatter_add(tgt, idx, src, axis=0):
    return tgt.at[idx].add(src)

def _segment_sum(src, seg, n):
    return jax.ops.segment_sum(src, seg, n)
kernel_name = 'mk_adaln_d1_jaxref_r4_19ba95'

def setup_inputs(seed: int=0):
    np.random.seed(seed)
    _w = jnp.asarray

    def _L0_attn_setup():
        import jax, jax.numpy as jnp
        import numpy as np
        from jax import lax
        D_MODEL = 512
        D_STATE = 128
        D_CONV = 4
        EXPAND = 2
        HEADDIM = 64
        NGROUPS = 1
        CHUNK = 64
        D_INNER = EXPAND * D_MODEL
        NHEADS = D_INNER // HEADDIM
        CONV_DIM = D_INNER + 2 * NGROUPS * D_STATE
        D_IN_PROJ = 2 * D_INNER + 2 * NGROUPS * D_STATE + NHEADS
        B_SZ = 1
        L_SEQ = 512

        def _segsum_exp(x):
            l = x.shape[-1]
            cs = jnp.cumsum(x, axis=-1)
            diff = cs[..., :, None] - cs[..., None, :]
            mask = jnp.tril(jnp.ones((l, l), dtype=bool))
            return jnp.exp(jnp.where(mask, diff, 0.0)) * mask

        def _ssd(X, A, B, C, block):
            b, l, h, p = X.shape
            c = l // block
            Xb = X.reshape(b, c, block, h, p)
            Ab = A.reshape(b, c, block, h).transpose(0, 3, 1, 2)
            Bb = B.reshape(b, c, block, -1)
            Cb = C.reshape(b, c, block, -1)
            A_cumsum = jnp.cumsum(Ab, axis=-1)
            L = _segsum_exp(Ab)
            Y_diag = jnp.einsum('bcln,bcsn,bhcls,bcshp->bclhp', Cb, Bb, L, Xb)
            decay_states = jnp.exp(A_cumsum[:, :, :, -1:] - A_cumsum)
            states = jnp.einsum('bcln,bhcl,bclhp->bchpn', Bb, decay_states, Xb)
            init = jnp.zeros_like(states[:, :1])
            states = jnp.concatenate([init, states], axis=1)
            chunk_sum = jnp.pad(A_cumsum[:, :, :, -1], ((0, 0), (0, 0), (1, 0)))
            decay_chunk = _segsum_exp(chunk_sum)
            new_states = jnp.einsum('bhzc,bchpn->bzhpn', decay_chunk, states)
            states, final_state = (new_states[:, :-1], new_states[:, -1])
            state_decay_out = jnp.exp(A_cumsum)
            Y_off = jnp.einsum('bcln,bchpn,bhcl->bclhp', Cb, states, state_decay_out)
            Y = (Y_diag + Y_off).reshape(b, l, h, p)
            return (Y, final_state)

        def _forward(u, W_in, W_conv, b_conv, dt_bias, A_log, Dp, norm_w, W_out):
            b, l, _ = u.shape
            zxbcdt = u @ W_in.T
            z = zxbcdt[..., :D_INNER]
            xBC = zxbcdt[..., D_INNER:D_INNER + CONV_DIM]
            dt_raw = zxbcdt[..., D_INNER + CONV_DIM:]
            dt = jax.nn.softplus(dt_raw + dt_bias)
            xBC_t = xBC.transpose(0, 2, 1)
            conv = lax.conv_general_dilated(xBC_t, W_conv, (1,), [(D_CONV - 1, 0)], dimension_numbers=('NCH', 'OIH', 'NCH'), feature_group_count=CONV_DIM)
            xBC = jax.nn.silu(conv + b_conv[None, :, None]).transpose(0, 2, 1)
            x = xBC[..., :D_INNER]
            Bm = xBC[..., D_INNER:D_INNER + NGROUPS * D_STATE]
            Cm = xBC[..., D_INNER + NGROUPS * D_STATE:]
            X = x.reshape(b, l, NHEADS, HEADDIM)
            A = -jnp.exp(A_log)
            Y, _ = _ssd(X, dt * A, Bm, Cm, CHUNK)
            y = Y + Dp[None, None, :, None] * X
            y = y.reshape(b, l, D_INNER)
            y = y * jax.nn.silu(z)
            y = y * lax.rsqrt(jnp.mean(y * y, axis=-1, keepdims=True) + 1e-05) * norm_w
            return y @ W_out.T
        key = jax.random.key(seed)
        ks = jax.random.split(key, 8)
        u = jax.random.normal(ks[0], (B_SZ, L_SEQ, D_MODEL), jnp.float32)
        W_in = jax.random.normal(ks[1], (D_IN_PROJ, D_MODEL), jnp.float32) * D_MODEL ** (-0.5)
        W_conv = jax.random.normal(ks[2], (CONV_DIM, 1, D_CONV), jnp.float32) * 0.2
        b_conv = jax.random.normal(ks[3], (CONV_DIM,), jnp.float32) * 0.02
        dt_bias = jax.random.normal(ks[4], (NHEADS,), jnp.float32) * 0.5 - 4.0
        A_log = jax.random.uniform(ks[5], (NHEADS,), jnp.float32, minval=0.0, maxval=2.0)
        Dp = jnp.ones((NHEADS,), jnp.float32)
        norm_w = jnp.ones((D_INNER,), jnp.float32)
        W_out = jax.random.normal(ks[6], (D_MODEL, D_INNER), jnp.float32) * D_INNER ** (-0.5)
        return {'u': u, 'W_in': W_in, 'W_conv': W_conv, 'b_conv': b_conv, 'dt_bias': dt_bias, 'A_log': A_log, 'Dp': Dp, 'norm_w': norm_w, 'W_out': W_out}
    _L0_attn_in = _L0_attn_setup()

    def _L0_ffn_setup():
        import jax, jax.numpy as jnp
        import numpy as np
        DIM = 512
        HID = 1408
        ZERO_POINT = 128.0

        def _qlinear(x, wq, scale):
            W = (wq.astype(jnp.float32) - ZERO_POINT) * scale[:, None]
            return jnp.einsum('bsd,hd->bsh', x, W)
        key = jax.random.key(seed)
        ks = jax.random.split(key, 7)
        B, S = (4, 512)
        sg = jax.random.uniform(ks[1], (HID,)) * (0.02 / np.sqrt(DIM)) + 0.0001
        su = jax.random.uniform(ks[3], (HID,)) * (0.02 / np.sqrt(DIM)) + 0.0001
        sd = jax.random.uniform(ks[5], (DIM,)) * (0.02 / np.sqrt(HID)) + 0.0001
        return {'x': jax.random.normal(ks[0], (B, S, DIM), dtype=jnp.float32), 'wq_gate': jax.random.randint(ks[2], (HID, DIM), 0, 64, dtype=jnp.int32), 's_gate': sg, 'wq_up': jax.random.randint(ks[4], (HID, DIM), 0, 64, dtype=jnp.int32), 's_up': su, 'wq_down': jax.random.randint(ks[6], (DIM, HID), 0, 64, dtype=jnp.int32), 's_down': sd}
    _L0_ffn_in = _L0_ffn_setup()
    _L0_c = _w((lambda *s: np.random.randn(*s).astype(np.float32) * 0.05)(2, 512))
    _L0_wmod = _w((lambda *s: np.random.randn(*s).astype(np.float32) * 0.05)(512, 6 * 512) * 512 ** (-0.5))
    _d = {'L0_attn_u': _L0_attn_in['u'], 'L0_attn_W_in': _L0_attn_in['W_in'], 'L0_attn_W_conv': _L0_attn_in['W_conv'], 'L0_attn_b_conv': _L0_attn_in['b_conv'], 'L0_attn_dt_bias': _L0_attn_in['dt_bias'], 'L0_attn_A_log': _L0_attn_in['A_log'], 'L0_attn_Dp': _L0_attn_in['Dp'], 'L0_attn_norm_w': _L0_attn_in['norm_w'], 'L0_attn_W_out': _L0_attn_in['W_out'], 'L0_ffn_wq_gate': _L0_ffn_in['wq_gate'], 'L0_ffn_s_gate': _L0_ffn_in['s_gate'], 'L0_ffn_wq_up': _L0_ffn_in['wq_up'], 'L0_ffn_s_up': _L0_ffn_in['s_up'], 'L0_ffn_wq_down': _L0_ffn_in['wq_down'], 'L0_ffn_s_down': _L0_ffn_in['s_down'], 'L0_c': _L0_c, 'L0_wmod': _L0_wmod}
    _x0 = _d['L0_attn_u']
    _d['L0_attn_u'] = jax.random.normal(jax.random.fold_in(jax.random.key(seed), 1), (2, 2048, 512), dtype=_x0.dtype)
    del _x0
    return _d

def reference(L0_attn_u, L0_attn_W_in, L0_attn_W_conv, L0_attn_b_conv, L0_attn_dt_bias, L0_attn_A_log, L0_attn_Dp, L0_attn_norm_w, L0_attn_W_out, L0_ffn_wq_gate, L0_ffn_s_gate, L0_ffn_wq_up, L0_ffn_s_up, L0_ffn_wq_down, L0_ffn_s_down, L0_c, L0_wmod):

    def _L0_attn_ref(u, W_in, W_conv, b_conv, dt_bias, A_log, Dp, norm_w, W_out):
        import jax, jax.numpy as jnp
        import numpy as np
        from jax import lax
        D_MODEL = 512
        D_STATE = 128
        D_CONV = 4
        EXPAND = 2
        HEADDIM = 64
        NGROUPS = 1
        CHUNK = 64
        D_INNER = EXPAND * D_MODEL
        NHEADS = D_INNER // HEADDIM
        CONV_DIM = D_INNER + 2 * NGROUPS * D_STATE
        D_IN_PROJ = 2 * D_INNER + 2 * NGROUPS * D_STATE + NHEADS
        B_SZ = 1
        L_SEQ = 512

        def _segsum_exp(x):
            l = x.shape[-1]
            cs = jnp.cumsum(x, axis=-1)
            diff = cs[..., :, None] - cs[..., None, :]
            mask = jnp.tril(jnp.ones((l, l), dtype=bool))
            return jnp.exp(jnp.where(mask, diff, 0.0)) * mask

        def _ssd(X, A, B, C, block):
            b, l, h, p = X.shape
            c = l // block
            Xb = X.reshape(b, c, block, h, p)
            Ab = A.reshape(b, c, block, h).transpose(0, 3, 1, 2)
            Bb = B.reshape(b, c, block, -1)
            Cb = C.reshape(b, c, block, -1)
            A_cumsum = jnp.cumsum(Ab, axis=-1)
            L = _segsum_exp(Ab)
            Y_diag = jnp.einsum('bcln,bcsn,bhcls,bcshp->bclhp', Cb, Bb, L, Xb)
            decay_states = jnp.exp(A_cumsum[:, :, :, -1:] - A_cumsum)
            states = jnp.einsum('bcln,bhcl,bclhp->bchpn', Bb, decay_states, Xb)
            init = jnp.zeros_like(states[:, :1])
            states = jnp.concatenate([init, states], axis=1)
            chunk_sum = jnp.pad(A_cumsum[:, :, :, -1], ((0, 0), (0, 0), (1, 0)))
            decay_chunk = _segsum_exp(chunk_sum)
            new_states = jnp.einsum('bhzc,bchpn->bzhpn', decay_chunk, states)
            states, final_state = (new_states[:, :-1], new_states[:, -1])
            state_decay_out = jnp.exp(A_cumsum)
            Y_off = jnp.einsum('bcln,bchpn,bhcl->bclhp', Cb, states, state_decay_out)
            Y = (Y_diag + Y_off).reshape(b, l, h, p)
            return (Y, final_state)

        def _forward(u, W_in, W_conv, b_conv, dt_bias, A_log, Dp, norm_w, W_out):
            b, l, _ = u.shape
            zxbcdt = u @ W_in.T
            z = zxbcdt[..., :D_INNER]
            xBC = zxbcdt[..., D_INNER:D_INNER + CONV_DIM]
            dt_raw = zxbcdt[..., D_INNER + CONV_DIM:]
            dt = jax.nn.softplus(dt_raw + dt_bias)
            xBC_t = xBC.transpose(0, 2, 1)
            conv = lax.conv_general_dilated(xBC_t, W_conv, (1,), [(D_CONV - 1, 0)], dimension_numbers=('NCH', 'OIH', 'NCH'), feature_group_count=CONV_DIM)
            xBC = jax.nn.silu(conv + b_conv[None, :, None]).transpose(0, 2, 1)
            x = xBC[..., :D_INNER]
            Bm = xBC[..., D_INNER:D_INNER + NGROUPS * D_STATE]
            Cm = xBC[..., D_INNER + NGROUPS * D_STATE:]
            X = x.reshape(b, l, NHEADS, HEADDIM)
            A = -jnp.exp(A_log)
            Y, _ = _ssd(X, dt * A, Bm, Cm, CHUNK)
            y = Y + Dp[None, None, :, None] * X
            y = y.reshape(b, l, D_INNER)
            y = y * jax.nn.silu(z)
            y = y * lax.rsqrt(jnp.mean(y * y, axis=-1, keepdims=True) + 1e-05) * norm_w
            return y @ W_out.T
        return _forward(u, W_in, W_conv, b_conv, dt_bias, A_log, Dp, norm_w, W_out)

    def _L0_ffn_ref(x, wq_gate, s_gate, wq_up, s_up, wq_down, s_down):
        import jax, jax.numpy as jnp
        import numpy as np
        DIM = 512
        HID = 1408
        ZERO_POINT = 128.0

        def _qlinear(x, wq, scale):
            W = (wq.astype(jnp.float32) - ZERO_POINT) * scale[:, None]
            return jnp.einsum('bsd,hd->bsh', x, W)
        gate = _qlinear(x, wq_gate, s_gate)
        gate = jax.nn.silu(gate)
        up = _qlinear(x, wq_up, s_up)
        return _qlinear(gate * up, wq_down, s_down)
    x = L0_attn_u
    mod = (_silu(L0_c) @ L0_wmod).reshape(L0_c.shape[0], 6, 1, -1)
    sa, ca, ga, sb, cb, gb = (mod[:, 0], mod[:, 1], mod[:, 2], mod[:, 3], mod[:, 4], mod[:, 5])
    ga = (2 * (ga >= 0) - 1) * jnp.maximum(jnp.abs(ga), 0.25)
    gb = (2 * (gb >= 0) - 1) * jnp.maximum(jnp.abs(gb), 0.25)
    h = _layernorm(x, axis=-1) * (1 + ca) + sa
    x = x + ga * _L0_attn_ref(h, L0_attn_W_in, L0_attn_W_conv, L0_attn_b_conv, L0_attn_dt_bias, L0_attn_A_log, L0_attn_Dp, L0_attn_norm_w, L0_attn_W_out)
    h = _layernorm(x, axis=-1) * (1 + cb) + sb
    x = x + gb * _L0_ffn_ref(h, L0_ffn_wq_gate, L0_ffn_s_gate, L0_ffn_wq_up, L0_ffn_s_up, L0_ffn_wq_down, L0_ffn_s_down)
    return x

_drawn_inputs = setup_inputs


def setup_inputs(seed=0):
    import zlib

    import numpy as np

    out = dict(_drawn_inputs(seed))
    spreads = {'L0_attn_Dp': (1.0, 0.578), 'L0_attn_norm_w': (1.0, 0.2)}
    factors = {'L0_ffn_s_gate': 8.0, 'L0_ffn_s_up': 8.0, 'L0_ffn_s_down': 8.0}
    for name, (base, spread) in spreads.items():
        noise = np.random.default_rng([zlib.crc32(name.encode()), seed]).standard_normal(out[name].shape)
        drawn = base * np.exp(spread * noise) if base else spread * noise
        out[name] = jnp.asarray(drawn.astype(out[name].dtype))
    for name, factor in factors.items():
        out[name] = (out[name] * factor).astype(out[name].dtype)
    return out
```

```python
from contextlib import ExitStack

import concourse.bass as bass
from concourse import mybir

F32 = mybir.dt.float32
FR = mybir.dt.float32r
I32 = mybir.dt.int32
ALU = mybir.AluOpType
ACT = mybir.ActivationFunctionType
AX_X = mybir.AxisListType.X

P = 128
EPS = 1e-5
FLOOR = 0.25
ZERO_POINT = 128.0
EXACT_INT = 4096.0


def count(n, per, c):
    if isinstance(n, tuple):
        i, a, b = n
        return i * (a * per) + (b * per + c)
    return n * per + c


def before(n):
    return (n[0], n[1], n[2] - 1) if isinstance(n, tuple) else n - 1


def after(n):
    return (n[0], n[1], n[2] + 1) if isinstance(n, tuple) else n + 1


def wait(eng, sem, n, per, c):
    v = count(n, per, c)
    if isinstance(v, int) and v <= 0:
        return
    eng.wait_ge(sem, v)


def wait_apart(eng, sem, n, per, c):
    v = count(n, per, c)
    if isinstance(v, int):
        wait(eng, sem, n, per, c)
        return
    v = eng.snap(eng.to_reg(v))
    eng.wait_ge(sem, 1)
    eng.wait_ge(sem, v)


def start_token(n, size):
    if isinstance(n, tuple):
        i, a, b = n
        return i * size + (b // 2) * size
    return (n // 2) * size


class Tensors:
    pass


def setup_stage(nc, T, A):
    D, DI, CD, H = T.D, T.DI, T.CD, T.H
    KD, KI = D // P, DI // P
    NIN = T.NIN
    with ExitStack() as ctx:
        sem = lambda name: ctx.enter_context(nc.semaphore(name))
        params_in, wout_in = sem("params_in"), sem("wout_in")
        mod_in, win_in = ([sem(f"{s}{j}") for j in range(2)] for s in ("mod_in", "win_in"))
        silu_c_done, spread_done = sem("silu_c_done"), sem("spread_done")
        cols_done, cols_read = sem("cols_done"), sem("cols_read")
        rows_done, row_step = sem("rows_done"), sem("row_step")
        win_high, win_low, const_step = sem("win_high"), sem("win_low"), sem("const_step")
        a_done, a_read = sem("a_done"), sem("a_read")
        gate2_ready, gate2_out = sem("gate2_ready"), sem("gate2_out")
        stage = [A.xc[b][:, :, :].rearrange("p m t -> p (m t)")[:, 0:NIN] for b in range(2)]
        wm = [A.L[c][:, :, :].rearrange("p (k x) l -> p k (x l)", k=KD) for c in range(2)]
        cT, sc = A.cT, A.sc
        scb = A.X[:, :].rearrange("p (k b t) -> p k b t", k=KD, b=2)
        sdown = A.yt[:, 0:D]
        w_mod = T.wmod.rearrange("(k p) (s n) -> s p k n", p=P, s=6)
        w_in = T.winT.rearrange("(k p) n -> k p n", p=P)
        COLS = {0: 0, 1: 1, 3: 2, 4: 3}
        ROWS = {2: 0, 5: 1}

        with nc.Block() as block:

            @block.sync
            def _(sp):
                with nc.allow_non_contiguous_dma(reason="small parameters"):
                    sp.dma_start(cT[:], T.cT.rearrange("(k p) b -> p k b", p=P)).then_inc(params_in, 16)
                    sp.dma_start(A.wconv[:], T.wconv.rearrange("(m p) o k -> p m (o k)", p=P)).then_inc(params_in, 16)
                    sp.dma_start(A.bconv[:], T.bconv.rearrange("(m p) -> p m", p=P)).then_inc(params_in, 16)
                    sp.dma_start(A.normw[:], T.normw.rearrange("(m p) -> p m", p=P)).then_inc(params_in, 16)
                    for row, src in ((A.dtb, T.dtb), (A.negA, T.alog), (A.Drow, T.Dp), (sdown, T.sdown)):
                        sp.dma_start(row[:] if row is not sdown else row,
                                     src.rearrange("(a h) -> a h", a=1).broadcast_to([P, src.shape[0]])).then_inc(params_in, 16)
                    for w, src in ((T.sgate, T.sgate_in), (T.sup, T.sup_in)):
                        sp.dma_start(w[:], src.rearrange("(m p) -> p m", p=P)).then_inc(params_in, 16)
                for s in range(2):
                    sp.dma_start(wm[s], w_mod[s]).then_inc(mod_in[s], 16)
                for k in range(2):
                    sp.dma_start(stage[k], w_in[k]).then_inc(win_in[k], 16)
                for s in range(2, 6):
                    if s - 2 in COLS:
                        sp.wait_ge(cols_done, COLS[s - 2] + 1)
                    else:
                        sp.wait_ge(rows_done, ROWS[s - 2] + 1)
                    sp.dma_start(wm[s % 2], w_mod[s]).then_inc(mod_in[s % 2], 16)
                    if s < 4:
                        sp.wait_ge(win_low, s - 1)
                        sp.dma_start(stage[s % 2], w_in[s]).then_inc(win_in[s % 2], 16)
                sp.dma_start(A.Wo[:], T.woutT.rearrange("(k p) n -> p k n", p=P)).then_inc(wout_in, 16)
                sp.wait_ge(gate2_ready, 2)
                for b in range(2):
                    sp.dma_start(T.gate2_d[b:b + 1, :], A.siluz[0:1, b, 0:D]).then_inc(gate2_out, 16)
                sp.wait_ge(gate2_out, 32)

            @block.gpsimd
            def _(pool):
                nc.gpsimd.memset(A.ident[:], 0.0).then_inc(const_step, 1)
                nc.gpsimd.memset(A.triu[:], 1.0).then_inc(const_step, 1)
                nc.gpsimd.memset(T.neg_half[:], -0.5).then_inc(const_step, 1)
                nc.gpsimd.memset(A.ones[:], 1.0).then_inc(const_step, 1)
                pool.wait_ge(const_step, 4)
                nc.gpsimd.affine_select(out=A.ident[:], in_=A.ident[:], compare_op=ALU.not_equal, fill=1.0,
                                        base=0, pattern=[[-1, P]], channel_multiplier=1).then_inc(const_step, 1)
                nc.gpsimd.affine_select(out=A.triu[:], in_=A.triu[:], compare_op=ALU.is_ge, fill=0.0,
                                        base=0, pattern=[[1, P]], channel_multiplier=-1).then_inc(const_step, 1)
                for b in range(2):
                    nc.gpsimd.memset(A.S[b][:], 0.0).then_inc(const_step, 1)
                    nc.gpsimd.memset(A.tail[b][:], 0.0).then_inc(const_step, 1)
                nc.gpsimd.memset(A.raw[:], 0.0).then_inc(const_step, 1)

            @block.scalar
            def _(act):
                act.wait_ge(params_in, 160)
                nc.scalar.activation(sc[:], cT[:], ACT.Silu).then_inc(silu_c_done, 1)
                nc.scalar.activation(A.negA[:], A.negA[:], ACT.Exp).then_inc(a_done, 1)
                for k in range(KD):
                    act.wait_ge(win_in[k % 2], 16 * (k // 2 + 1))
                    nc.scalar.activation(A.Whi[:, k, :], stage[k % 2], ACT.Copy).then_inc(win_high, 1)

            @block.vector
            def _(dve):
                dve.wait_ge(silu_c_done, 1)
                nc.vector.tensor_copy(scb, sc[:].unsqueeze(3).broadcast_to([P, KD, 2, P])).then_inc(spread_done, 1)
                dve.wait_ge(a_done, 1)
                nc.vector.tensor_scalar(A.negA[:], A.negA[:], -1.0, None, ALU.mult).then_inc(a_read, 1)

                def low(k):
                    dve.wait_ge(win_high, k + 1)
                    nc.vector.tensor_tensor(A.Wlo[:, k, :], stage[k % 2], A.Whi[:, k, :].bitcast(F32),
                                            ALU.subtract).then_inc(win_low, 1)

                for s in range(6):
                    if s in COLS:
                        i = COLS[s]
                        dve.wait_ge(cols_done, i + 1)
                        nc.vector.tensor_scalar(T.modc[:, i], A.psum[0][:, 0:2 * KD].rearrange("p (k b) -> p k b", b=2),
                                                float(s in (1, 4)), None, ALU.add).then_inc(cols_read, 1)
                    else:
                        i = ROWS[s]
                        dve.wait_ge(rows_done, i + 1)
                        for b in range(2):
                            g = A.siluz[:, b, 0:D] if i else T.gate_row[b][:]
                            t, m = A.XD[:, 0:D], A.XD[:, D:2 * D]
                            o = 4 * (2 * i + b)
                            if o:
                                dve.wait_ge(row_step, o)
                            nc.vector.tensor_scalar(t, A.psum[1 + b][:], 0.0, 2.0, ALU.is_ge, ALU.mult).then_inc(row_step, 1)
                            dve.wait_ge(row_step, o + 1)
                            nc.vector.tensor_scalar(t, t, -1.0, None, ALU.add).then_inc(row_step, 1)
                            dve.wait_ge(row_step, o + 2)
                            nc.vector.tensor_tensor(m, A.psum[1 + b][:], t, ALU.mult).then_inc(row_step, 1)
                            dve.wait_ge(row_step, o + 3)
                            nc.vector.scalar_tensor_tensor(g, m, FLOOR, t, ALU.max, ALU.mult).then_inc(row_step, 1)
                            if i:
                                dve.wait_ge(row_step, o + 4)
                                nc.vector.tensor_tensor(g, g, sdown, ALU.mult).then_inc(gate2_ready, 1)
                    if s < KD:
                        low(s)
                dve.wait_ge(wout_in, 16)
                for k in range(KI):
                    nc.vector.tensor_scalar(A.Wo[:, k, :], A.Wo[:, k, :], A.normw[:, k:k + 1], None,
                                            ALU.mult).then_inc(a_read, 1)
                dve.wait_ge(a_read, 1 + KI)

            @block.tensor
            def _(pe):
                pe.wait_ge(spread_done, 1)
                for s in range(6):
                    pe.wait_ge(mod_in[s % 2], 16 * (s // 2 + 1))
                    if s in COLS:
                        i = COLS[s]
                        if i:
                            pe.wait_ge(cols_read, i)
                        for k in range(KD):
                            for q in range(KD):
                                mm = nc.tensor.matmul(A.psum[0][:, 2 * k:2 * k + 2], wm[s % 2][:, q, k * P:(k + 1) * P],
                                                      sc[:, q, :], start=(q == 0), stop=(q == KD - 1))
                        mm.then_inc(cols_done, 1)
                    else:
                        i = ROWS[s]
                        if i:
                            pe.wait_ge(row_step, 8)
                        for b in range(2):
                            for q in range(KD):
                                mm = nc.tensor.matmul(A.psum[1 + b][:], scb[:, q, b, :], wm[s % 2][:, q, :],
                                                      start=(q == 0), stop=(q == KD - 1))
                        mm.then_inc(rows_done, 1)


def mixer_stage(nc, T, A):
    D, DI, H, HD = T.D, T.DI, T.H, T.HD
    KD, KI = D // P, DI // P
    MX = T.CD // P
    SC, NC = T.SC, T.SC // P
    N = 2 * T.S // SC
    HH = H // 2
    W = HH * HD
    SP_STEPS = 17
    T_USES, A_USES = 12, 18
    DT0, X0 = DI, DI + H
    ZQ = T.ZQ
    Z = DI - ZQ
    with ExitStack() as ctx:
        sem = lambda name: ctx.enter_context(nc.semaphore(name))
        resid_in, cs_out = sem("resid_in"), sem("cs_out")
        x_in, cs_in, x1_out = ([sem(f"{s}{c}") for c in range(NC)] for s in ("x_in", "cs_in", "x1_out"))
        cs_done, G_done = sem("cs_done"), sem("G_done")
        a_filled, a_emptied = sem("a_filled"), sem("a_emptied")
        t_filled, t_emptied = sem("t_filled"), sem("t_emptied")
        yoff_done, ydiag_done, state_done = sem("yoff_done"), sem("ydiag_done"), sem("state_done")
        silu_done, siluq_done, e3_done, edt_done, decay_done, sq_done = (
            sem(s) for s in ("silu_done", "siluq_done", "e3_done", "edt_done", "decay_done", "sq_done"))
        stats_step, normed, split, conv_step, softplus_step, sums_step = (
            sem(s) for s in ("stats_step", "normed", "split", "conv_step", "softplus_step", "sums_step"))
        tail_step, diff_done, G_masked, M_done, Xdec_done = (
            sem(s) for s in ("tail_step", "diff_done", "G_masked", "M_done", "Xdec_done"))
        yoff_read, ydiag_read, S_step = sem("yoff_read"), sem("ydiag_read"), sem("S_step")
        rstd_step, XD_done, y_summed, gated, rs_step, out_step = (
            sem(s) for s in ("rstd_step", "XD_done", "y_summed", "gated", "rs_step", "out_step"))

        accs, tps = A.psum[0:2], A.psum[2:4]
        small, yoff, ydiag, state = A.psum[4:8]
        x_d, x1_d = T.x, T.x1
        hT = (A.hThi, A.hTlo)
        h32 = A.XD[:, :].rearrange("p (k t) -> p k t", k=KD)
        Win = (A.Whi, A.Wlo)
        PARTS = ((0, 0), (0, 1), (1, 0))

        A_ORDER = [("zdt", 0), ("zdt", 1)] + [("m", m) for m in range(8)] + [("out", 0)] + \
                  [("m", m) for m in range(8, MX)] + [("z", j) for j in range(4)] + [("out", 1)]
        T_ORDER = [("x", 0, 0), ("x", 0, 1), ("x", 0, 2), ("x", 1, 0), ("x", 1, 1), ("x", 1, 2),
                   ("g", 0, 0), ("g", 0, 1), ("g", 1, 0), ("g", 1, 1), ("ln", 0), ("ln", 1)]

        def a_slot(n, key):
            if n == 0:
                return [k for k in A_ORDER if k[0] != "out"].index(key), 0
            order = A_ORDER if n != N else [k for k in A_ORDER if k[0] == "out"]
            return order.index(key), -2

        def a_wait(eng, sem_, n, key, back):
            r, off = a_slot(n, key)
            wait(eng, sem_, n, A_USES, off + r + back)
            return accs[r % 2]

        def t_slot(n, key):
            if n == -1:
                return key[1], 0, 0
            if n == 0:
                return key[1], 2, 0
            order = T_ORDER if not (isinstance(n, int) and n >= N - 1) else [k for k in T_ORDER if k[0] != "ln"]
            return order.index(key), -8 - (2 if n == N else 0), n

        def t_wait(eng, sem_, n, key, back):
            r, off, m = t_slot(n, key)
            wait(eng, sem_, m, T_USES, off + r + back)
            return tps[(r + off) % 2]

        block = ctx.enter_context(nc.Block())

        def turns(engine, prologue, turn):
            prologue()
            for n in range(3):
                turn(n, n % 2)
            pairs = (N - 1 - 3) // 2
            with engine.Fori(0, pairs) as i:
                turn((i, 2, 3), 1)
                turn((i, 2, 4), 0)
            for n in range(3 + 2 * pairs, N + 1):
                turn(n, n % 2)

        def has_own(n):
            return not (isinstance(n, int) and n == N)

        def has_before(n):
            return not (isinstance(n, int) and n == 0)

        def has_next(n):
            return not (isinstance(n, int) and n >= N - 1)

        @block.sync
        def _(sp):
            def rows(t, b, n, c):
                return t[b][bass.ds(start_token(n, SC) + c * P, P), :]

            def load_x(n, b):
                if n != 0:
                    r, off, m = t_slot(-1 if n == 1 else before(before(n)), ("ln", 1))
                    wait_apart(sp, t_filled, m, T_USES, off + r + 1)
                for c in range(NC):
                    sp.dma_start(A.xl[c][:], rows(x_d, b, n, c)).then_inc(x_in[c], 16)

            def prologue():
                load_x(0, 0)

            def turn(n, b):
                u = before(n)
                if has_next(n):
                    load_x(after(n), 1 - b)
                if has_before(n):
                    for c in range(NC):
                        wait_apart(sp, x1_out[c], u, 16, 0)
                        sp.dma_start(A.xr[c][:], rows(x_d, 1 - b, u, c)).then_inc(resid_in, 16)
                if has_own(n):
                    wait_apart(sp, sums_step, n, 3, 3)
                    for c in range(NC):
                        wait_apart(sp, cs_in[c], u, 16, 16)
                    sp.dma_start(T.cs_d.rearrange("c h l -> h c l"), A.csT[:]).then_inc(cs_out, 16)
                    wait_apart(sp, cs_out, n, 16, 16)
                for c in range(NC):
                    if has_own(n):
                        wait_apart(sp, ydiag_done, u, 2 * NC, 2 * (c + 1))
                        sp.dma_start(A.L[c][:].rearrange("p h l -> p (h l)"),
                                     T.cs_d[c].rearrange("h l -> (h l)").rearrange("(a x) -> a x", a=1)
                                     .broadcast_to([P, H * P])).then_inc(cs_in[c], 16)
                    if has_before(n):
                        wait_apart(sp, out_step, u, 2 * NC, 2 * (c + 1))
                        sp.dma_start(rows(x1_d, 1 - b, u, c), A.xr[c][:]).then_inc(x1_out[c], 16)

            turns(sp, prologue, turn)
            for c in range(NC):
                sp.wait_ge(x1_out[c], N * 16)

        @block.gpsimd
        def _(pool):
            def rstd(n):
                for c in range(NC):
                    wait(pool, stats_step, n, 2 * NC, 2 * (c + 1))
                    wait_apart(pool, normed, before(n), NC, c + 1)
                    nc.gpsimd.tensor_scalar(A.rstd[:, c:c + 1], A.mv[c][:, 1:2], 1.0, EPS, ALU.mult, ALU.add) \
                        .then_inc(rstd_step, 1)
                    wait(pool, rstd_step, n, 2 * NC, 2 * c + 1)
                    nc.gpsimd.tensor_tensor(A.rstd[:, c:c + 1], A.rstd[:, c:c + 1], T.neg_half[:], ALU.pow) \
                        .then_inc(rstd_step, 1)

            def times_D(n, u, c):
                t_wait(pool, t_emptied, n, ("x", c, 1), 1)
                wait(pool, sq_done, u, NC, c)
                if c == 0 and has_own(n):
                    wait(pool, split, n, 2 * NC, 2 * NC)
                nc.gpsimd.tensor_tensor(A.XD[:].rearrange("p (h d) -> p h d", h=H),
                                        A.X[:].rearrange("p (h d) -> p h d", h=H),
                                        A.Drow[:].unsqueeze(2).broadcast_to([P, H, HD]), ALU.mult).then_inc(XD_done, 1)

            def gate(n, u, b, c):
                wait(pool, yoff_read, u, 2 * NC, 2 * c + 2)
                wait(pool, ydiag_read, u, 2 * NC, 2 * c + 2)
                nc.gpsimd.tensor_tensor(A.yt[:], A.yt[:], A.XD[:], ALU.add).then_inc(y_summed, 1)
                wait(pool, y_summed, u, NC, c + 1)
                a_wait(pool, a_emptied, u, ("z", 2 * c + 1), 1)
                nc.gpsimd.tensor_tensor(A.yt[:, 0:Z], A.yt[:, 0:Z], A.siluz[:, c, :], ALU.mult)
                wait(pool, siluq_done, u, 1, 1)
                nc.gpsimd.tensor_tensor(A.yt[:, Z:], A.yt[:, Z:], A.zdt[1 - b][:, c, 0:ZQ], ALU.mult).then_inc(gated, 1)

            def inv_rms(n, u, c):
                if u != 0:
                    r, off = a_slot(u, ("out", c))
                    wait_apart(pool, a_emptied, u, A_USES, off + r + 1)
                wait_apart(pool, sq_done, u, NC, c + 1)
                nc.gpsimd.tensor_scalar(A.rs[:, c:c + 1], A.ssq[:, c:c + 1], 1.0 / DI, EPS, ALU.mult, ALU.add) \
                    .then_inc(rs_step, 1)
                wait(pool, rs_step, u, 2 * NC, 2 * c + 1)
                nc.gpsimd.tensor_tensor(A.rs[:, c:c + 1], A.rs[:, c:c + 1], T.neg_half[:], ALU.pow).then_inc(rs_step, 1)

            def residual(n, u, b, c):
                a_wait(pool, a_emptied, n, ("out", c), 1)
                nc.gpsimd.tensor_tensor(A.ob[:], A.ob[:], T.gate_row[1 - b][:], ALU.mult).then_inc(out_step, 1)
                wait(pool, out_step, u, 2 * NC, 2 * c + 1)
                wait(pool, resid_in, u, NC * 16, NC * 16)
                nc.gpsimd.tensor_tensor(A.xr[c][:], A.ob[:], A.xr[c][:], ALU.add).then_inc(out_step, 1)

            def turn(n, b):
                u = before(n)
                own, bef, nxt = has_own(n), has_before(n), has_next(n)
                if bef:
                    times_D(n, u, 0)
                    gate(n, u, b, 0)
                    inv_rms(n, u, 0)
                    times_D(n, u, 1)
                if nxt:
                    rstd(after(n))
                if bef:
                    residual(n, u, b, 0)
                    gate(n, u, b, 1)
                    inv_rms(n, u, 1)
                    residual(n, u, b, 1)

            turns(pool, lambda: rstd(0), turn)

        @block.scalar
        def _(act):
            def evac_ln(n, b, turn_n):
                for j in range(2):
                    ps = t_wait(act, t_filled, turn_n, ("ln", j), 1)
                    if j == 0 and turn_n != -1:
                        wait(act, sq_done, before(turn_n), NC, NC)
                    for q in range(2):
                        k = 2 * j + q
                        last = nc.scalar.activation(h32[:, k, :], ps[:, q * SC:(q + 1) * SC], ACT.Identity,
                                                    bias=T.modc[:, 0, k, b:b + 1], scale=T.modc[:, 1, k, b:b + 1])
                    last.then_inc(t_emptied, 1)

            def evac_tile(n, key):
                m = key[1]
                ps = a_wait(act, a_filled, n, key, 1)
                b = nb[0]
                wait(act, tail_step, n, 2, 0)
                wait(act, yoff_done, before(n), 2 * NC, 0)
                nc.scalar.activation(A.raw[:, m, 3:3 + SC], ps[:, 0:SC], ACT.Copy)
                nc.scalar.activation(A.xc[b][:, m, :], ps[:, 0:SC], ACT.Identity, bias=A.bconv[:, m:m + 1],
                                     scale=A.wconv[:, m, 3:4]).then_inc(a_emptied, 1)

            def silu_tile(n, m):
                wait(act, conv_step, n, 3 * MX, 3 * (m + 1))
                x = A.xc[nb[0]][:, m, :]
                nc.scalar.activation(x, x, ACT.Silu).then_inc(silu_done, 1)

            def silu_z(n, j):
                ps = a_wait(act, a_filled, n, ("z", j), 1)
                c, f = divmod(j, 2)
                e = min((f + 1) * W, Z)
                wait(act, gated, n, NC, c + 1 - NC)
                nc.scalar.activation(A.siluz[:, c, f * W:e], ps[:, 0:e - f * W], ACT.Silu).then_inc(a_emptied, 1)

            def evac_zdt(n, b, c):
                ps = a_wait(act, a_filled, n, ("zdt", c), 1)
                if c == 0:
                    wait(act, gated, before(n), NC, 0)
                    wait(act, softplus_step, before(n), SP_STEPS, 0)
                nc.scalar.activation(A.zdt[b][:, c, :], ps[:, 0:ZQ + H], ACT.Copy).then_inc(a_emptied, 1)

            def silu_q(n, b):
                a_wait(act, a_emptied, n, ("zdt", 1), 1)
                z = A.zdt[b][:, :, 0:ZQ]
                nc.scalar.activation(z, z, ACT.Silu).then_inc(siluq_done, 1)

            def evac_x(n, u, c):
                for f in range(2):
                    ps = t_wait(act, t_filled, n, ("x", c, f), 1)
                    if f == 0:
                        wait(act, ydiag_done, u, 2 * NC, 2 * c)
                        wait(act, state_done, u, 2 * NC, 2 * c)
                        wait(act, Xdec_done, u, NC, c)
                        wait(act, XD_done, u, NC, c)
                    nc.scalar.activation(A.X[:, f * W:(f + 1) * W], ps[:, 0:W], ACT.Copy).then_inc(t_emptied, 1)
                ps = t_wait(act, t_filled, n, ("x", c, 2), 1)
                nc.scalar.activation(A.Btok[:], ps[:, 0:P], ACT.Copy).then_inc(t_emptied, 1)

            def evac_g(n, u, c):
                for f in range(2):
                    ps = t_wait(act, t_filled, n, ("g", c, f), 1)
                    if f == 0:
                        if c:
                            a_wait(act, a_filled, n, ("out", 0), 1)
                        elif u != 0:
                            a_wait(act, a_filled, u, ("out", 1), 1)
                    nc.scalar.activation(A.gT[:, 4 * f:4 * f + 4, :].rearrange("p k t -> p (k t)"), ps[:, 0:W],
                                         ACT.Copy).then_inc(t_emptied, 1)

            def exp_sums(u):
                wait(act, sums_step, u, 3, 3)
                wait(act, S_step, u, 4 * NC, 0)
                wait(act, Xdec_done, u, NC, 0)
                wait(act, yoff_read, u, 2 * NC, 0)
                nc.scalar.activation(A.e3[:], A.s3[:], ACT.Exp).then_inc(e3_done, 1)

            def exp_decay(u, c, f):
                wait(act, diff_done, u, 2 * NC, 2 * c + f + 1)
                x = A.L[c][:, f * HH:(f + 1) * HH, :]
                nc.scalar.activation(x, x, ACT.Exp).then_inc(decay_done, 1)

            def exp_dt(n):
                wait(act, softplus_step, n, SP_STEPS, 2)
                nc.scalar.activation(A.sp[1][:], A.sp[1][:], ACT.Exp).then_inc(edt_done, 1)

            def square(u, c):
                wait(act, gated, u, NC, c + 1)
                wait(act, rs_step, u, 2 * NC, 2 * c + 2 - 2 * NC)
                nc.scalar.activation(A.XD[:], A.yt[:], ACT.Square, accum_out=A.ssq[:, c:c + 1]).then_inc(sq_done, 1)

            def scale_out(n, u, c):
                ps = a_wait(act, a_filled, n, ("out", c), 1)
                wait(act, rs_step, u, 2 * NC, 2 * c + 2)
                wait(act, out_step, u, 2 * NC, 2 * c)
                nc.scalar.activation(A.ob[:], ps[:], ACT.Identity, scale=A.rs[:, c:c + 1]).then_inc(a_emptied, 1)

            nb = [0]

            def turn(n, b):
                nb[0] = b
                u = before(n)
                own, bef, nxt = has_own(n), has_before(n), has_next(n)
                if own:
                    evac_zdt(n, b, 0)
                if bef:
                    evac_x(n, u, 0)
                if own:
                    evac_zdt(n, b, 1)
                    evac_tile(n, ("m", 0))
                    exp_dt(n)
                    evac_tile(n, ("m", 1))
                    evac_tile(n, ("m", 2))
                    evac_tile(n, ("m", 3))
                if bef:
                    evac_x(n, u, 1)
                if own:
                    evac_tile(n, ("m", 4))
                    evac_tile(n, ("m", 5))
                    evac_tile(n, ("m", 6))
                if bef:
                    square(u, 0)
                    evac_g(n, u, 0)
                if own:
                    evac_tile(n, ("m", 7))
                    silu_tile(n, 0)
                    silu_q(n, b)
                    silu_tile(n, 1)
                    silu_tile(n, 2)
                if bef:
                    scale_out(n, u, 0)
                if own:
                    silu_tile(n, 3)
                    evac_tile(n, ("m", 8))
                    silu_tile(n, 4)
                    evac_tile(n, ("m", 9))
                    silu_tile(n, 5)
                    silu_z(n, 0)
                    silu_tile(n, 6)
                    silu_z(n, 1)
                if bef:
                    square(u, 1)
                if own:
                    silu_z(n, 2)
                if bef:
                    evac_g(n, u, 1)
                if own:
                    silu_tile(n, 7)
                    silu_z(n, 3)
                if nxt:
                    evac_ln(after(n), 1 - b, n)
                if own:
                    silu_tile(n, 8)
                    silu_tile(n, 9)
                    exp_sums(n)
                    exp_decay(n, 0, 0)
                    exp_decay(n, 0, 1)
                    exp_decay(n, 1, 0)
                    exp_decay(n, 1, 1)
                if bef:
                    scale_out(n, u, 1)

            turns(act, lambda: evac_ln(0, 0, -1), turn)

        @block.vector
        def _(dve):
            def stats(n, c):
                wait(dve, x_in[c], n, 16, 16)
                wait(dve, rstd_step, n, 2 * NC, 2 * c + 2 - 2 * NC)
                wait(dve, normed, before(n), NC, c + 1)
                wait(dve, stats_step, n, 2 * NC, 2 * c + 2 - 2 * NC)
                nc.vector.bn_stats(A.bst[c][:], A.xl[c][:]).then_inc(stats_step, 1)
                wait_apart(dve, stats_step, n, 2 * NC, 2 * c + 1)
                nc.vector.bn_aggr(A.mv[c][:], A.bst[c][:]).then_inc(stats_step, 1)

            def norm(n, turn_n, c):
                wait(dve, rstd_step, n, 2 * NC, 2 * c + 2)
                nc.vector.tensor_scalar(A.xl[c][:], A.xl[c][:], A.mv[c][:, 0:1], A.rstd[:, c:c + 1],
                                        ALU.subtract, ALU.mult).then_inc(normed, 1)

            def split_h(n, turn_n, c):
                t_wait(dve, t_emptied, turn_n, ("ln", 1), 1)
                if turn_n != -1:
                    a_wait(dve, a_filled, turn_n, ("z", 3), 1)
                wait(dve, split, n, 2 * NC, 2 * c)
                s = slice(c * P, (c + 1) * P)
                h = h32[:, :, s]
                nc.vector.tensor_copy(A.hThi[:, :, s], h).then_inc(split, 1)
                wait(dve, split, n, 2 * NC, 2 * c + 1)
                nc.vector.tensor_tensor(A.hTlo[:, :, s], h, A.hThi[:, :, s].bitcast(F32),
                                        ALU.subtract).then_inc(split, 1)

            def conv(n, b, m):
                a_wait(dve, a_emptied, n, ("m", m), 1)
                for j in range(3):
                    if j:
                        wait(dve, conv_step, n, 3 * MX, 3 * m + j)
                    nc.vector.scalar_tensor_tensor(A.xc[b][:, m, :], A.raw[:, m, j:j + SC], A.wconv[:, m, j:j + 1],
                                                   A.xc[b][:, m, :], ALU.mult, ALU.add).then_inc(conv_step, 1)

            def tails(n, b):
                wait(dve, conv_step, n, 3 * MX, 3 * MX)
                wait(dve, tail_step, n, 2, 0)
                nc.vector.tensor_copy(A.tail[b][:], A.raw[:, :, SC:SC + 3]).then_inc(tail_step, 1)
                nc.vector.tensor_copy(A.raw[:, :, 0:3], A.tail[1 - b][:]).then_inc(tail_step, 1)

            sp0, sp1, sp2, sp3, sp4, sp5 = A.sp

            def dt_first(n, b):
                a_wait(dve, a_emptied, n, ("zdt", 1), 1)
                wait(dve, softplus_step, n, SP_STEPS, 0)
                nc.vector.tensor_tensor(sp0[:], A.zdt[b][:, :, ZQ:ZQ + H],
                                        A.dtb[:].unsqueeze(1).broadcast_to([P, NC, H]), ALU.add) \
                    .then_inc(softplus_step, 1)
                wait(dve, softplus_step, n, SP_STEPS, 1)
                nc.vector.scalar_tensor_tensor(sp1[:], sp0[:], -1.0, sp0[:], ALU.mult, ALU.min).then_inc(softplus_step, 1)

            def softplus(n):
                wait(dve, edt_done, n, 1, 1)
                step = [2]

                def did(ins):
                    ins.then_inc(softplus_step, 1)
                    step[0] += 1
                    wait(dve, softplus_step, n, SP_STEPS, step[0])

                did(nc.vector.tensor_scalar(sp2[:], sp1[:], 2.0, None, ALU.add))
                did(nc.vector.reciprocal(sp2[:], sp2[:]))
                did(nc.vector.tensor_tensor(sp3[:], sp1[:], sp2[:], ALU.mult))
                did(nc.vector.tensor_tensor(sp4[:], sp3[:], sp3[:], ALU.mult))
                did(nc.vector.tensor_scalar(sp5[:], sp4[:], 1.0 / 15.0, None, ALU.mult))
                for k in (13, 11, 9, 7, 5, 3):
                    did(nc.vector.scalar_tensor_tensor(sp5[:], sp5[:], 1.0 / k, sp4[:], ALU.add, ALU.mult))
                did(nc.vector.scalar_tensor_tensor(sp5[:], sp5[:], 1.0, sp3[:], ALU.add, ALU.mult))
                did(nc.vector.tensor_scalar(sp0[:], sp0[:], 0.0, None, ALU.max))
                did(nc.vector.scalar_tensor_tensor(sp5[:], sp5[:], 2.0, sp0[:], ALU.mult, ALU.add))
                nc.vector.tensor_tensor(A.a[:], sp5[:], A.negA[:].unsqueeze(1).broadcast_to([P, NC, H]),
                                        ALU.mult).then_inc(softplus_step, 1)

            def sums(n):
                wait(dve, cs_done, n, 1, 1)
                wait(dve, e3_done, n, 1, 0)
                wait(dve, cs_out, n, 16, 0)
                wait(dve, diff_done, n, 2 * NC, 0)
                nc.vector.tensor_copy(A.s3[:, 0:2 * NC * H], small[:, 0:2 * NC * H]).then_inc(sums_step, 1)
                wait(dve, sums_step, n, 3, 1)
                nc.vector.tensor_tensor(A.s3[:, 2 * NC * H:3 * NC * H], A.s3[:, NC * H:2 * NC * H],
                                        A.s3[:, 0:NC * H], ALU.subtract).then_inc(sums_step, 1)
                nc.vector.tensor_copy(A.csT[:].rearrange("h c l -> h (c l)"), small[0:H, 2 * P:2 * P + NC * P]) \
                    .then_inc(sums_step, 1)

            def diff(u, c, f):
                if f == 0:
                    wait(dve, cs_in[c], u, 16, 16)
                    wait(dve, sums_step, u, 3, 3)
                for h in range(f * HH, (f + 1) * HH):
                    last = nc.vector.tensor_scalar(A.L[c][:, h, :], A.L[c][:, h, :], A.s3[:, c * H + h:c * H + h + 1],
                                                   0.0, ALU.subtract, ALU.min)
                last.then_inc(diff_done, 1)

            def mask_G(u):
                wait(dve, G_done, u, 1, 1)
                wait(dve, M_done, u, 2 * NC, 0)
                nc.vector.tensor_tensor(A.Gm[:], small[:, 0:NC * P].rearrange("p (c l) -> p c l", c=NC),
                                        A.triu[:].unsqueeze(1).broadcast_to([P, NC, P]), ALU.mult).then_inc(G_masked, 1)

            def scores(u, c, f):
                if c == 0 and f == 0:
                    wait(dve, G_masked, u, 1, 1)
                wait(dve, decay_done, u, 2 * NC, 2 * c + f + 1)
                x = A.L[c][:, f * HH:(f + 1) * HH, :]
                nc.vector.tensor_tensor(x, x, A.Gm[:, c, :].unsqueeze(1).broadcast_to([P, HH, P]), ALU.mult) \
                    .then_inc(M_done, 1)

            def e3(kind, c, f):
                o = kind * NC * H + c * H + f * HH
                return A.e3[:, o:o + HH].unsqueeze(2).broadcast_to([P, HH, HD])

            def heads(x, f):
                return x[:, f * W:(f + 1) * W].rearrange("p (h d) -> p h d", h=HH)

            def decay_X(n, u, c):
                t_wait(dve, t_emptied, n, ("x", c, 1), 1)
                wait(dve, e3_done, u, 1, 1)
                wait(dve, state_done, u, 2 * NC, 2 * c)
                o = 2 * NC * H + c * H
                nc.vector.tensor_tensor(A.Xd[:].rearrange("p (h d) -> p h d", h=H),
                                        A.X[:].rearrange("p (h d) -> p h d", h=H),
                                        A.e3[:, o:o + H].unsqueeze(2).broadcast_to([P, H, HD]),
                                        ALU.mult).then_inc(Xdec_done, 1)

            def read_yoff(n, u, b, c, f):
                wait(dve, yoff_done, u, 2 * NC, 2 * c + f + 1)
                if f == 0:
                    if c:
                        t_wait(dve, t_filled, n, ("g", 0, 1), 1)
                    elif u != 0:
                        t_wait(dve, t_filled, u, ("g", 1, 1), 1)
                    wait(dve, sq_done, u, NC, c)
                    wait(dve, e3_done, u, 1, 1)
                nc.vector.tensor_tensor(heads(A.yt, f), yoff[:, 0:W].rearrange("p (h d) -> p h d", h=HH), e3(0, c, f),
                                        ALU.mult).then_inc(yoff_read, 1)
                nc.vector.tensor_tensor(heads(A.S[1 - b], f), heads(A.S[1 - b], f), e3(1, c, f),
                                        ALU.mult).then_inc(S_step, 1)

            def read_ydiag(u, c, f):
                wait(dve, ydiag_done, u, 2 * NC, 2 * c + f + 1)
                wait(dve, XD_done, u, NC, c + 1)
                nc.vector.tensor_tensor(A.XD[:, f * W:(f + 1) * W], ydiag[:, 0:W], A.XD[:, f * W:(f + 1) * W],
                                        ALU.add).then_inc(ydiag_read, 1)

            def read_state(u, b, c, f):
                wait(dve, state_done, u, 2 * NC, 2 * c + f + 1)
                wait(dve, S_step, u, 4 * NC, 4 * c + 2)
                s = A.S[1 - b][:, f * W:(f + 1) * W]
                nc.vector.tensor_tensor(s, state[:, 0:W], s, ALU.add).then_inc(S_step, 1)

            def prologue():
                for c in range(NC):
                    stats(0, c)
                for c in range(NC):
                    norm(0, -1, c)
                for c in range(NC):
                    split_h(0, -1, c)

            def turn(n, b):
                u = before(n)
                own, bef, nxt = has_own(n), has_before(n), has_next(n)
                if bef:
                    mask_G(u)
                    scores(u, 0, 0)
                    read_yoff(n, u, b, 0, 0)
                    scores(u, 0, 1)
                    decay_X(n, u, 0)
                if own:
                    dt_first(n, b)
                if bef:
                    read_ydiag(u, 0, 0)
                    read_yoff(n, u, b, 0, 1)
                if own:
                    conv(n, b, 0)
                if bef:
                    read_ydiag(u, 0, 1)
                    read_state(u, b, 0, 0)
                if own:
                    softplus(n)
                if bef:
                    read_state(u, b, 0, 1)
                if own:
                    conv(n, b, 1)
                if bef:
                    scores(u, 1, 0)
                if own:
                    conv(n, b, 2)
                if bef:
                    decay_X(n, u, 1)
                    scores(u, 1, 1)
                if own:
                    sums(n)
                    conv(n, b, 3)
                if bef:
                    read_yoff(n, u, b, 1, 0)
                if own:
                    conv(n, b, 4)
                    conv(n, b, 5)
                if bef:
                    read_ydiag(u, 1, 0)
                if nxt:
                    stats(after(n), 0)
                    stats(after(n), 1)
                if own:
                    conv(n, b, 6)
                if bef:
                    read_yoff(n, u, b, 1, 1)
                    read_ydiag(u, 1, 1)
                    read_state(u, b, 1, 0)
                if nxt:
                    norm(after(n), n, 0)
                    norm(after(n), n, 1)
                if own:
                    conv(n, b, 7)
                if bef:
                    read_state(u, b, 1, 1)
                if own:
                    conv(n, b, 8)
                    conv(n, b, 9)
                    tails(n, b)
                    diff(n, 0, 0)
                    diff(n, 0, 1)
                    diff(n, 1, 0)
                    diff(n, 1, 1)
                if nxt:
                    split_h(after(n), n, 0)
                    split_h(after(n), n, 1)

            turns(dve, prologue, turn)

        @block.tensor
        def _(pe):
            def transpose_ln(n, turn_n):
                for j in range(2):
                    ps = t_wait(pe, t_emptied, turn_n, ("ln", j), -1)
                    for c in range(NC):
                        if j == 0:
                            wait(pe, normed, n, NC, c + 1)
                        for q in range(2):
                            k = 2 * j + q
                            mm = nc.tensor.transpose(ps[:, q * SC + c * P:q * SC + (c + 1) * P],
                                                     A.xl[c][:, k * P:(k + 1) * P], A.ident[:])
                    mm.then_inc(t_filled, 1)

            def product(out, pairs, parts):
                last = len(pairs) * len(parts) - 1
                i = 0
                for wp, ap in parts:
                    for lhs, rhs in pairs:
                        mm = nc.tensor.matmul(out, lhs(wp, ap), rhs(wp, ap), start=(i == 0), stop=(i == last))
                        i += 1
                return mm

            def project_zdt(n, c):
                if c == 0:
                    wait(pe, split, n, 2 * NC, 2 * NC)
                ps = a_wait(pe, a_emptied, n, ("zdt", c), -1)
                s = slice(c * P, (c + 1) * P)
                mm = product(ps[:, 0:ZQ + H],
                             [(lambda w, a, k=k: hT[a][:, k, s], lambda w, a, k=k: Win[w][:, k, Z:Z + ZQ + H])
                              for k in range(KD)], PARTS)
                mm.then_inc(a_filled, 1)

            def project_tile(n, m):
                ps = a_wait(pe, a_emptied, n, ("m", m), -1)
                o = X0 + m * P
                mm = product(ps[:, 0:SC],
                             [(lambda w, a, k=k: Win[w][:, k, o:o + P], lambda w, a, k=k: hT[a][:, k, :])
                              for k in range(KD)], PARTS)
                mm.then_inc(a_filled, 1)

            def project_z(n, j):
                ps = a_wait(pe, a_emptied, n, ("z", j), -1)
                c, f = divmod(j, 2)
                s = slice(c * P, (c + 1) * P)
                o, e = f * W, min((f + 1) * W, Z)
                mm = product(ps[:, 0:e - o],
                             [(lambda w, a, k=k: hT[a][:, k, s], lambda w, a, k=k: Win[w][:, k, o:e])
                              for k in range(KD)], PARTS)
                mm.then_inc(a_filled, 1)

            def scores_G(n, u, b):
                wait(pe, silu_done, u, MX, MX)
                wait(pe, sums_step, n, 3, 0)
                for c in range(NC):
                    s = slice(c * P, (c + 1) * P)
                    mm = nc.tensor.matmul(small[:, c * P:(c + 1) * P], A.xc[1 - b][:, MX - 2, s],
                                          A.xc[1 - b][:, MX - 1, s], start=True, stop=True)
                mm.then_inc(G_done, 1)

            def cumulate(n):
                wait(pe, softplus_step, n, SP_STEPS, SP_STEPS)
                wait(pe, G_masked, n, 1, 0)
                for c in range(NC):
                    nc.tensor.matmul(small[:, c * H:(c + 1) * H], A.triu[:], A.a[:, c, :], start=True, stop=True)
                for c in range(NC):
                    nc.tensor.matmul(small[:, (NC + c) * H:(NC + c + 1) * H], A.ones[:], A.a[:, c, :],
                                     start=True, stop=True)
                for c in range(NC):
                    mm = nc.tensor.matmul(small[0:H, (2 + c) * P:(3 + c) * P], A.a[:, c, :], A.triu[:],
                                          start=True, stop=True)
                mm.then_inc(cs_done, 1)

            def transpose_x(n, u, b, c):
                s = slice(c * P, (c + 1) * P)
                for f in range(2):
                    ps = t_wait(pe, t_emptied, n, ("x", c, f), -1)
                    for q in range(4):
                        mm = nc.tensor.transpose(ps[:, q * P:(q + 1) * P], A.xc[1 - b][:, 4 * f + q, s], A.ident[:])
                    mm.then_inc(t_filled, 1)
                ps = t_wait(pe, t_emptied, n, ("x", c, 2), -1)
                nc.tensor.transpose(ps[:, 0:P], A.xc[1 - b][:, MX - 2, s], A.ident[:]).then_inc(t_filled, 1)

            def y_off(u, b, c, f):
                s = slice(c * P, (c + 1) * P)
                wait(pe, yoff_read, u, 2 * NC, 2 * c + f)
                if c:
                    wait(pe, S_step, u, 4 * NC, 4 * c)
                else:
                    wait(pe, S_step, before(u), 4 * NC, 0)
                nc.tensor.matmul(yoff[:, 0:W], A.xc[1 - b][:, MX - 1, s], A.S[1 - b][:, f * W:(f + 1) * W],
                                 start=True, stop=True).then_inc(yoff_done, 1)

            def y_diag(n, u, c, f):
                wait(pe, M_done, u, 2 * NC, 2 * c + f + 1)
                t_wait(pe, t_emptied, n, ("x", c, f), 1)
                wait(pe, ydiag_read, u, 2 * NC, 2 * c + f)
                for h in range(HH):
                    g = f * HH + h
                    mm = nc.tensor.matmul(ydiag[:, h * HD:(h + 1) * HD], A.L[c][:, g, :],
                                          A.X[:, g * HD:(g + 1) * HD], start=True, stop=True)
                mm.then_inc(ydiag_done, 1)

            def states(n, u, c, f):
                wait(pe, Xdec_done, u, NC, c + 1)
                t_wait(pe, t_emptied, n, ("x", c, 2), 1)
                if f:
                    wait(pe, S_step, u, 4 * NC, 4 * c + 3)
                else:
                    wait(pe, S_step, u, 4 * NC, 4 * c)
                nc.tensor.matmul(state[:, 0:W], A.Btok[:], A.Xd[:, f * W:(f + 1) * W],
                                 start=True, stop=True).then_inc(state_done, 1)

            def transpose_g(n, u, c):
                wait(pe, gated, u, NC, c + 1)
                for f in range(2):
                    ps = t_wait(pe, t_emptied, n, ("g", c, f), -1)
                    for q in range(4):
                        k = 4 * f + q
                        mm = nc.tensor.transpose(ps[:, q * P:(q + 1) * P], A.yt[:, k * P:(k + 1) * P], A.ident[:])
                    mm.then_inc(t_filled, 1)

            def project_out(n, c):
                t_wait(pe, t_emptied, n, ("g", c, 1), 1)
                ps = a_wait(pe, a_emptied, n, ("out", c), -1)
                for k in range(KI):
                    mm = nc.tensor.matmul(ps[:], A.gT[:, k, :], A.Wo[:, k, :], start=(k == 0), stop=(k == KI - 1))
                mm.then_inc(a_filled, 1)

            def turn(n, b):
                u = before(n)
                own, bef, nxt = has_own(n), has_before(n), has_next(n)
                if bef:
                    scores_G(n, u, b)
                    y_off(u, b, 0, 0)
                if own:
                    project_zdt(n, 0)
                if bef:
                    transpose_x(n, u, b, 0)
                if own:
                    project_zdt(n, 1)
                if bef:
                    y_off(u, b, 0, 1)
                if own:
                    project_tile(n, 0)
                if bef:
                    y_diag(n, u, 0, 0)
                if own:
                    project_tile(n, 1)
                if bef:
                    y_diag(n, u, 0, 1)
                    states(n, u, 0, 0)
                if own:
                    project_tile(n, 2)
                if bef:
                    states(n, u, 0, 1)
                if own:
                    project_tile(n, 3)
                if bef:
                    transpose_x(n, u, b, 1)
                if own:
                    project_tile(n, 4)
                    cumulate(n)
                if bef:
                    y_off(u, b, 1, 0)
                if own:
                    project_tile(n, 5)
                if bef:
                    y_diag(n, u, 1, 0)
                if own:
                    project_tile(n, 6)
                if bef:
                    transpose_g(n, u, 0)
                if own:
                    project_tile(n, 7)
                if bef:
                    project_out(n, 0)
                    y_off(u, b, 1, 1)
                    y_diag(n, u, 1, 1)
                    states(n, u, 1, 0)
                if own:
                    project_tile(n, 8)
                if bef:
                    states(n, u, 1, 1)
                if own:
                    project_tile(n, 9)
                    project_z(n, 0)
                    project_z(n, 1)
                    project_z(n, 2)
                if bef:
                    transpose_g(n, u, 1)
                if own:
                    project_z(n, 3)
                if nxt:
                    transpose_ln(after(n), n)
                if bef:
                    project_out(n, 1)

            turns(pe, lambda: transpose_ln(0, -1), turn)


def quantised_weights_stage(nc, T, B):
    with ExitStack() as ctx:
        sem = lambda name: ctx.enter_context(nc.semaphore(name))
        R = 3
        widened, measured = sem("widened"), sem("measured")
        wq_in, placed = ([sem(f"{s}{j}") for j in range(R)] for s in ("wq_in", "placed"))
        gate_in = sem("gate_in")
        flag_step, flag_turned = sem("flag_step"), sem("flag_turned")
        D, KH = T.D, T.HID // P
        jobs = []
        for w, src in ((B.Wg, T.wgT), (B.Wu, T.wuT)):
            for k in range(D // P):
                jobs.append((w[:, k, :], src[k * P:(k + 1) * P, :], T.HID))
        down = T.wdT.rearrange("(k p) n -> p k n", p=P)
        for k in range(0, KH, 3):
            e = min(k + 3, KH)
            jobs.append((B.Wd[:, k:e, :], down[:, k:e, :], (e - k) * D))

        def view(buf, w, size):
            v = buf[:, 0:size]
            return v if len(w.shape) == 2 else v.rearrange("p (k n) -> p k n", n=D)

        with nc.Block() as block:

            @block.sync
            def _(sp):
                for b in range(2):
                    sp.dma_start(B.gate_row[b][:], T.gate2_d[b:b + 1, :].broadcast_to([P, D])).then_inc(gate_in, 16)
                for j, (w, src, size) in enumerate(jobs):
                    if j >= R:
                        sp.wait_ge(widened, j - R + 1)
                    sp.dma_start(view(B.wint[j % R], w, size), src).then_inc(wq_in[j % R], 16)
                sp.wait_ge(gate_in, 32)

            @block.scalar
            def _(act):
                for j, (w, src, size) in enumerate(jobs):
                    act.wait_ge(wq_in[j % R], 16 * (j // R + 1))
                    if j >= R:
                        act.wait_ge(measured, j - R + 1)
                        act.wait_ge(placed[j % R], 16 * (j // R))
                    nc.scalar.activation(B.wflt[j % R][:, 0:size], B.wint[j % R][:, 0:size], ACT.Copy,
                                         bias=-ZERO_POINT).then_inc(widened, 1)

            @block.gpsimd
            def _(pool):
                for j, (w, src, size) in enumerate(jobs):
                    pool.wait_ge(widened, j + 1)
                    pool.dma_start(w.bitcast(F32), view(B.wflt[j % R], w, size)).then_inc(placed[j % R], 16)
                for r in range(R):
                    pool.wait_ge(placed[r], 16 * len(range(r, len(jobs), R)))

            @block.vector
            def _(dve):
                for j, (w, src, size) in enumerate(jobs):
                    dve.wait_ge(widened, j + 1)
                    nc.vector.tensor_reduce(B.wmax[:, j:j + 1], B.wflt[j % R][:, 0:size], AX_X, ALU.max,
                                            apply_absolute_value=True).then_inc(measured, 1)
                dve.wait_ge(measured, len(jobs))
                nc.vector.tensor_reduce(B.wtop[:], B.wmax[:, 0:len(jobs)], AX_X, ALU.max).then_inc(flag_step, 1)
                dve.wait_ge(flag_turned, 1)
                nc.vector.tensor_reduce(B.top1[:], B.psum[0][0:1, 0:P], AX_X, ALU.max).then_inc(flag_step, 1)
                dve.wait_ge(flag_step, 2)
                nc.vector.tensor_scalar(B.flag[:], B.top1[:], EXACT_INT, None, ALU.is_gt).then_inc(flag_step, 1)
                dve.wait_ge(flag_step, 3)

            @block.tensor
            def _(pe):
                pe.wait_ge(flag_step, 1)
                nc.tensor.transpose(B.psum[0][0:1, 0:P], B.wtop[:], B.ident[:]).then_inc(flag_turned, 1)


def feed_forward_stage(nc, T, B):
    D, HID = T.D, T.HID
    KD, KH = D // P, HID // P
    SC = T.SC2
    NC = SC // P
    N = 2 * T.S // SC
    with ExitStack() as ctx:
        sem = lambda name: ctx.enter_context(nc.semaphore(name))
        resid_in = sem("ff_resid_in")
        x_in, out_sent = ([sem(f"{s}{c}") for c in range(NC)] for s in ("ff_x_in", "ff_out_sent"))
        t_filled, t_emptied = sem("ff_t_filled"), sem("ff_t_emptied")
        gate_done, up_done, down_done, gate_read, hid_step = (
            sem(s) for s in ("gate_done", "up_done", "down_done", "gate_read", "hid_step"))
        stats_step, rstd_step, normed, split, down_read, summed = (
            sem(s) for s in ("ff_stats_step", "ff_rstd_step", "ff_normed", "ff_split", "down_read", "summed"))
        tps, gates, ups, downs = B.psum[0:2], B.psum[2:4], B.psum[4:6], B.psum[6:8]
        block = ctx.enter_context(nc.Block())

        def turns(engine, prologue, turn):
            prologue()
            turn(0, 0)
            pairs = (N - 2) // 2
            with engine.Fori(0, pairs) as i:
                turn((i, 2, 1), 1)
                turn((i, 2, 2), 0)
            for n in range(1 + 2 * pairs, N):
                turn(n, n % 2)

        def has_next(n):
            return not (isinstance(n, int) and n == N - 1)

        @block.sync
        def _(sp):
            def rows(t, b, n, c):
                return t[b][bass.ds(start_token(n, SC) + c * P, P), :]

            def load_x(n, b):
                for c in range(NC):
                    wait_apart(sp, normed, before(n), NC, c + 1)
                    sp.dma_start(B.xl[c][:], rows(T.x1, b, n, c)).then_inc(x_in[c], 16)

            def turn(n, b):
                if has_next(n):
                    load_x(after(n), 1 - b)
                for c in range(NC):
                    wait_apart(sp, out_sent[c], n, 16, 0)
                    sp.dma_start(B.xr[c][:], rows(T.x1, b, n, c)).then_inc(resid_in, 16)
                for c in range(NC):
                    wait_apart(sp, summed, n, NC, c + 1)
                    sp.dma_start(rows(T.out, b, n, c), B.xr[c][:]).then_inc(out_sent[c], 16)

            turns(sp, lambda: load_x(0, 0), turn)
            for c in range(NC):
                sp.wait_ge(out_sent[c], N * 16)

        @block.gpsimd
        def _(pool):
            def rstd(n):
                for c in range(NC):
                    wait(pool, stats_step, n, 2 * NC, 2 * (c + 1))
                    wait_apart(pool, normed, before(n), NC, c + 1)
                    nc.gpsimd.tensor_scalar(B.rstd[:, c:c + 1], B.mv[c][:, 1:2], 1.0, EPS, ALU.mult, ALU.add) \
                        .then_inc(rstd_step, 1)
                    wait(pool, rstd_step, n, 2 * NC, 2 * c + 1)
                    nc.gpsimd.tensor_tensor(B.rstd[:, c:c + 1], B.rstd[:, c:c + 1], T.neg_half[:], ALU.pow) \
                        .then_inc(rstd_step, 1)

            def turn(n, b):
                if has_next(n):
                    rstd(after(n))
                for c in range(NC):
                    wait(pool, down_read, n, NC, c + 1)
                    wait(pool, resid_in, n, NC * 16, NC * 16)
                    nc.gpsimd.tensor_tensor(B.xr[c][:], B.ob[c % 2][:], B.xr[c][:], ALU.add).then_inc(summed, 1)

            turns(pool, lambda: rstd(0), turn)

        @block.scalar
        def _(act):
            def evac_ln(n, b):
                for k in range(KD):
                    wait(act, t_filled, n, KD, k + 1)
                    if k == 0:
                        wait(act, split, n, 2 * KD, 0)
                    nc.scalar.activation(B.h32[:, k, :], tps[k % 2][:], ACT.Identity, bias=T.modc[:, 2, k, b:b + 1],
                                         scale=T.modc[:, 3, k, b:b + 1]).then_inc(t_emptied, 1)

            def turn(n, b):
                for m in range(KH):
                    wait(act, gate_done, n, KH, m + 1)
                    wait(act, hid_step, n, 3 * KH, 3 * (m - 2) + 1)
                    nc.scalar.activation(B.sg[m % 2][:], gates[m % 2][:], ACT.Silu, scale=T.sgate[:, m:m + 1]) \
                        .then_inc(gate_read, 1)
                    if m == 7 and has_next(n):
                        evac_ln(after(n), 1 - b)

            turns(act, lambda: evac_ln(0, 0), turn)

        @block.vector
        def _(dve):
            def stats(n, c):
                wait(dve, x_in[c], n, 16, 16)
                wait(dve, rstd_step, n, 2 * NC, 2 * c + 2 - 2 * NC)
                wait(dve, normed, before(n), NC, c + 1)
                wait(dve, stats_step, n, 2 * NC, 2 * c + 2 - 2 * NC)
                nc.vector.bn_stats(B.bst[c][:], B.xl[c][:]).then_inc(stats_step, 1)
                wait_apart(dve, stats_step, n, 2 * NC, 2 * c + 1)
                nc.vector.bn_aggr(B.mv[c][:], B.bst[c][:]).then_inc(stats_step, 1)

            def norm(n, c):
                wait(dve, rstd_step, n, 2 * NC, 2 * c + 2)
                wait(dve, t_filled, n, KD, 0)
                nc.vector.tensor_scalar(B.hn[c][:], B.xl[c][:], B.mv[c][:, 0:1], B.rstd[:, c:c + 1],
                                        ALU.subtract, ALU.mult).then_inc(normed, 1)

            def split_h(n):
                for k in range(KD):
                    wait(dve, t_emptied, n, KD, k + 1)
                    if k == 0:
                        wait(dve, up_done, n, KH, 0)
                        wait(dve, split, n, 2 * KD, 0)
                    nc.vector.tensor_copy(B.hThi[:, k, :], B.h32[:, k, :]).then_inc(split, 1)
                    wait(dve, split, n, 2 * KD, 2 * k + 1)
                    nc.vector.tensor_tensor(B.hTlo[:, k, :], B.h32[:, k, :], B.hThi[:, k, :].bitcast(F32),
                                            ALU.subtract).then_inc(split, 1)

            def hidden(n, m):
                wait(dve, gate_read, n, KH, m + 1)
                wait(dve, up_done, n, KH, m + 1)
                wait(dve, hid_step, n, 3 * KH, 3 * (m - 1))
                if m == 0:
                    wait(dve, down_done, n, NC, 0)
                nc.vector.scalar_tensor_tensor(B.hid[m % 2][:], ups[m % 2][:], T.sup[:, m:m + 1], B.sg[m % 2][:],
                                               ALU.mult, ALU.mult).then_inc(hid_step, 1)
                wait(dve, hid_step, n, 3 * KH, 3 * m + 1)
                nc.vector.tensor_copy(B.hidhi[:, m, :], B.hid[m % 2][:]).then_inc(hid_step, 1)
                wait(dve, hid_step, n, 3 * KH, 3 * m + 2)
                nc.vector.tensor_tensor(B.hidlo[:, m, :], B.hid[m % 2][:], B.hidhi[:, m, :].bitcast(F32),
                                        ALU.subtract).then_inc(hid_step, 1)

            def prologue():
                for c in range(NC):
                    stats(0, c)
                for c in range(NC):
                    norm(0, c)
                split_h(0)

            def turn(n, b):
                for m in range(KH):
                    hidden(n, m)
                    if has_next(n) and 1 <= m <= NC:
                        stats(after(n), m - 1)
                        if m == NC:
                            for c in range(NC):
                                norm(after(n), c)
                if has_next(n):
                    split_h(after(n))
                for c in range(NC):
                    wait(dve, down_done, n, NC, c + 1)
                    wait(dve, summed, n, NC, c - 1)
                    nc.vector.tensor_tensor(B.ob[c % 2][:], downs[c % 2][:], B.gate_row[b][:], ALU.mult) \
                        .then_inc(down_read, 1)

            turns(dve, prologue, turn)

        @block.tensor
        def _(pe):
            def transpose_ln(n):
                for k in range(KD):
                    wait(pe, t_emptied, n, KD, k - 1)
                    if k == 0:
                        wait(pe, normed, n, NC, NC)
                    for c in range(NC):
                        mm = nc.tensor.transpose(tps[k % 2][:, c * P:(c + 1) * P], B.hn[c][:, k * P:(k + 1) * P],
                                                 B.ident[:])
                    mm.then_inc(t_filled, 1)

            def program(dt):

                def project(ps, W, m):
                    for k in range(KD):
                        for a, h in enumerate((B.hThi, B.hTlo)):
                            mm = nc.tensor.matmul(ps[:], W[:, k, m * P:(m + 1) * P].bitcast(dt),
                                                  h[:, k, :].bitcast(dt),
                                                  start=(k == 0 and a == 0), stop=(k == KD - 1 and a == 1))
                    return mm

                def turn(n, b):
                    wait(pe, split, n, 2 * KD, 2 * KD)
                    for m in range(KH):
                        wait(pe, gate_read, n, KH, m - 1)
                        project(gates[m % 2], B.Wg, m).then_inc(gate_done, 1)
                        wait(pe, hid_step, n, 3 * KH, 3 * (m - 2) + 1)
                        project(ups[m % 2], B.Wu, m).then_inc(up_done, 1)
                        if m == 7 and has_next(n):
                            transpose_ln(after(n))
                    for c in range(NC):
                        wait(pe, down_read, n, NC, c - 1)
                        s = slice(c * P, (c + 1) * P)
                        for m in range(KH):
                            if c == 0:
                                wait(pe, hid_step, n, 3 * KH, 3 * (m + 1))
                            for a, h in enumerate((B.hidhi, B.hidlo)):
                                mm = nc.tensor.matmul(downs[c % 2][:], h[:, m, s].bitcast(dt), B.Wd[:, m, :].bitcast(dt),
                                                      start=(m == 0 and a == 0), stop=(m == KH - 1 and a == 1))
                        mm.then_inc(down_done, 1)

                turns(pe, lambda: transpose_ln(0), turn)

            wide = pe.value_load(B.flag[0:1, 0:1], min_val=0, max_val=1)
            with pe.If(wide == 0):
                program(FR)
            with pe.Else():
                program(F32)


def adaln_block(nc, T):
    T.D, T.DI, T.CD, T.H, T.HD, T.S, T.HID = 512, 1024, 1280, 16, 64, 2048, 1408
    T.NIN = T.DI + T.CD + T.H
    T.SC, T.SC2 = 256, 512
    T.ZQ = 256
    KD, KI, MX, KH = T.D // P, T.DI // P, T.CD // P, T.HID // P
    NC = T.SC // P
    T.x1 = nc.dram_tensor("x1_scratch", [2, T.S, T.D], F32, kind="Internal").ap()
    T.gate2_d = nc.dram_tensor("gate2_scratch", [2, T.D], F32, kind="Internal").ap()
    T.cs_d = nc.dram_tensor("sums_scratch", [NC, T.H, P], F32, kind="Internal").ap()
    with ExitStack() as outer:
        def sb(ctx, name, shape, dt=F32):
            return ctx.enter_context(nc.sbuf_tensor(name, shape, dt))

        psum = [outer.enter_context(nc.psum_tensor(f"bank{i}", [P, 512], F32)) for i in range(8)]
        T.modc = sb(outer, "modc", [P, 4, KD, 2])
        T.neg_half = sb(outer, "neg_half", [P, 1])
        T.sgate, T.sup = sb(outer, "sgate", [P, KH]), sb(outer, "sup", [P, KH])
        ident = sb(outer, "ident", [P, P])

        with ExitStack() as ctx:
            A = Tensors()
            A.psum, A.ident = psum, ident
            T.gate_row = [sb(ctx, f"gate_row{b}", [P, T.D]) for b in range(2)]
            A.triu, A.ones = sb(ctx, "triu", [P, P]), sb(ctx, "ones", [P, P])
            A.Whi, A.Wlo = sb(ctx, "W_in_high", [P, KD, T.NIN], FR), sb(ctx, "W_in_low", [P, KD, T.NIN], FR)
            A.Wo = sb(ctx, "W_out", [P, KI, T.D])
            A.cT, A.sc = sb(ctx, "cT", [P, KD, 2]), sb(ctx, "silu_c", [P, KD, 2])
            A.wconv, A.bconv = sb(ctx, "wconv", [P, MX, 4]), sb(ctx, "bconv", [P, MX])
            A.normw = sb(ctx, "normw", [P, KI])
            A.dtb, A.negA, A.Drow = sb(ctx, "dt_bias", [P, T.H]), sb(ctx, "negA", [P, T.H]), sb(ctx, "Drow", [P, T.H])
            A.xl = [sb(ctx, f"x_tile{c}", [P, T.D]) for c in range(NC)]
            A.xr = [sb(ctx, f"x_resid{c}", [P, T.D]) for c in range(NC)]
            A.ob = sb(ctx, "branch", [P, T.D])
            A.bst = [sb(ctx, f"bn_stats{c}", [P, 6]) for c in range(NC)]
            A.mv = [sb(ctx, f"mean_var{c}", [P, 2]) for c in range(NC)]
            A.rstd, A.rs, A.ssq = (sb(ctx, s, [P, NC]) for s in ("rstd", "inv_rms", "square_sum"))
            A.hThi, A.hTlo = sb(ctx, "h_high", [P, KD, T.SC], FR), sb(ctx, "h_low", [P, KD, T.SC], FR)
            A.raw = sb(ctx, "conv_in", [P, MX, 3 + T.SC])
            A.tail = [sb(ctx, f"conv_tail{b}", [P, MX, 3]) for b in range(2)]
            A.xc = [sb(ctx, f"xBC{b}", [P, MX, T.SC]) for b in range(2)]
            A.siluz = sb(ctx, "silu_z", [P, NC, T.DI - T.ZQ])
            A.zdt = [sb(ctx, f"z_dt{b}", [P, NC, T.ZQ + T.H]) for b in range(2)]
            A.sp = [sb(ctx, f"softplus{j}", [P, NC, T.H]) for j in range(6)]
            A.a = sb(ctx, "dtA", [P, NC, T.H])
            A.s3, A.e3 = sb(ctx, "sums", [P, 3 * NC * T.H]), sb(ctx, "exp_sums", [P, 3 * NC * T.H])
            A.csT = sb(ctx, "sumsT", [T.H, NC, P])
            A.L = [sb(ctx, f"decay{c}", [P, T.H, P]) for c in range(NC)]
            A.Gm = sb(ctx, "G_masked", [P, NC, P])
            A.X, A.Xd, A.XD = (sb(ctx, s, [P, T.DI]) for s in ("X", "X_decayed", "X_D"))
            A.Btok = sb(ctx, "B_rows", [P, P])
            A.yt = sb(ctx, "y", [P, T.DI])
            A.gT = sb(ctx, "gT", [P, KI, P])
            A.S = [sb(ctx, f"state{b}", [P, T.DI]) for b in range(2)]
            setup_stage(nc, T, A)
            mixer_stage(nc, T, A)

        with ExitStack() as ctx:
            B = Tensors()
            NC2 = T.SC2 // P
            B.psum, B.ident = psum, ident
            B.Wg, B.Wu = sb(ctx, "W_gate", [P, KD, T.HID], FR), sb(ctx, "W_up", [P, KD, T.HID], FR)
            B.Wd = sb(ctx, "W_down", [P, KH, T.D], FR)
            B.wmax, B.wtop, B.top1 = sb(ctx, "wmax", [P, 16]), sb(ctx, "wtop", [P, 1]), sb(ctx, "top1", [1, 1])
            B.gate_row = [sb(ctx, f"gate2_row{b}", [P, T.D]) for b in range(2)]
            B.flag = sb(ctx, "wide_flag", [1, 1], I32)
            with ExitStack() as staging:
                B.wint = [sb(staging, f"wint{j}", [P, 3 * T.D], I32) for j in range(3)]
                B.wflt = [sb(staging, f"wfloat{j}", [P, 3 * T.D]) for j in range(3)]
                quantised_weights_stage(nc, T, B)
            B.xl = [sb(ctx, f"ff_x_tile{c}", [P, T.D]) for c in range(NC2)]
            B.xr = [sb(ctx, f"ff_x_resid{c}", [P, T.D]) for c in range(NC2)]
            B.hn = [sb(ctx, f"ff_normed{c}", [P, T.D]) for c in range(NC2)]
            B.ob = [sb(ctx, f"ff_branch{c}", [P, T.D]) for c in range(2)]
            B.bst = [sb(ctx, f"ff_bn_stats{c}", [P, 6]) for c in range(NC2)]
            B.mv = [sb(ctx, f"ff_mean_var{c}", [P, 2]) for c in range(NC2)]
            B.rstd = sb(ctx, "ff_rstd", [P, NC2])
            B.h32 = sb(ctx, "ff_h", [P, KD, T.SC2])
            B.hThi, B.hTlo = sb(ctx, "ff_h_high", [P, KD, T.SC2], FR), sb(ctx, "ff_h_low", [P, KD, T.SC2], FR)
            B.sg = [sb(ctx, f"silu_gate{j}", [P, T.SC2]) for j in range(2)]
            B.hid = [sb(ctx, f"hidden{j}", [P, T.SC2]) for j in range(2)]
            B.hidhi, B.hidlo = (sb(ctx, s, [P, KH, T.SC2], FR) for s in ("hidden_high", "hidden_low"))
            feed_forward_stage(nc, T, B)


def kernel(**inputs):
    import numpy as np
    import concourse.bacc as bacc
    from concourse.bass_utils import run_bass_kernel_spmd

    nc = bacc.Bacc("TRN2", target_bir_lowering=False, num_devices=1)
    arrays = {}

    def put(name, a):
        a = np.ascontiguousarray(a)
        arrays[name] = a
        return nc.dram_tensor(name, a.shape, mybir.dt.from_np(a.dtype), kind="ExternalInput").ap()

    T = Tensors()
    T.x = put("x", inputs["L0_attn_u"])
    w_in = np.asarray(inputs["L0_attn_W_in"]).T
    h = np.asarray(inputs["L0_attn_dt_bias"]).shape[0]
    di = np.asarray(inputs["L0_attn_norm_w"]).shape[0]
    T.winT = put("W_inT", np.concatenate([w_in[:, :di], w_in[:, -h:], w_in[:, di:-h]], axis=1))
    T.woutT = put("W_outT", np.asarray(inputs["L0_attn_W_out"]).T)
    T.wconv = put("W_conv", inputs["L0_attn_W_conv"])
    T.bconv = put("b_conv", inputs["L0_attn_b_conv"])
    T.dtb = put("dt_bias_in", inputs["L0_attn_dt_bias"])
    T.alog = put("A_log", inputs["L0_attn_A_log"])
    T.Dp = put("Dp", inputs["L0_attn_Dp"])
    T.normw = put("norm_w", inputs["L0_attn_norm_w"])
    T.wgT = put("wq_gateT", np.asarray(inputs["L0_ffn_wq_gate"]).T)
    T.wuT = put("wq_upT", np.asarray(inputs["L0_ffn_wq_up"]).T)
    T.wdT = put("wq_downT", np.asarray(inputs["L0_ffn_wq_down"]).T)
    T.sgate_in = put("s_gate", inputs["L0_ffn_s_gate"])
    T.sup_in = put("s_up", inputs["L0_ffn_s_up"])
    T.sdown = put("s_down", inputs["L0_ffn_s_down"])
    T.cT = put("cT_in", np.asarray(inputs["L0_c"]).T)
    T.wmod = put("w_mod", inputs["L0_wmod"])
    T.out = nc.dram_tensor("out", inputs["L0_attn_u"].shape, F32, kind="ExternalOutput").ap()
    adaln_block(nc, T)
    r = run_bass_kernel_spmd(nc, [arrays], core_ids=[0])
    return r.results[0]["out"]
```

```python
from contextlib import ExitStack

import concourse.bass as bass
from concourse import mybir

F32 = mybir.dt.float32
FR = mybir.dt.float32r
I32 = mybir.dt.int32
ALU = mybir.AluOpType
ACT = mybir.ActivationFunctionType
AX_X = mybir.AxisListType.X

P = 128
EPS = 1e-5
FLOOR = 0.25
ZERO_POINT = 128.0
EXACT_INT = 4096.0


def count(n, per, c):
    if isinstance(n, tuple):
        i, a, b = n
        return i * (a * per) + (b * per + c)
    return n * per + c


def before(n):
    return (n[0], n[1], n[2] - 1) if isinstance(n, tuple) else n - 1


def after(n):
    return (n[0], n[1], n[2] + 1) if isinstance(n, tuple) else n + 1


def wait(eng, sem, n, per, c):
    v = count(n, per, c)
    if isinstance(v, int) and v <= 0:
        return
    eng.wait_ge(sem, v)


def wait_apart(eng, sem, n, per, c):
    v = count(n, per, c)
    if isinstance(v, int):
        wait(eng, sem, n, per, c)
        return
    v = eng.snap(eng.to_reg(v))
    eng.wait_ge(sem, 1)
    eng.wait_ge(sem, v)


def start_token(n, size):
    if isinstance(n, tuple):
        i, a, b = n
        return i * size + (b // 2) * size
    return (n // 2) * size


class Tensors:
    pass


def spread_gate(nc, dve, out, cols, done):
    nc.vector.tensor_copy(out, cols.unsqueeze(2).broadcast_to([P, out.shape[1], P])).then_inc(done, 1)


class Setup:

    SMALL = 9
    ORDER = (0, 1, 4, 5, 2, 3)

    def __init__(self, nc, T, A, sem):
        self.nc, self.T, self.A = nc, T, A
        self.c_in, self.params_in, self.wout_in = sem("c_in"), sem("params_in"), sem("wout_in")
        self.mod_in = [sem(f"mod_in{s}") for s in range(6)]
        self.win_in = [sem(f"win_in{k}") for k in range(T.D // P)]
        self.silu_c_done, self.cols_done, self.cols_read = sem("silu_c_done"), sem("cols_done"), sem("cols_read")
        self.gate_step, self.spread_done, self.rows_done, self.rows_read = (
            sem(s) for s in ("gate_step", "spread_done", "rows_done", "rows_read"))
        self.win_high, self.win_low, self.const_step = sem("win_high"), sem("win_low"), sem("const_step")
        self.a_done, self.a_ready, self.wout_scaled = sem("a_done"), sem("a_ready"), sem("wout_scaled")
        KD = T.D // P
        k_tiles = lambda t: t.rearrange("p (k n) -> p k n", n=T.D)
        flat = lambda t: t[:, :, :].rearrange("p a b -> p (a b)")
        whole = [[(k_tiles(flat(t)[:, 0:KD * T.D]), 0, KD)] for t in (A.L[0], A.L[1])]
        halves = [[(k_tiles(t0[:, :]), 0, KD // 2), (k_tiles(t1[:, :]), KD // 2, KD)]
                  for t0, t1 in ((A.Xd, A.yt), (A.S[0], A.S[1]))]
        self.wm = whole + whole + halves
        self.stage = [flat(t)[:, 0:T.NIN] for t in (A.xc[0], A.xc[1], A.raw, A.xc[0])]
        banks = dict(zip(self.ORDER, (0, 1, 4, 5, 0, 1)))
        self.cols = [A.psum[banks[s]][:, 0:2 * KD].rearrange("p (k b) -> p k b", b=2) for s in range(6)]
        self.gates = {2: A.gate1c, 5: T.gate2c}

    def sync(self, sp, load_x):
        nc, T, A = self.nc, self.T, self.A
        w_mod = T.wmod.rearrange("(k p) (s n) -> s p k n", p=P, s=6)

        def section(s):
            for w, k0, k1 in self.wm[s]:
                sp.dma_start(w, w_mod[s][:, k0:k1, :]).then_inc(self.mod_in[s], 16)

        def win(k):
            sp.dma_start(self.stage[k], T.winT[k * P:(k + 1) * P, :]).then_inc(self.win_in[k], 16)

        with nc.allow_non_contiguous_dma(reason="small parameters"):
            sp.dma_start(A.cT[:], T.cT.rearrange("(k p) b -> p k b", p=P)).then_inc(self.c_in, 16)
            section(0)
            section(1)
            load_x()
            win(0)
            sp.dma_start(A.wconv[:], T.wconv.rearrange("(m p) o k -> p m (o k)", p=P)).then_inc(self.params_in, 16)
            for w, src in ((A.bconv, T.bconv), (A.normw, T.normw), (T.sgate, T.sgate_in), (T.sup, T.sup_in),
                           (A.sdown, T.sdown)):
                sp.dma_start(w[:], src.rearrange("(m p) -> p m", p=P)).then_inc(self.params_in, 16)
            for row, src in ((A.dtb, T.dtb), (A.negA, T.alog), (A.Drow, T.Dp)):
                sp.dma_start(row[:], src.rearrange("(a h) -> a h", a=1).broadcast_to([P, src.shape[0]])) \
                    .then_inc(self.params_in, 16)
            win(1)
            win(2)
            for s in (4, 5):
                section(s)
            sp.wait_ge(self.cols_done, 2)
            for s in (2, 3):
                section(s)
            sp.wait_ge(self.win_low, 1)
            win(3)
        sp.dma_start(A.Wo[:], T.woutT.rearrange("(k p) n -> p k n", p=P)).then_inc(self.wout_in, 16)

    def gpsimd(self, pool, rstd):
        nc, T, A = self.nc, self.T, self.A
        step = self.const_step
        nc.gpsimd.memset(A.ident[:], 0.0).then_inc(step, 1)
        nc.gpsimd.memset(A.triu[:], 1.0).then_inc(step, 1)
        nc.gpsimd.memset(T.neg_half[:], -0.5).then_inc(step, 1)
        nc.gpsimd.memset(A.ones[:], 1.0).then_inc(step, 1)
        pool.wait_ge(step, 4)
        nc.gpsimd.affine_select(out=A.ident[:], in_=A.ident[:], compare_op=ALU.not_equal, fill=1.0,
                                base=0, pattern=[[-1, P]], channel_multiplier=1).then_inc(step, 1)
        nc.gpsimd.affine_select(out=A.triu[:], in_=A.triu[:], compare_op=ALU.is_ge, fill=0.0,
                                base=0, pattern=[[1, P]], channel_multiplier=-1).then_inc(step, 1)
        nc.gpsimd.memset(T.wtop[:], 0.0).then_inc(step, 1)
        for b in range(2):
            nc.gpsimd.memset(A.tail[b][:], 0.0).then_inc(step, 1)
        rstd()
        pool.wait_ge(self.win_low, 3)
        nc.gpsimd.memset(A.raw[:, :, 0:3], 0.0).then_inc(step, 1)
        pool.wait_ge(self.cols_done, 6)
        for b in range(2):
            nc.gpsimd.memset(A.S[b][:], 0.0).then_inc(step, 1)
        pool.wait_ge(self.params_in, 16 * self.SMALL)
        pool.wait_ge(self.wout_in, 16)
        for k in range(T.DI // P):
            nc.gpsimd.tensor_scalar(A.Wo[:, k, :], A.Wo[:, k, :], A.normw[:, k:k + 1], None, ALU.mult) \
                .then_inc(self.wout_scaled, 1)

    def scalar(self, act, evac_ln):
        nc, T, A = self.nc, self.T, self.A
        act.wait_ge(self.c_in, 16)
        nc.scalar.activation(A.sc[:], A.cT[:], ACT.Silu).then_inc(self.silu_c_done, 1)
        act.wait_ge(self.cols_read, 2)
        evac_ln()
        for k in range(T.D // P):
            act.wait_ge(self.win_in[k], 16)
            nc.scalar.activation(A.Whi[:, k, :], self.stage[k], ACT.Copy).then_inc(self.win_high, 1)
        act.wait_ge(self.params_in, 16 * self.SMALL)
        nc.scalar.activation(A.negA[:], A.negA[:], ACT.Exp).then_inc(self.a_done, 1)
        act.wait_ge(self.win_low, T.D // P)
        act.wait_ge(self.const_step, 12)

    def vector(self, dve, normalise, split_h):
        nc, T, A = self.nc, self.T, self.A

        def vectors(s):
            i = (0, 1, 3, 4).index(s)
            dve.wait_ge(self.cols_done, self.ORDER.index(s) + 1)
            nc.vector.tensor_scalar(T.modc[:, i], self.cols[s], float(i % 2), None, ALU.add) \
                .then_inc(self.cols_read, 1)

        def gate(s, i):
            g, t = self.gates[s], A.gtmp[i]
            dve.wait_ge(self.cols_done, self.ORDER.index(s) + 1)
            nc.vector.tensor_scalar(t[:], self.cols[s], 0.0, 2.0, ALU.is_ge, ALU.mult).then_inc(self.gate_step, 1)
            dve.wait_ge(self.gate_step, 4 * i + 1)
            nc.vector.tensor_scalar(t[:], t[:], -1.0, None, ALU.add).then_inc(self.gate_step, 1)
            dve.wait_ge(self.gate_step, 4 * i + 2)
            nc.vector.tensor_tensor(g[:], self.cols[s], t[:], ALU.mult).then_inc(self.gate_step, 1)
            dve.wait_ge(self.gate_step, 4 * i + 3)
            nc.vector.scalar_tensor_tensor(g[:], g[:], FLOOR, t[:], ALU.max, ALU.mult).then_inc(self.gate_step, 1)
            dve.wait_ge(self.gate_step, 4 * i + 4)

        def low(k):
            dve.wait_ge(self.win_high, k + 1)
            nc.vector.tensor_tensor(A.Wlo[:, k, :], self.stage[k], A.Whi[:, k, :].bitcast(F32),
                                    ALU.subtract).then_inc(self.win_low, 1)

        vectors(0)
        vectors(1)
        normalise()
        split_h()
        low(0)
        vectors(4)
        gate(5, 0)
        low(1)
        gate(2, 1)
        vectors(3)
        dve.wait_ge(self.params_in, 16 * self.SMALL)
        nc.vector.tensor_tensor(T.gate2c[:], T.gate2c[:], A.sdown[:].unsqueeze(2).broadcast_to([P, T.D // P, 2]),
                                ALU.mult).then_inc(self.gate_step, 1)
        low(2)
        for b in range(2):
            spread_gate(nc, dve, A.gsp[b], A.gate1c[:, :, b], self.spread_done)
        low(3)
        for b in range(2):
            dve.wait_ge(self.rows_done, b + 1)
            nc.vector.tensor_copy(T.gate_row[b][:], A.psum[6 + b][:]).then_inc(self.rows_read, 1)
        dve.wait_ge(self.a_done, 1)
        nc.vector.tensor_scalar(A.negA[:], A.negA[:], -1.0, None, ALU.mult).then_inc(self.a_ready, 1)
        dve.wait_ge(self.a_ready, 1)
        dve.wait_ge(self.const_step, 12)

    def tensor(self, pe, transpose_ln):
        nc, T, A = self.nc, self.T, self.A
        KD = T.D // P

        def section(s):
            pe.wait_ge(self.mod_in[s], 16 * len(self.wm[s]))
            for k in range(KD):
                for w, k0, k1 in self.wm[s]:
                    for q in range(k0, k1):
                        mm = nc.tensor.matmul(self.cols[s][:, k, :], w[:, q - k0, k * P:(k + 1) * P], A.sc[:, q, :],
                                              start=(q == 0), stop=(q == KD - 1))
            mm.then_inc(self.cols_done, 1)

        pe.wait_ge(self.silu_c_done, 1)
        section(0)
        section(1)
        pe.wait_ge(self.const_step, 6)
        transpose_ln()
        for s in self.ORDER[2:]:
            if s == self.ORDER[4]:
                pe.wait_ge(self.cols_read, 2)
            section(s)
        for b in range(2):
            pe.wait_ge(self.spread_done, b + 1)
            for k in range(KD):
                mm = nc.tensor.matmul(A.psum[6 + b][:, k * P:(k + 1) * P], A.gsp[b][:, k, :], A.ident[:],
                                      start=True, stop=True)
            mm.then_inc(self.rows_done, 1)
        pe.wait_ge(self.win_low, KD)
        pe.wait_ge(self.cols_read, 4)
        pe.wait_ge(self.gate_step, 9)
        pe.wait_ge(self.rows_read, 2)


def mixer_stage(nc, T, A):
    D, DI, H, HD = T.D, T.DI, T.H, T.HD
    KD, KI = D // P, DI // P
    MX = T.CD // P
    SC, NC = T.SC, T.SC // P
    N = 2 * T.S // SC
    HH = H // 2
    W = HH * HD
    SP_STEPS = 17
    T_USES, A_USES = 12, 18
    DT0, X0 = DI, DI + H
    ZQ = T.ZQ
    Z = DI - ZQ
    with ExitStack() as ctx:
        sem = lambda name: ctx.enter_context(nc.semaphore(name))
        setup = Setup(nc, T, A, sem)
        resid_in, cs_out = sem("resid_in"), sem("cs_out")
        wq_in, wq_out = ([sem(f"{s}{c}") for c in range(2)] for s in ("wq_in", "wq_out"))
        widened, measured = sem("widened"), sem("measured")
        x_in, cs_in, x1_out = ([sem(f"{s}{c}") for c in range(NC)] for s in ("x_in", "cs_in", "x1_out"))
        cs_done, G_done = sem("cs_done"), sem("G_done")
        a_filled, a_emptied = sem("a_filled"), sem("a_emptied")
        t_filled, t_emptied = sem("t_filled"), sem("t_emptied")
        yoff_done, ydiag_done, state_done = sem("yoff_done"), sem("ydiag_done"), sem("state_done")
        silu_done, siluq_done, e3_done, edt_done, decay_done, sq_done = (
            sem(s) for s in ("silu_done", "siluq_done", "e3_done", "edt_done", "decay_done", "sq_done"))
        stats_step, normed, split, conv_step, softplus_step, sums_step = (
            sem(s) for s in ("stats_step", "normed", "split", "conv_step", "softplus_step", "sums_step"))
        tail_step, diff_done, G_masked, M_done, Xdec_done = (
            sem(s) for s in ("tail_step", "diff_done", "G_masked", "M_done", "Xdec_done"))
        yoff_read, ydiag_read, S_step = sem("yoff_read"), sem("ydiag_read"), sem("S_step")
        rstd_step, XD_done, y_summed, gated, rs_step, out_step = (
            sem(s) for s in ("rstd_step", "XD_done", "y_summed", "gated", "rs_step", "out_step"))

        accs, tps = A.psum[0:2], A.psum[2:4]
        small, yoff, ydiag, state = A.psum[4:8]
        x_d, x1_d = T.x, T.x1
        hT = (A.hThi, A.hTlo)
        h32 = A.XD[:, :].rearrange("p (k t) -> p k t", k=KD)
        Win = (A.Whi, A.Wlo)
        PARTS = ((0, 0), (0, 1), (1, 0))

        A_ORDER = [("zdt", 0), ("zdt", 1)] + [("m", m) for m in range(8)] + [("out", 0)] + \
                  [("m", m) for m in range(8, MX)] + [("z", j) for j in range(4)] + [("out", 1)]
        T_ORDER = [("x", 0, 0), ("x", 0, 1), ("x", 0, 2), ("x", 1, 0), ("x", 1, 1), ("x", 1, 2),
                   ("g", 0, 0), ("g", 0, 1), ("g", 1, 0), ("g", 1, 1), ("ln", 0), ("ln", 1)]

        def a_slot(n, key):
            if n == 0:
                return [k for k in A_ORDER if k[0] != "out"].index(key), 0
            order = A_ORDER if n != N else [k for k in A_ORDER if k[0] == "out"]
            return order.index(key), -2

        def a_wait(eng, sem_, n, key, back):
            r, off = a_slot(n, key)
            wait(eng, sem_, n, A_USES, off + r + back)
            return accs[r % 2]

        def t_slot(n, key):
            if n == -1:
                return key[1], 0, 0
            if n == 0:
                return key[1], 2, 0
            order = T_ORDER if not (isinstance(n, int) and n >= N - 1) else [k for k in T_ORDER if k[0] != "ln"]
            return order.index(key), -8 - (2 if n == N else 0), n

        def t_wait(eng, sem_, n, key, back):
            r, off, m = t_slot(n, key)
            wait(eng, sem_, m, T_USES, off + r + back)
            return tps[(r + off) % 2]

        block = ctx.enter_context(nc.Block())

        def turns(engine, prologue, turn):
            prologue()
            for n in range(3):
                turn(n, n % 2)
            pairs = (N - 1 - 3) // 2
            with engine.Fori(0, pairs) as i:
                turn((i, 2, 3), 1)
                turn((i, 2, 4), 0)
            for n in range(3 + 2 * pairs, N + 1):
                turn(n, n % 2)

        def has_own(n):
            return not (isinstance(n, int) and n == N)

        def wq_slots(n):
            jobs = T.wq.shape[0] // P
            assert jobs == 2 * N + 1
            return range(2) if has_own(n) else range(1)

        def wq_rows(t, n, s):
            return t[bass.ds(count(n, 2 * P, s * P), P), :]

        def has_before(n):
            return not (isinstance(n, int) and n == 0)

        def has_next(n):
            return not (isinstance(n, int) and n >= N - 1)

        @block.sync
        def _(sp):
            def rows(t, b, n, c):
                return t[b][bass.ds(start_token(n, SC) + c * P, P), :]

            def load_x(n, b):
                if n != 0:
                    r, off, m = t_slot(-1 if n == 1 else before(before(n)), ("ln", 1))
                    wait_apart(sp, t_filled, m, T_USES, off + r + 1)
                for c in range(NC):
                    sp.dma_start(A.xl[c][:], rows(x_d, b, n, c)).then_inc(x_in[c], 16)

            def prologue():
                setup.sync(sp, lambda: load_x(0, 0))

            def load_wq(n, s):
                wait_apart(sp, measured, n, 4, 2 * s - 2)
                wait_apart(sp, wq_out[s], n, 16, 0)
                sp.dma_start(A.wst[s][:].bitcast(I32), wq_rows(T.wq, n, s)).then_inc(wq_in[s], 16)

            def store_wq(n, s):
                wait_apart(sp, widened, n, 2, s + 1)
                sp.dma_start(wq_rows(T.wf, n, s), A.wst[s][:]).then_inc(wq_out[s], 16)

            def turn(n, b):
                u = before(n)
                if has_next(n):
                    load_x(after(n), 1 - b)
                if has_before(n):
                    for c in range(NC):
                        wait_apart(sp, x1_out[c], u, 16, 0)
                        sp.dma_start(A.xr[c][:], rows(x_d, 1 - b, u, c)).then_inc(resid_in, 16)
                for s in wq_slots(n):
                    load_wq(n, s)
                if has_own(n):
                    wait_apart(sp, sums_step, n, 3, 3)
                    for c in range(NC):
                        wait_apart(sp, cs_in[c], u, 16, 16)
                    sp.dma_start(T.cs_d.rearrange("c h l -> h c l"), A.csT[:]).then_inc(cs_out, 16)
                    wait_apart(sp, cs_out, n, 16, 16)
                for c in range(NC):
                    if has_own(n):
                        wait_apart(sp, ydiag_done, u, 2 * NC, 2 * (c + 1))
                        sp.dma_start(A.L[c][:].rearrange("p h l -> p (h l)"),
                                     T.cs_d[c].rearrange("h l -> (h l)").rearrange("(a x) -> a x", a=1)
                                     .broadcast_to([P, H * P])).then_inc(cs_in[c], 16)
                    if c == 0:
                        for s in wq_slots(n):
                            store_wq(n, s)
                    if has_before(n):
                        wait_apart(sp, out_step, u, 2 * NC, 2 * (c + 1))
                        sp.dma_start(rows(x1_d, 1 - b, u, c), A.xr[c][:]).then_inc(x1_out[c], 16)

            turns(sp, prologue, turn)
            for c in range(NC):
                sp.wait_ge(x1_out[c], N * 16)
            for s in range(2):
                sp.wait_ge(wq_out[s], (N + 1 - s) * 16)

        @block.gpsimd
        def _(pool):
            def rstd(n):
                for c in range(NC):
                    wait(pool, stats_step, n, 2 * NC, 2 * (c + 1))
                    wait_apart(pool, normed, before(n), NC, c + 1)
                    nc.gpsimd.tensor_scalar(A.rstd[:, c:c + 1], A.mv[c][:, 1:2], 1.0, EPS, ALU.mult, ALU.add) \
                        .then_inc(rstd_step, 1)
                    wait(pool, rstd_step, n, 2 * NC, 2 * c + 1)
                    nc.gpsimd.tensor_tensor(A.rstd[:, c:c + 1], A.rstd[:, c:c + 1], T.neg_half[:], ALU.pow) \
                        .then_inc(rstd_step, 1)

            def times_D(n, u, c):
                t_wait(pool, t_emptied, n, ("x", c, 1), 1)
                wait(pool, sq_done, u, NC, c)
                if c == 0 and has_own(n):
                    wait(pool, split, n, 2 * NC, 2 * NC)
                nc.gpsimd.tensor_tensor(A.XD[:].rearrange("p (h d) -> p h d", h=H),
                                        A.X[:].rearrange("p (h d) -> p h d", h=H),
                                        A.Drow[:].unsqueeze(2).broadcast_to([P, H, HD]), ALU.mult).then_inc(XD_done, 1)

            def gate(n, u, b, c):
                wait(pool, yoff_read, u, 2 * NC, 2 * c + 2)
                wait(pool, ydiag_read, u, 2 * NC, 2 * c + 2)
                nc.gpsimd.tensor_tensor(A.yt[:], A.yt[:], A.XD[:], ALU.add).then_inc(y_summed, 1)
                wait(pool, y_summed, u, NC, c + 1)
                a_wait(pool, a_emptied, u, ("z", 2 * c + 1), 1)
                nc.gpsimd.tensor_tensor(A.yt[:, 0:Z], A.yt[:, 0:Z], A.siluz[:, c, :], ALU.mult)
                wait(pool, siluq_done, u, 1, 1)
                nc.gpsimd.tensor_tensor(A.yt[:, Z:], A.yt[:, Z:], A.zdt[1 - b][:, c, 0:ZQ], ALU.mult).then_inc(gated, 1)

            def inv_rms(n, u, c):
                if u != 0:
                    r, off = a_slot(u, ("out", c))
                    wait_apart(pool, a_emptied, u, A_USES, off + r + 1)
                wait_apart(pool, sq_done, u, NC, c + 1)
                nc.gpsimd.tensor_scalar(A.rs[:, c:c + 1], A.ssq[:, c:c + 1], 1.0 / DI, EPS, ALU.mult, ALU.add) \
                    .then_inc(rs_step, 1)
                wait(pool, rs_step, u, 2 * NC, 2 * c + 1)
                nc.gpsimd.tensor_tensor(A.rs[:, c:c + 1], A.rs[:, c:c + 1], T.neg_half[:], ALU.pow).then_inc(rs_step, 1)

            def residual(n, u, b, c):
                a_wait(pool, a_emptied, n, ("out", c), 1)
                nc.gpsimd.tensor_tensor(A.ob[:], A.ob[:], T.gate_row[1 - b][:], ALU.mult).then_inc(out_step, 1)
                wait(pool, out_step, u, 2 * NC, 2 * c + 1)
                wait(pool, resid_in, u, NC * 16, NC * 16)
                nc.gpsimd.tensor_tensor(A.xr[c][:], A.ob[:], A.xr[c][:], ALU.add).then_inc(out_step, 1)

            def turn(n, b):
                u = before(n)
                own, bef, nxt = has_own(n), has_before(n), has_next(n)
                if bef:
                    times_D(n, u, 0)
                    gate(n, u, b, 0)
                    inv_rms(n, u, 0)
                    times_D(n, u, 1)
                if nxt:
                    rstd(after(n))
                if bef:
                    residual(n, u, b, 0)
                    gate(n, u, b, 1)
                    inv_rms(n, u, 1)
                    residual(n, u, b, 1)

            turns(pool, lambda: setup.gpsimd(pool, lambda: rstd(0)), turn)

        @block.scalar
        def _(act):
            def evac_ln(n, b, turn_n):
                for j in range(2):
                    ps = t_wait(act, t_filled, turn_n, ("ln", j), 1)
                    if j == 0 and turn_n != -1:
                        wait(act, sq_done, before(turn_n), NC, NC)
                    for q in range(2):
                        k = 2 * j + q
                        last = nc.scalar.activation(h32[:, k, :], ps[:, q * SC:(q + 1) * SC], ACT.Identity,
                                                    bias=T.modc[:, 0, k, b:b + 1], scale=T.modc[:, 1, k, b:b + 1])
                    last.then_inc(t_emptied, 1)

            def widen(n, s):
                wait(act, wq_in[s], n, 16, 16)
                nc.scalar.activation(A.wst[s][:], A.wst[s][:].bitcast(I32), ACT.Copy, bias=-ZERO_POINT) \
                    .then_inc(widened, 1)

            def evac_tile(n, b, m):
                ps = a_wait(act, a_filled, n, ("m", m), 1)
                wait(act, tail_step, n, 2, 0)
                wait(act, yoff_done, before(n), 2 * NC, 0)
                nc.scalar.activation(A.raw[:, m, 3:3 + SC], ps[:, 0:SC], ACT.Copy)
                nc.scalar.activation(A.xc[b][:, m, :], ps[:, 0:SC], ACT.Identity, bias=A.bconv[:, m:m + 1],
                                     scale=A.wconv[:, m, 3:4]).then_inc(a_emptied, 1)

            def silu_tile(n, b, m):
                wait(act, conv_step, n, 3 * MX, 3 * (m + 1))
                x = A.xc[b][:, m, :]
                nc.scalar.activation(x, x, ACT.Silu).then_inc(silu_done, 1)

            def silu_z(n, j):
                ps = a_wait(act, a_filled, n, ("z", j), 1)
                c, f = divmod(j, 2)
                e = min((f + 1) * W, Z)
                wait(act, gated, n, NC, c + 1 - NC)
                nc.scalar.activation(A.siluz[:, c, f * W:e], ps[:, 0:e - f * W], ACT.Silu).then_inc(a_emptied, 1)

            def evac_zdt(n, b, c):
                ps = a_wait(act, a_filled, n, ("zdt", c), 1)
                if c == 0:
                    wait(act, gated, before(n), NC, 0)
                    wait(act, softplus_step, before(n), SP_STEPS, 0)
                nc.scalar.activation(A.zdt[b][:, c, :], ps[:, 0:ZQ + H], ACT.Copy).then_inc(a_emptied, 1)

            def silu_q(n, b):
                a_wait(act, a_emptied, n, ("zdt", 1), 1)
                z = A.zdt[b][:, :, 0:ZQ]
                nc.scalar.activation(z, z, ACT.Silu).then_inc(siluq_done, 1)

            def evac_x(n, u, c):
                for f in range(2):
                    ps = t_wait(act, t_filled, n, ("x", c, f), 1)
                    if f == 0:
                        wait(act, ydiag_done, u, 2 * NC, 2 * c)
                        wait(act, state_done, u, 2 * NC, 2 * c)
                        wait(act, Xdec_done, u, NC, c)
                        wait(act, XD_done, u, NC, c)
                    nc.scalar.activation(A.X[:, f * W:(f + 1) * W], ps[:, 0:W], ACT.Copy).then_inc(t_emptied, 1)

            def evac_B(n, u, c):
                ps = t_wait(act, t_filled, n, ("x", c, 2), 1)
                wait(act, state_done, u, 2 * NC, 2 * c)
                nc.scalar.activation(A.Btok[:], ps[:, 0:P], ACT.Copy).then_inc(t_emptied, 1)

            def evac_g(n, u, c):
                for f in range(2):
                    ps = t_wait(act, t_filled, n, ("g", c, f), 1)
                    if f == 0:
                        if c:
                            a_wait(act, a_filled, n, ("out", 0), 1)
                        elif u != 0:
                            a_wait(act, a_filled, u, ("out", 1), 1)
                    nc.scalar.activation(A.gT[:, 4 * f:4 * f + 4, :].rearrange("p k t -> p (k t)"), ps[:, 0:W],
                                         ACT.Copy).then_inc(t_emptied, 1)

            def exp_sums(u):
                wait(act, sums_step, u, 3, 3)
                wait(act, S_step, u, 4 * NC, 0)
                wait(act, Xdec_done, u, NC, 0)
                wait(act, yoff_read, u, 2 * NC, 0)
                nc.scalar.activation(A.e3[:], A.s3[:], ACT.Exp).then_inc(e3_done, 1)

            def exp_decay(u, c, f):
                wait(act, diff_done, u, 2 * NC, 2 * c + f + 1)
                x = A.L[c][:, f * HH:(f + 1) * HH, :]
                nc.scalar.activation(x, x, ACT.Exp).then_inc(decay_done, 1)

            def exp_dt(n):
                wait(act, softplus_step, n, SP_STEPS, 2)
                nc.scalar.activation(A.sp[1][:], A.sp[1][:], ACT.Exp).then_inc(edt_done, 1)

            def square(u, c):
                wait(act, gated, u, NC, c + 1)
                wait(act, rs_step, u, 2 * NC, 2 * c + 2 - 2 * NC)
                nc.scalar.activation(A.XD[:], A.yt[:], ACT.Square, accum_out=A.ssq[:, c:c + 1]).then_inc(sq_done, 1)

            def scale_out(n, u, c):
                ps = a_wait(act, a_filled, n, ("out", c), 1)
                wait(act, rs_step, u, 2 * NC, 2 * c + 2)
                wait(act, out_step, u, 2 * NC, 2 * c)
                nc.scalar.activation(A.ob[:], ps[:], ACT.Identity, scale=A.rs[:, c:c + 1]).then_inc(a_emptied, 1)

            def turn(n, b):
                u = before(n)
                own, bef, nxt = has_own(n), has_before(n), has_next(n)
                if own:
                    evac_zdt(n, b, 0)
                if bef:
                    evac_x(n, u, 0)
                if own:
                    evac_zdt(n, b, 1)
                if bef:
                    evac_B(n, u, 0)
                if own:
                    evac_tile(n, b, 0)
                    exp_dt(n)
                    evac_tile(n, b, 1)
                    evac_tile(n, b, 2)
                    evac_tile(n, b, 3)
                for s in wq_slots(n):
                    widen(n, s)
                if bef:
                    evac_x(n, u, 1)
                if own:
                    evac_tile(n, b, 4)
                if bef:
                    evac_B(n, u, 1)
                if own:
                    evac_tile(n, b, 5)
                if bef:
                    square(u, 0)
                    evac_g(n, u, 0)
                if own:
                    evac_tile(n, b, 6)
                    evac_tile(n, b, 7)
                    silu_tile(n, b, 0)
                    silu_q(n, b)
                    silu_tile(n, b, 1)
                    silu_tile(n, b, 2)
                if bef:
                    scale_out(n, u, 0)
                if own:
                    silu_tile(n, b, 3)
                    evac_tile(n, b, 8)
                    silu_tile(n, b, 4)
                    evac_tile(n, b, 9)
                    silu_tile(n, b, 5)
                    silu_z(n, 0)
                    silu_tile(n, b, 6)
                    silu_z(n, 1)
                if bef:
                    square(u, 1)
                if own:
                    silu_z(n, 2)
                if bef:
                    evac_g(n, u, 1)
                if own:
                    silu_tile(n, b, 7)
                    silu_z(n, 3)
                if nxt:
                    evac_ln(after(n), 1 - b, n)
                if own:
                    silu_tile(n, b, 8)
                    silu_tile(n, b, 9)
                    exp_sums(n)
                    exp_decay(n, 0, 0)
                    exp_decay(n, 0, 1)
                    exp_decay(n, 1, 0)
                    exp_decay(n, 1, 1)
                if bef:
                    scale_out(n, u, 1)

            turns(act, lambda: setup.scalar(act, lambda: evac_ln(0, 0, -1)), turn)

        @block.vector
        def _(dve):
            def stats(n, c):
                wait(dve, x_in[c], n, 16, 16)
                wait(dve, rstd_step, n, 2 * NC, 2 * c + 2 - 2 * NC)
                wait(dve, normed, before(n), NC, c + 1)
                wait(dve, stats_step, n, 2 * NC, 2 * c + 2 - 2 * NC)
                nc.vector.bn_stats(A.bst[c][:], A.xl[c][:]).then_inc(stats_step, 1)
                wait_apart(dve, stats_step, n, 2 * NC, 2 * c + 1)
                nc.vector.bn_aggr(A.mv[c][:], A.bst[c][:]).then_inc(stats_step, 1)

            def norm(n, turn_n, c):
                wait(dve, rstd_step, n, 2 * NC, 2 * c + 2)
                nc.vector.tensor_scalar(A.xl[c][:], A.xl[c][:], A.mv[c][:, 0:1], A.rstd[:, c:c + 1],
                                        ALU.subtract, ALU.mult).then_inc(normed, 1)

            def split_h(n, turn_n, c):
                t_wait(dve, t_emptied, turn_n, ("ln", 1), 1)
                if turn_n != -1:
                    a_wait(dve, a_filled, turn_n, ("z", 3), 1)
                wait(dve, split, n, 2 * NC, 2 * c)
                s = slice(c * P, (c + 1) * P)
                h = h32[:, :, s]
                nc.vector.tensor_copy(A.hThi[:, :, s], h).then_inc(split, 1)
                wait(dve, split, n, 2 * NC, 2 * c + 1)
                nc.vector.tensor_tensor(A.hTlo[:, :, s], h, A.hThi[:, :, s].bitcast(F32),
                                        ALU.subtract).then_inc(split, 1)

            def conv(n, b, m):
                a_wait(dve, a_emptied, n, ("m", m), 1)
                for j in range(3):
                    if j:
                        wait(dve, conv_step, n, 3 * MX, 3 * m + j)
                    nc.vector.scalar_tensor_tensor(A.xc[b][:, m, :], A.raw[:, m, j:j + SC], A.wconv[:, m, j:j + 1],
                                                   A.xc[b][:, m, :], ALU.mult, ALU.add).then_inc(conv_step, 1)

            def tails(n, b):
                wait(dve, conv_step, n, 3 * MX, 3 * MX)
                wait(dve, tail_step, n, 2, 0)
                nc.vector.tensor_copy(A.tail[b][:], A.raw[:, :, SC:SC + 3]).then_inc(tail_step, 1)
                nc.vector.tensor_copy(A.raw[:, :, 0:3], A.tail[1 - b][:]).then_inc(tail_step, 1)

            sp0, sp1, sp2, sp3, sp4, sp5 = A.sp

            def dt_first(n, b):
                a_wait(dve, a_emptied, n, ("zdt", 1), 1)
                wait(dve, softplus_step, n, SP_STEPS, 0)
                nc.vector.tensor_tensor(sp0[:], A.zdt[b][:, :, ZQ:ZQ + H],
                                        A.dtb[:].unsqueeze(1).broadcast_to([P, NC, H]), ALU.add) \
                    .then_inc(softplus_step, 1)
                wait(dve, softplus_step, n, SP_STEPS, 1)
                nc.vector.scalar_tensor_tensor(sp1[:], sp0[:], -1.0, sp0[:], ALU.mult, ALU.min).then_inc(softplus_step, 1)

            def softplus(n):
                wait(dve, edt_done, n, 1, 1)
                step = [2]

                def did(ins):
                    ins.then_inc(softplus_step, 1)
                    step[0] += 1
                    wait(dve, softplus_step, n, SP_STEPS, step[0])

                did(nc.vector.tensor_scalar(sp2[:], sp1[:], 2.0, None, ALU.add))
                did(nc.vector.reciprocal(sp2[:], sp2[:]))
                did(nc.vector.tensor_tensor(sp3[:], sp1[:], sp2[:], ALU.mult))
                did(nc.vector.tensor_tensor(sp4[:], sp3[:], sp3[:], ALU.mult))
                did(nc.vector.tensor_scalar(sp5[:], sp4[:], 1.0 / 15.0, None, ALU.mult))
                for k in (13, 11, 9, 7, 5, 3):
                    did(nc.vector.scalar_tensor_tensor(sp5[:], sp5[:], 1.0 / k, sp4[:], ALU.add, ALU.mult))
                did(nc.vector.scalar_tensor_tensor(sp5[:], sp5[:], 1.0, sp3[:], ALU.add, ALU.mult))
                did(nc.vector.tensor_scalar(sp0[:], sp0[:], 0.0, None, ALU.max))
                did(nc.vector.scalar_tensor_tensor(sp5[:], sp5[:], 2.0, sp0[:], ALU.mult, ALU.add))
                nc.vector.tensor_tensor(A.a[:], sp5[:], A.negA[:].unsqueeze(1).broadcast_to([P, NC, H]),
                                        ALU.mult).then_inc(softplus_step, 1)

            def sums(n):
                wait(dve, cs_done, n, 1, 1)
                wait(dve, e3_done, n, 1, 0)
                wait(dve, cs_out, n, 16, 0)
                wait(dve, diff_done, n, 2 * NC, 0)
                nc.vector.tensor_copy(A.s3[:, 0:2 * NC * H], small[:, 0:2 * NC * H]).then_inc(sums_step, 1)
                wait(dve, sums_step, n, 3, 1)
                nc.vector.tensor_tensor(A.s3[:, 2 * NC * H:3 * NC * H], A.s3[:, NC * H:2 * NC * H],
                                        A.s3[:, 0:NC * H], ALU.subtract).then_inc(sums_step, 1)
                nc.vector.tensor_copy(A.csT[:].rearrange("h c l -> h (c l)"), small[0:H, 2 * P:2 * P + NC * P]) \
                    .then_inc(sums_step, 1)

            def diff(u, c, f):
                if f == 0:
                    wait(dve, cs_in[c], u, 16, 16)
                    wait(dve, sums_step, u, 3, 3)
                for h in range(f * HH, (f + 1) * HH):
                    last = nc.vector.tensor_scalar(A.L[c][:, h, :], A.L[c][:, h, :], A.s3[:, c * H + h:c * H + h + 1],
                                                   0.0, ALU.subtract, ALU.min)
                last.then_inc(diff_done, 1)

            def mask_G(u):
                wait(dve, G_done, u, 1, 1)
                wait(dve, M_done, u, 2 * NC, 0)
                nc.vector.tensor_tensor(A.Gm[:], small[:, 0:NC * P].rearrange("p (c l) -> p c l", c=NC),
                                        A.triu[:].unsqueeze(1).broadcast_to([P, NC, P]), ALU.mult).then_inc(G_masked, 1)

            def scores(u, c, f):
                if c == 0 and f == 0:
                    wait(dve, G_masked, u, 1, 1)
                wait(dve, decay_done, u, 2 * NC, 2 * c + f + 1)
                x = A.L[c][:, f * HH:(f + 1) * HH, :]
                nc.vector.tensor_tensor(x, x, A.Gm[:, c, :].unsqueeze(1).broadcast_to([P, HH, P]), ALU.mult) \
                    .then_inc(M_done, 1)

            def e3(kind, c, f):
                o = kind * NC * H + c * H + f * HH
                return A.e3[:, o:o + HH].unsqueeze(2).broadcast_to([P, HH, HD])

            def heads(x, f):
                return x[:, f * W:(f + 1) * W].rearrange("p (h d) -> p h d", h=HH)

            def decay_X(n, u, c):
                t_wait(dve, t_emptied, n, ("x", c, 1), 1)
                wait(dve, e3_done, u, 1, 1)
                wait(dve, state_done, u, 2 * NC, 2 * c)
                o = 2 * NC * H + c * H
                nc.vector.tensor_tensor(A.Xd[:].rearrange("p (h d) -> p h d", h=H),
                                        A.X[:].rearrange("p (h d) -> p h d", h=H),
                                        A.e3[:, o:o + H].unsqueeze(2).broadcast_to([P, H, HD]),
                                        ALU.mult).then_inc(Xdec_done, 1)

            def read_yoff(n, u, b, c, f):
                wait(dve, yoff_done, u, 2 * NC, 2 * c + f + 1)
                if f == 0:
                    if c:
                        t_wait(dve, t_filled, n, ("g", 0, 1), 1)
                    elif u != 0:
                        t_wait(dve, t_filled, u, ("g", 1, 1), 1)
                    wait(dve, sq_done, u, NC, c)
                    wait(dve, e3_done, u, 1, 1)
                nc.vector.tensor_tensor(heads(A.yt, f), yoff[:, 0:W].rearrange("p (h d) -> p h d", h=HH), e3(0, c, f),
                                        ALU.mult).then_inc(yoff_read, 1)
                nc.vector.tensor_tensor(heads(A.S[1 - b], f), heads(A.S[1 - b], f), e3(1, c, f),
                                        ALU.mult).then_inc(S_step, 1)

            def read_ydiag(u, c, f):
                wait(dve, ydiag_done, u, 2 * NC, 2 * c + f + 1)
                wait(dve, XD_done, u, NC, c + 1)
                nc.vector.tensor_tensor(A.XD[:, f * W:(f + 1) * W], ydiag[:, 0:W], A.XD[:, f * W:(f + 1) * W],
                                        ALU.add).then_inc(ydiag_read, 1)

            def read_state(u, b, c, f):
                wait(dve, state_done, u, 2 * NC, 2 * c + f + 1)
                wait(dve, S_step, u, 4 * NC, 4 * c + 2)
                s = A.S[1 - b][:, f * W:(f + 1) * W]
                nc.vector.tensor_tensor(s, state[:, 0:W], s, ALU.add).then_inc(S_step, 1)

            def measure(n, s):
                wait(dve, widened, n, 2, s + 1)
                wait(dve, measured, n, 4, 2 * s)
                nc.vector.tensor_reduce(A.wm1[:], A.wst[s][:], AX_X, ALU.max, apply_absolute_value=True) \
                    .then_inc(measured, 1)
                wait(dve, measured, n, 4, 2 * s + 1)
                nc.vector.tensor_tensor(T.wtop[:], T.wtop[:], A.wm1[:], ALU.max).then_inc(measured, 1)

            def normalise():
                for c in range(NC):
                    stats(0, c)
                for c in range(NC):
                    norm(0, -1, c)

            def prologue():
                setup.vector(dve, normalise, lambda: [split_h(0, -1, c) for c in range(NC)])

            def turn(n, b):
                u = before(n)
                own, bef, nxt = has_own(n), has_before(n), has_next(n)
                if bef:
                    mask_G(u)
                    scores(u, 0, 0)
                    read_yoff(n, u, b, 0, 0)
                    scores(u, 0, 1)
                    decay_X(n, u, 0)
                if own:
                    dt_first(n, b)
                if bef:
                    read_ydiag(u, 0, 0)
                    read_yoff(n, u, b, 0, 1)
                if own:
                    conv(n, b, 0)
                if bef:
                    read_ydiag(u, 0, 1)
                    read_state(u, b, 0, 0)
                if own:
                    softplus(n)
                if bef:
                    read_state(u, b, 0, 1)
                if own:
                    conv(n, b, 1)
                if bef:
                    scores(u, 1, 0)
                if own:
                    conv(n, b, 2)
                if bef:
                    decay_X(n, u, 1)
                    scores(u, 1, 1)
                if own:
                    sums(n)
                    conv(n, b, 3)
                for s in wq_slots(n):
                    measure(n, s)
                if bef:
                    read_yoff(n, u, b, 1, 0)
                if own:
                    conv(n, b, 4)
                    conv(n, b, 5)
                if bef:
                    read_ydiag(u, 1, 0)
                if nxt:
                    stats(after(n), 0)
                    stats(after(n), 1)
                if own:
                    conv(n, b, 6)
                if bef:
                    read_yoff(n, u, b, 1, 1)
                    read_ydiag(u, 1, 1)
                    read_state(u, b, 1, 0)
                if nxt:
                    norm(after(n), n, 0)
                    norm(after(n), n, 1)
                if own:
                    conv(n, b, 7)
                if bef:
                    read_state(u, b, 1, 1)
                if own:
                    conv(n, b, 8)
                    conv(n, b, 9)
                    tails(n, b)
                    diff(n, 0, 0)
                    diff(n, 0, 1)
                    diff(n, 1, 0)
                    diff(n, 1, 1)
                if nxt:
                    split_h(after(n), n, 0)
                    split_h(after(n), n, 1)

            turns(dve, prologue, turn)

        @block.tensor
        def _(pe):
            def transpose_ln(n, turn_n):
                for j in range(2):
                    ps = t_wait(pe, t_emptied, turn_n, ("ln", j), -1)
                    for c in range(NC):
                        if j == 0:
                            wait(pe, normed, n, NC, c + 1)
                        for q in range(2):
                            k = 2 * j + q
                            mm = nc.tensor.transpose(ps[:, q * SC + c * P:q * SC + (c + 1) * P],
                                                     A.xl[c][:, k * P:(k + 1) * P], A.ident[:])
                    mm.then_inc(t_filled, 1)

            def product(out, pairs, parts):
                last = len(pairs) * len(parts) - 1
                i = 0
                for wp, ap in parts:
                    for lhs, rhs in pairs:
                        mm = nc.tensor.matmul(out, lhs(wp, ap), rhs(wp, ap), start=(i == 0), stop=(i == last))
                        i += 1
                return mm

            def project_zdt(n, c):
                if c == 0:
                    wait(pe, split, n, 2 * NC, 2 * NC)
                ps = a_wait(pe, a_emptied, n, ("zdt", c), -1)
                s = slice(c * P, (c + 1) * P)
                mm = product(ps[:, 0:ZQ + H],
                             [(lambda w, a, k=k: hT[a][:, k, s], lambda w, a, k=k: Win[w][:, k, Z:Z + ZQ + H])
                              for k in range(KD)], PARTS)
                mm.then_inc(a_filled, 1)

            def project_tile(n, m):
                ps = a_wait(pe, a_emptied, n, ("m", m), -1)
                o = X0 + m * P
                mm = product(ps[:, 0:SC],
                             [(lambda w, a, k=k: Win[w][:, k, o:o + P], lambda w, a, k=k: hT[a][:, k, :])
                              for k in range(KD)], PARTS)
                mm.then_inc(a_filled, 1)

            def project_z(n, j):
                ps = a_wait(pe, a_emptied, n, ("z", j), -1)
                c, f = divmod(j, 2)
                s = slice(c * P, (c + 1) * P)
                o, e = f * W, min((f + 1) * W, Z)
                mm = product(ps[:, 0:e - o],
                             [(lambda w, a, k=k: hT[a][:, k, s], lambda w, a, k=k: Win[w][:, k, o:e])
                              for k in range(KD)], PARTS)
                mm.then_inc(a_filled, 1)

            def scores_G(n, u, b):
                wait(pe, silu_done, u, MX, MX)
                wait(pe, sums_step, n, 3, 0)
                for c in range(NC):
                    s = slice(c * P, (c + 1) * P)
                    mm = nc.tensor.matmul(small[:, c * P:(c + 1) * P], A.xc[1 - b][:, MX - 2, s],
                                          A.xc[1 - b][:, MX - 1, s], start=True, stop=True)
                mm.then_inc(G_done, 1)

            def cumulate(n):
                wait(pe, softplus_step, n, SP_STEPS, SP_STEPS)
                wait(pe, G_masked, n, 1, 0)
                for c in range(NC):
                    nc.tensor.matmul(small[:, c * H:(c + 1) * H], A.triu[:], A.a[:, c, :], start=True, stop=True)
                for c in range(NC):
                    nc.tensor.matmul(small[:, (NC + c) * H:(NC + c + 1) * H], A.ones[:], A.a[:, c, :],
                                     start=True, stop=True)
                for c in range(NC):
                    mm = nc.tensor.matmul(small[0:H, (2 + c) * P:(3 + c) * P], A.a[:, c, :], A.triu[:],
                                          start=True, stop=True)
                mm.then_inc(cs_done, 1)

            def transpose_x(n, u, b, c):
                s = slice(c * P, (c + 1) * P)
                for f in range(2):
                    ps = t_wait(pe, t_emptied, n, ("x", c, f), -1)
                    for q in range(4):
                        mm = nc.tensor.transpose(ps[:, q * P:(q + 1) * P], A.xc[1 - b][:, 4 * f + q, s], A.ident[:])
                    mm.then_inc(t_filled, 1)

            def transpose_B(n, u, b, c):
                s = slice(c * P, (c + 1) * P)
                ps = t_wait(pe, t_emptied, n, ("x", c, 2), -1)
                nc.tensor.transpose(ps[:, 0:P], A.xc[1 - b][:, MX - 2, s], A.ident[:]).then_inc(t_filled, 1)

            def y_off(u, b, c, f):
                s = slice(c * P, (c + 1) * P)
                wait(pe, yoff_read, u, 2 * NC, 2 * c + f)
                if c:
                    wait(pe, S_step, u, 4 * NC, 4 * c)
                else:
                    wait(pe, S_step, before(u), 4 * NC, 0)
                nc.tensor.matmul(yoff[:, 0:W], A.xc[1 - b][:, MX - 1, s], A.S[1 - b][:, f * W:(f + 1) * W],
                                 start=True, stop=True).then_inc(yoff_done, 1)

            def y_diag(n, u, c, f):
                wait(pe, M_done, u, 2 * NC, 2 * c + f + 1)
                t_wait(pe, t_emptied, n, ("x", c, f), 1)
                wait(pe, ydiag_read, u, 2 * NC, 2 * c + f)
                for h in range(HH):
                    g = f * HH + h
                    mm = nc.tensor.matmul(ydiag[:, h * HD:(h + 1) * HD], A.L[c][:, g, :],
                                          A.X[:, g * HD:(g + 1) * HD], start=True, stop=True)
                mm.then_inc(ydiag_done, 1)

            def states(n, u, c, f):
                wait(pe, Xdec_done, u, NC, c + 1)
                t_wait(pe, t_emptied, n, ("x", c, 2), 1)
                if f:
                    wait(pe, S_step, u, 4 * NC, 4 * c + 3)
                else:
                    wait(pe, S_step, u, 4 * NC, 4 * c)
                nc.tensor.matmul(state[:, 0:W], A.Btok[:], A.Xd[:, f * W:(f + 1) * W],
                                 start=True, stop=True).then_inc(state_done, 1)

            def transpose_g(n, u, c):
                wait(pe, gated, u, NC, c + 1)
                for f in range(2):
                    ps = t_wait(pe, t_emptied, n, ("g", c, f), -1)
                    for q in range(4):
                        k = 4 * f + q
                        mm = nc.tensor.transpose(ps[:, q * P:(q + 1) * P], A.yt[:, k * P:(k + 1) * P], A.ident[:])
                    mm.then_inc(t_filled, 1)

            def project_out(n, c):
                t_wait(pe, t_emptied, n, ("g", c, 1), 1)
                if n == 1:
                    pe.wait_ge(setup.wout_scaled, KI)
                ps = a_wait(pe, a_emptied, n, ("out", c), -1)
                for k in range(KI):
                    mm = nc.tensor.matmul(ps[:], A.gT[:, k, :], A.Wo[:, k, :], start=(k == 0), stop=(k == KI - 1))
                mm.then_inc(a_filled, 1)

            def turn(n, b):
                u = before(n)
                own, bef, nxt = has_own(n), has_before(n), has_next(n)
                if bef:
                    scores_G(n, u, b)
                    y_off(u, b, 0, 0)
                if own:
                    project_zdt(n, 0)
                if bef:
                    transpose_x(n, u, b, 0)
                if own:
                    project_zdt(n, 1)
                if bef:
                    transpose_B(n, u, b, 0)
                    y_off(u, b, 0, 1)
                if own:
                    project_tile(n, 0)
                if bef:
                    y_diag(n, u, 0, 0)
                if own:
                    project_tile(n, 1)
                if bef:
                    y_diag(n, u, 0, 1)
                    states(n, u, 0, 0)
                if own:
                    project_tile(n, 2)
                if bef:
                    states(n, u, 0, 1)
                if own:
                    project_tile(n, 3)
                if bef:
                    transpose_x(n, u, b, 1)
                if own:
                    project_tile(n, 4)
                if bef:
                    transpose_B(n, u, b, 1)
                if own:
                    cumulate(n)
                if bef:
                    y_off(u, b, 1, 0)
                if own:
                    project_tile(n, 5)
                if bef:
                    y_diag(n, u, 1, 0)
                    transpose_g(n, u, 0)
                if own:
                    project_tile(n, 6)
                    project_tile(n, 7)
                if bef:
                    project_out(n, 0)
                    y_off(u, b, 1, 1)
                    y_diag(n, u, 1, 1)
                    states(n, u, 1, 0)
                if own:
                    project_tile(n, 8)
                if bef:
                    states(n, u, 1, 1)
                if own:
                    project_tile(n, 9)
                    project_z(n, 0)
                    project_z(n, 1)
                    project_z(n, 2)
                if bef:
                    transpose_g(n, u, 1)
                if own:
                    project_z(n, 3)
                if nxt:
                    transpose_ln(after(n), n)
                if bef:
                    project_out(n, 1)

            turns(pe, lambda: setup.tensor(pe, lambda: transpose_ln(0, -1)), turn)


def feed_forward_stage(nc, T, B):
    D, HID = T.D, T.HID
    KD, KH = D // P, HID // P
    SC = T.SC2
    NC = SC // P
    N = 2 * T.S // SC
    with ExitStack() as ctx:
        sem = lambda name: ctx.enter_context(nc.semaphore(name))
        resid_in = sem("ff_resid_in")
        x_in, out_sent = ([sem(f"{s}{c}") for c in range(NC)] for s in ("ff_x_in", "ff_out_sent"))
        t_filled, t_emptied = sem("ff_t_filled"), sem("ff_t_emptied")
        gate_done, up_done, down_done, gate_read, hid_step = (
            sem(s) for s in ("gate_done", "up_done", "down_done", "gate_read", "hid_step"))
        stats_step, rstd_step, normed, split, down_read, summed = (
            sem(s) for s in ("ff_stats_step", "ff_rstd_step", "ff_normed", "ff_split", "down_read", "summed"))
        flag_step, flag_turned = sem("flag_step"), sem("flag_turned")
        rows_spread, rows_done, rows_read = sem("ff_rows_spread"), sem("ff_rows_done"), sem("ff_rows_read")
        tps, gates, ups, downs = B.psum[0:2], B.psum[2:4], B.psum[4:6], B.psum[6:8]
        HID_GROUPS = ((0, 1), (1, 3), (3, 7), (7, KH))
        DOWN_GROUPS = ((0, KH // 2), (KH // 2, KH))
        hid_w_in = [sem(f"hid_w_in{g}") for g in range(len(HID_GROUPS))]
        down_w_in = [sem(f"down_w_in{g}") for g in range(len(DOWN_GROUPS))]
        w_rows = T.wf.shape[0] // 3
        w_flat = [T.wf[j * w_rows:(j + 1) * w_rows, :].rearrange("a b -> (a b)") for j in range(3)]
        wg_d, wu_d = (w.rearrange("(k p n) -> p k n", p=P, n=HID) for w in w_flat[0:2])
        wd_d = w_flat[2].rearrange("(k p n) -> p k n", p=P, n=D)
        block = ctx.enter_context(nc.Block())

        def turns(engine, prologue, turn):
            prologue()
            turn(0, 0)
            pairs = (N - 2) // 2
            with engine.Fori(0, pairs) as i:
                turn((i, 2, 1), 1)
                turn((i, 2, 2), 0)
            for n in range(1 + 2 * pairs, N):
                turn(n, n % 2)

        def has_next(n):
            return not (isinstance(n, int) and n == N - 1)

        @block.sync
        def _(sp):
            def rows(t, b, n, c):
                return t[b][bass.ds(start_token(n, SC) + c * P, P), :]

            def load_x(n, b):
                for c in range(NC):
                    wait_apart(sp, normed, before(n), NC, c + 1)
                    sp.dma_start(B.xl[c][:], rows(T.x1, b, n, c)).then_inc(x_in[c], 16)

            def turn(n, b):
                if has_next(n):
                    load_x(after(n), 1 - b)
                for c in range(NC):
                    wait_apart(sp, out_sent[c], n, 16, 0)
                    sp.dma_start(B.xr[c][:], rows(T.x1, b, n, c)).then_inc(resid_in, 16)
                for c in range(NC):
                    wait_apart(sp, summed, n, NC, c + 1)
                    sp.dma_start(rows(T.out, b, n, c), B.xr[c][:]).then_inc(out_sent[c], 16)

            turns(sp, lambda: load_x(0, 0), turn)
            for c in range(NC):
                sp.wait_ge(out_sent[c], N * 16)

        @block.gpsimd
        def _(pool):
            def rstd(n):
                for c in range(NC):
                    wait(pool, stats_step, n, 2 * NC, 2 * (c + 1))
                    wait_apart(pool, normed, before(n), NC, c + 1)
                    nc.gpsimd.tensor_scalar(B.rstd[:, c:c + 1], B.mv[c][:, 1:2], 1.0, EPS, ALU.mult, ALU.add) \
                        .then_inc(rstd_step, 1)
                    wait(pool, rstd_step, n, 2 * NC, 2 * c + 1)
                    nc.gpsimd.tensor_tensor(B.rstd[:, c:c + 1], B.rstd[:, c:c + 1], T.neg_half[:], ALU.pow) \
                        .then_inc(rstd_step, 1)

            def turn(n, b):
                if has_next(n):
                    rstd(after(n))
                for c in range(NC):
                    wait(pool, down_read, n, NC, c + 1)
                    wait(pool, resid_in, n, NC * 16, NC * 16)
                    nc.gpsimd.tensor_tensor(B.xr[c][:], B.ob[c % 2][:], B.xr[c][:], ALU.add).then_inc(summed, 1)

            def prologue():
                for g, (m0, m1) in enumerate(HID_GROUPS):
                    s = slice(m0 * P, m1 * P)
                    for w, src in ((B.Wg, wg_d), (B.Wu, wu_d)):
                        pool.dma_start(w[:, :, s].bitcast(F32), src[:, :, s]).then_inc(hid_w_in[g], 16)
                for g, (m0, m1) in enumerate(DOWN_GROUPS):
                    pool.dma_start(B.Wd[:, m0:m1, :].bitcast(F32), wd_d[:, m0:m1, :]).then_inc(down_w_in[g], 16)
                rstd(0)

            turns(pool, prologue, turn)

        @block.scalar
        def _(act):
            def evac_ln(n, b):
                for k in range(KD):
                    wait(act, t_filled, n, KD, k + 1)
                    if k == 0:
                        wait(act, split, n, 2 * KD, 0)
                    nc.scalar.activation(B.h32[:, k, :], tps[k % 2][:], ACT.Identity, bias=T.modc[:, 2, k, b:b + 1],
                                         scale=T.modc[:, 3, k, b:b + 1]).then_inc(t_emptied, 1)

            def turn(n, b):
                for m in range(KH):
                    wait(act, gate_done, n, KH, m + 1)
                    wait(act, hid_step, n, 3 * KH, 3 * (m - 2) + 1)
                    nc.scalar.activation(B.sg[m % 2][:], gates[m % 2][:], ACT.Silu, scale=T.sgate[:, m:m + 1]) \
                        .then_inc(gate_read, 1)
                    if m == 7 and has_next(n):
                        evac_ln(after(n), 1 - b)

            turns(act, lambda: evac_ln(0, 0), turn)

        @block.vector
        def _(dve):
            def stats(n, c):
                wait(dve, x_in[c], n, 16, 16)
                wait(dve, rstd_step, n, 2 * NC, 2 * c + 2 - 2 * NC)
                wait(dve, normed, before(n), NC, c + 1)
                wait(dve, stats_step, n, 2 * NC, 2 * c + 2 - 2 * NC)
                nc.vector.bn_stats(B.bst[c][:], B.xl[c][:]).then_inc(stats_step, 1)
                wait_apart(dve, stats_step, n, 2 * NC, 2 * c + 1)
                nc.vector.bn_aggr(B.mv[c][:], B.bst[c][:]).then_inc(stats_step, 1)

            def norm(n, c):
                wait(dve, rstd_step, n, 2 * NC, 2 * c + 2)
                wait(dve, t_filled, n, KD, 0)
                nc.vector.tensor_scalar(B.hn[c][:], B.xl[c][:], B.mv[c][:, 0:1], B.rstd[:, c:c + 1],
                                        ALU.subtract, ALU.mult).then_inc(normed, 1)

            def split_h(n):
                for k in range(KD):
                    wait(dve, t_emptied, n, KD, k + 1)
                    if k == 0:
                        wait(dve, up_done, n, KH, 0)
                        wait(dve, split, n, 2 * KD, 0)
                    nc.vector.tensor_copy(B.hThi[:, k, :], B.h32[:, k, :]).then_inc(split, 1)
                    wait(dve, split, n, 2 * KD, 2 * k + 1)
                    nc.vector.tensor_tensor(B.hTlo[:, k, :], B.h32[:, k, :], B.hThi[:, k, :].bitcast(F32),
                                            ALU.subtract).then_inc(split, 1)

            def hidden(n, m):
                wait(dve, gate_read, n, KH, m + 1)
                wait(dve, up_done, n, KH, m + 1)
                wait(dve, hid_step, n, 3 * KH, 3 * (m - 1))
                if m == 0:
                    wait(dve, down_done, n, NC, 0)
                nc.vector.scalar_tensor_tensor(B.hid[m % 2][:], ups[m % 2][:], T.sup[:, m:m + 1], B.sg[m % 2][:],
                                               ALU.mult, ALU.mult).then_inc(hid_step, 1)
                wait(dve, hid_step, n, 3 * KH, 3 * m + 1)
                nc.vector.tensor_copy(B.hidhi[:, m, :], B.hid[m % 2][:]).then_inc(hid_step, 1)
                wait(dve, hid_step, n, 3 * KH, 3 * m + 2)
                nc.vector.tensor_tensor(B.hidlo[:, m, :], B.hid[m % 2][:], B.hidhi[:, m, :].bitcast(F32),
                                        ALU.subtract).then_inc(hid_step, 1)

            def prologue():
                for b in range(2):
                    spread_gate(nc, dve, B.hid[b][:].rearrange("p (k j) -> p k j", k=KD), T.gate2c[:, :, b],
                                rows_spread)
                dve.wait_ge(flag_turned, 1)
                nc.vector.tensor_reduce(B.top1[:], gates[0][0:1, 0:P], AX_X, ALU.max).then_inc(flag_step, 1)
                dve.wait_ge(flag_step, 1)
                nc.vector.tensor_scalar(B.flag[:], B.top1[:], EXACT_INT, None, ALU.is_gt).then_inc(flag_step, 1)
                for b in range(2):
                    dve.wait_ge(rows_done, b + 1)
                    nc.vector.tensor_copy(B.gate_row[b][:], downs[b][:]).then_inc(rows_read, 1)
                dve.wait_ge(rows_read, 2)
                for c in range(NC):
                    stats(0, c)
                for c in range(NC):
                    norm(0, c)
                split_h(0)

            def turn(n, b):
                for m in range(KH):
                    hidden(n, m)
                    if has_next(n) and 1 <= m <= NC:
                        stats(after(n), m - 1)
                        if m == NC:
                            for c in range(NC):
                                norm(after(n), c)
                if has_next(n):
                    split_h(after(n))
                for c in range(NC):
                    wait(dve, down_done, n, NC, c + 1)
                    wait(dve, summed, n, NC, c - 1)
                    nc.vector.tensor_tensor(B.ob[c % 2][:], downs[c % 2][:], B.gate_row[b][:], ALU.mult) \
                        .then_inc(down_read, 1)

            turns(dve, prologue, turn)

        @block.tensor
        def _(pe):
            def transpose_ln(n):
                for k in range(KD):
                    wait(pe, t_emptied, n, KD, k - 1)
                    if k == 0:
                        wait(pe, normed, n, NC, NC)
                    for c in range(NC):
                        mm = nc.tensor.transpose(tps[k % 2][:, c * P:(c + 1) * P], B.hn[c][:, k * P:(k + 1) * P],
                                                 B.ident[:])
                    mm.then_inc(t_filled, 1)

            def program(dt):

                def project(ps, W, m):
                    for k in range(KD):
                        for a, h in enumerate((B.hThi, B.hTlo)):
                            mm = nc.tensor.matmul(ps[:], W[:, k, m * P:(m + 1) * P].bitcast(dt),
                                                  h[:, k, :].bitcast(dt),
                                                  start=(k == 0 and a == 0), stop=(k == KD - 1 and a == 1))
                    return mm

                def turn(n, b):
                    wait(pe, split, n, 2 * KD, 2 * KD)
                    for m in range(KH):
                        if n == 0:
                            for g, (m0, m1) in enumerate(HID_GROUPS):
                                if m == m0:
                                    pe.wait_ge(hid_w_in[g], 32)
                        wait(pe, gate_read, n, KH, m - 1)
                        project(gates[m % 2], B.Wg, m).then_inc(gate_done, 1)
                        wait(pe, hid_step, n, 3 * KH, 3 * (m - 2) + 1)
                        project(ups[m % 2], B.Wu, m).then_inc(up_done, 1)
                        if m == 7 and has_next(n):
                            transpose_ln(after(n))
                    if n == 0:
                        for g in range(len(DOWN_GROUPS)):
                            pe.wait_ge(down_w_in[g], 16)
                    for c in range(NC):
                        wait(pe, down_read, n, NC, c - 1)
                        s = slice(c * P, (c + 1) * P)
                        for m in range(KH):
                            if c == 0:
                                wait(pe, hid_step, n, 3 * KH, 3 * (m + 1))
                            for a, h in enumerate((B.hidhi, B.hidlo)):
                                mm = nc.tensor.matmul(downs[c % 2][:], h[:, m, s].bitcast(dt), B.Wd[:, m, :].bitcast(dt),
                                                      start=(m == 0 and a == 0), stop=(m == KH - 1 and a == 1))
                        mm.then_inc(down_done, 1)

                turns(pe, lambda: transpose_ln(0), turn)

            nc.tensor.transpose(gates[0][0:1, 0:P], T.wtop[:], B.ident[:]).then_inc(flag_turned, 1)
            for b in range(2):
                pe.wait_ge(rows_spread, b + 1)
                for k in range(KD):
                    mm = nc.tensor.matmul(downs[b][:, k * P:(k + 1) * P], B.hid[b][:, k * P:(k + 1) * P], B.ident[:],
                                          start=True, stop=True)
                mm.then_inc(rows_done, 1)
            pe.wait_ge(flag_step, 2)
            pe.wait_ge(rows_read, 2)
            wide = pe.value_load(B.flag[0:1, 0:1], min_val=0, max_val=1)
            with pe.If(wide == 0):
                program(FR)
            with pe.Else():
                program(F32)


def adaln_block(nc, T):
    T.D, T.DI, T.CD, T.H, T.HD, T.S, T.HID = 512, 1024, 1280, 16, 64, 2048, 1408
    T.NIN = T.DI + T.CD + T.H
    T.SC, T.SC2 = 256, 512
    T.ZQ = 256
    KD, KI, MX, KH = T.D // P, T.DI // P, T.CD // P, T.HID // P
    NC = T.SC // P
    T.x1 = nc.dram_tensor("x1_scratch", [2, T.S, T.D], F32, kind="Internal").ap()
    T.wf = nc.dram_tensor("widened_scratch", list(T.wq.shape), F32, kind="Internal").ap()
    T.cs_d = nc.dram_tensor("sums_scratch", [NC, T.H, P], F32, kind="Internal").ap()
    with ExitStack() as outer:
        def sb(ctx, name, shape, dt=F32):
            return ctx.enter_context(nc.sbuf_tensor(name, shape, dt))

        psum = [outer.enter_context(nc.psum_tensor(f"bank{i}", [P, 512], F32)) for i in range(8)]
        T.modc = sb(outer, "modc", [P, 4, KD, 2])
        T.neg_half = sb(outer, "neg_half", [P, 1])
        T.gate2c, T.wtop = sb(outer, "gate2_cols", [P, KD, 2]), sb(outer, "wtop", [P, 1])
        T.sgate, T.sup = sb(outer, "sgate", [P, KH]), sb(outer, "sup", [P, KH])
        ident = sb(outer, "ident", [P, P])

        with ExitStack() as ctx:
            A = Tensors()
            A.psum, A.ident = psum, ident
            T.gate_row = [sb(ctx, f"gate_row{b}", [P, T.D]) for b in range(2)]
            A.triu, A.ones = sb(ctx, "triu", [P, P]), sb(ctx, "ones", [P, P])
            A.Whi, A.Wlo = sb(ctx, "W_in_high", [P, KD, T.NIN], FR), sb(ctx, "W_in_low", [P, KD, T.NIN], FR)
            A.Wo = sb(ctx, "W_out", [P, KI, T.D])
            A.cT, A.sc = sb(ctx, "cT", [P, KD, 2]), sb(ctx, "silu_c", [P, KD, 2])
            A.wconv, A.bconv = sb(ctx, "wconv", [P, MX, 4]), sb(ctx, "bconv", [P, MX])
            A.normw, A.sdown = sb(ctx, "normw", [P, KI]), sb(ctx, "sdown", [P, KD])
            A.gate1c, A.gtmp = sb(ctx, "gate1_cols", [P, KD, 2]), [sb(ctx, f"gate_sign{i}", [P, KD, 2]) for i in range(2)]
            A.wst, A.wm1 = [sb(ctx, f"wq_rows{s}", [P, 512]) for s in range(2)], sb(ctx, "wmax", [P, 1])
            A.dtb, A.negA, A.Drow = sb(ctx, "dt_bias", [P, T.H]), sb(ctx, "negA", [P, T.H]), sb(ctx, "Drow", [P, T.H])
            A.xl = [sb(ctx, f"x_tile{c}", [P, T.D]) for c in range(NC)]
            A.xr = [sb(ctx, f"x_resid{c}", [P, T.D]) for c in range(NC)]
            A.ob = sb(ctx, "branch", [P, T.D])
            A.bst = [sb(ctx, f"bn_stats{c}", [P, 6]) for c in range(NC)]
            A.mv = [sb(ctx, f"mean_var{c}", [P, 2]) for c in range(NC)]
            A.rstd, A.rs, A.ssq = (sb(ctx, s, [P, NC]) for s in ("rstd", "inv_rms", "square_sum"))
            A.hThi, A.hTlo = sb(ctx, "h_high", [P, KD, T.SC], FR), sb(ctx, "h_low", [P, KD, T.SC], FR)
            A.raw = sb(ctx, "conv_in", [P, MX, 3 + T.SC])
            A.tail = [sb(ctx, f"conv_tail{b}", [P, MX, 3]) for b in range(2)]
            A.xc = [sb(ctx, f"xBC{b}", [P, MX, T.SC]) for b in range(2)]
            A.siluz = sb(ctx, "silu_z", [P, NC, T.DI - T.ZQ])
            A.zdt = [sb(ctx, f"z_dt{b}", [P, NC, T.ZQ + T.H]) for b in range(2)]
            A.sp = [sb(ctx, f"softplus{j}", [P, NC, T.H]) for j in range(6)]
            A.a = sb(ctx, "dtA", [P, NC, T.H])
            A.s3, A.e3 = sb(ctx, "sums", [P, 3 * NC * T.H]), sb(ctx, "exp_sums", [P, 3 * NC * T.H])
            A.csT = sb(ctx, "sumsT", [T.H, NC, P])
            A.L = [sb(ctx, f"decay{c}", [P, T.H, P]) for c in range(NC)]
            A.Gm = sb(ctx, "G_masked", [P, NC, P])
            A.X, A.Xd, A.XD = (sb(ctx, s, [P, T.DI]) for s in ("X", "X_decayed", "X_D"))
            A.Btok = sb(ctx, "B_rows", [P, P])
            A.yt = sb(ctx, "y", [P, T.DI])
            A.gT = sb(ctx, "gT", [P, KI, P])
            A.S = [sb(ctx, f"state{b}", [P, T.DI]) for b in range(2)]
            A.gsp = [A.X[:, b * T.D:(b + 1) * T.D].rearrange("p (k j) -> p k j", k=KD) for b in range(2)]
            mixer_stage(nc, T, A)

        with ExitStack() as ctx:
            B = Tensors()
            NC2 = T.SC2 // P
            B.psum, B.ident = psum, ident
            B.Wg, B.Wu = sb(ctx, "W_gate", [P, KD, T.HID], FR), sb(ctx, "W_up", [P, KD, T.HID], FR)
            B.Wd = sb(ctx, "W_down", [P, KH, T.D], FR)
            B.top1 = sb(ctx, "top1", [1, 1])
            B.gate_row = [sb(ctx, f"gate2_row{b}", [P, T.D]) for b in range(2)]
            B.flag = sb(ctx, "wide_flag", [1, 1], I32)
            B.xl = [sb(ctx, f"ff_x_tile{c}", [P, T.D]) for c in range(NC2)]
            B.xr = [sb(ctx, f"ff_x_resid{c}", [P, T.D]) for c in range(NC2)]
            B.hn = [sb(ctx, f"ff_normed{c}", [P, T.D]) for c in range(NC2)]
            B.ob = [sb(ctx, f"ff_branch{c}", [P, T.D]) for c in range(2)]
            B.bst = [sb(ctx, f"ff_bn_stats{c}", [P, 6]) for c in range(NC2)]
            B.mv = [sb(ctx, f"ff_mean_var{c}", [P, 2]) for c in range(NC2)]
            B.rstd = sb(ctx, "ff_rstd", [P, NC2])
            B.h32 = sb(ctx, "ff_h", [P, KD, T.SC2])
            B.hThi, B.hTlo = sb(ctx, "ff_h_high", [P, KD, T.SC2], FR), sb(ctx, "ff_h_low", [P, KD, T.SC2], FR)
            B.sg = [sb(ctx, f"silu_gate{j}", [P, T.SC2]) for j in range(2)]
            B.hid = [sb(ctx, f"hidden{j}", [P, T.SC2]) for j in range(2)]
            B.hidhi, B.hidlo = (sb(ctx, s, [P, KH, T.SC2], FR) for s in ("hidden_high", "hidden_low"))
            feed_forward_stage(nc, T, B)


def kernel(**inputs):
    import numpy as np
    import concourse.bacc as bacc
    from concourse.bass_utils import run_bass_kernel_spmd

    nc = bacc.Bacc("TRN2", target_bir_lowering=False, num_devices=1)
    arrays = {}

    def put(name, a):
        a = np.ascontiguousarray(a)
        arrays[name] = a
        return nc.dram_tensor(name, a.shape, mybir.dt.from_np(a.dtype), kind="ExternalInput").ap()

    T = Tensors()
    T.x = put("x", inputs["L0_attn_u"])
    w_in = np.asarray(inputs["L0_attn_W_in"]).T
    h = np.asarray(inputs["L0_attn_dt_bias"]).shape[0]
    di = np.asarray(inputs["L0_attn_norm_w"]).shape[0]
    T.winT = put("W_inT", np.concatenate([w_in[:, :di], w_in[:, -h:], w_in[:, di:-h]], axis=1))
    T.woutT = put("W_outT", np.asarray(inputs["L0_attn_W_out"]).T)
    T.wconv = put("W_conv", inputs["L0_attn_W_conv"])
    T.bconv = put("b_conv", inputs["L0_attn_b_conv"])
    T.dtb = put("dt_bias_in", inputs["L0_attn_dt_bias"])
    T.alog = put("A_log", inputs["L0_attn_A_log"])
    T.Dp = put("Dp", inputs["L0_attn_Dp"])
    T.normw = put("norm_w", inputs["L0_attn_norm_w"])
    wq = [np.ascontiguousarray(np.asarray(inputs[f"L0_ffn_wq_{w}"]).T).reshape(-1, 512) for w in ("gate", "up", "down")]
    T.wq = put("wqT", np.concatenate(wq, axis=0))
    T.sgate_in = put("s_gate", inputs["L0_ffn_s_gate"])
    T.sup_in = put("s_up", inputs["L0_ffn_s_up"])
    T.sdown = put("s_down", inputs["L0_ffn_s_down"])
    T.cT = put("cT_in", np.asarray(inputs["L0_c"]).T)
    T.wmod = put("w_mod", inputs["L0_wmod"])
    T.out = nc.dram_tensor("out", inputs["L0_attn_u"].shape, F32, kind="ExternalOutput").ap()
    adaln_block(nc, T)
    r = run_bass_kernel_spmd(nc, [arrays], core_ids=[0])
    return r.results[0]["out"]
```

```python
from contextlib import ExitStack

import concourse.bass as bass
from concourse import mybir

F32 = mybir.dt.float32
FR = mybir.dt.float32r
I32 = mybir.dt.int32
ALU = mybir.AluOpType
ACT = mybir.ActivationFunctionType
AX_X = mybir.AxisListType.X

P = 128
EPS = 1e-5
FLOOR = 0.25
ZERO_POINT = 128.0
EXACT_INT = 4096.0


def count(n, per, c):
    if isinstance(n, tuple):
        i, a, b = n
        return i * (a * per) + (b * per + c)
    return n * per + c


def before(n):
    return (n[0], n[1], n[2] - 1) if isinstance(n, tuple) else n - 1


def after(n):
    return (n[0], n[1], n[2] + 1) if isinstance(n, tuple) else n + 1


def wait(eng, sem, n, per, c):
    v = count(n, per, c)
    if isinstance(v, int) and v <= 0:
        return
    eng.wait_ge(sem, v)


def wait_apart(eng, sem, n, per, c):
    v = count(n, per, c)
    if isinstance(v, int):
        wait(eng, sem, n, per, c)
        return
    v = eng.snap(eng.to_reg(v))
    eng.wait_ge(sem, 1)
    eng.wait_ge(sem, v)


def start_token(n, size):
    if isinstance(n, tuple):
        i, a, b = n
        return i * size + (b // 2) * size
    return (n // 2) * size


class Tensors:
    pass


def spread_gate(nc, dve, out, cols, done):
    nc.vector.tensor_copy(out, cols.unsqueeze(2).broadcast_to([P, out.shape[1], P])).then_inc(done, 1)


class Setup:

    SMALL = 9

    def __init__(self, nc, T, A, sem):
        self.nc, self.T, self.A = nc, T, A
        self.c_in, self.params_in, self.wout_in = sem("c_in"), sem("params_in"), sem("wout_in")
        self.mod_in = [sem(f"mod_in{s}") for s in range(6)]
        self.win_in = [sem(f"win_in{k}") for k in range(T.D // P)]
        self.silu_c_done, self.cols_done, self.cols_read = sem("silu_c_done"), sem("cols_done"), sem("cols_read")
        self.gate_step, self.spread_done, self.rows_done, self.rows_read = (
            sem(s) for s in ("gate_step", "spread_done", "rows_done", "rows_read"))
        self.win_high, self.win_low, self.const_step = sem("win_high"), sem("win_low"), sem("const_step")
        self.a_done, self.a_ready, self.wout_scaled = sem("a_done"), sem("a_ready"), sem("wout_scaled")
        self.wout_high, self.wout_low = sem("wout_high"), sem("wout_low")
        self.wo_stage = [A.yt[:, 0:T.D], A.yt[:, T.D:2 * T.D], A.ob[:], A.xr[:]]
        KD = T.D // P
        flat = lambda t: t[:, :, :].rearrange("p a b -> p (a b)")
        whole = [flat(t)[:, 0:KD * T.D].rearrange("p (k n) -> p k n", n=T.D) for t in (A.L[0], A.L[1])]
        self.wm = [whole[s % 2] for s in range(6)]
        self.stage = [[(flat(t)[:, 0:T.NIN], 0, T.NIN)] for t in (A.xc[0], A.xc[1], A.raw)] + \
                     [[(t[:, 0:min(T.DI, T.NIN - o)], o, min(o + T.DI, T.NIN))
                       for t, o in ((A.S[0], 0), (A.S[1], T.DI), (A.yt, 2 * T.DI))]]
        self.cols = [A.psum[bank][:, 0:2 * KD].rearrange("p (k b) -> p k b", b=2) for bank in (5, 6, 7, 5, 6, 7)]
        self.gates = {2: A.gate1c, 5: T.gate2c}

    def sync(self, sp, load_x):
        nc, T, A = self.nc, self.T, self.A
        w_mod = T.wmod.rearrange("(k p) (s n) -> s p k n", p=P, s=6)

        def section(s):
            sp.dma_start(self.wm[s], w_mod[s]).then_inc(self.mod_in[s], 16)

        def win(k):
            for buf, n0, n1 in self.stage[k]:
                sp.dma_start(buf, T.winT[k * P:(k + 1) * P, n0:n1]).then_inc(self.win_in[k], 16)

        with nc.allow_non_contiguous_dma(reason="small parameters"):
            sp.dma_start(A.cT[:], T.cT.rearrange("(k p) b -> p k b", p=P)).then_inc(self.c_in, 16)
            section(0)
            section(1)
            load_x()
            win(0)
            sp.dma_start(A.wconv[:], T.wconv.rearrange("(m p) o k -> p m (o k)", p=P)).then_inc(self.params_in, 16)
            for w, src in ((A.bconv, T.bconv), (A.normw, T.normw), (T.sgate, T.sgate_in), (T.sup, T.sup_in),
                           (A.sdown, T.sdown)):
                sp.dma_start(w[:], src.rearrange("(m p) -> p m", p=P)).then_inc(self.params_in, 16)
            for row, src in ((A.dtb, T.dtb), (A.negA, T.alog), (A.Drow, T.Dp)):
                sp.dma_start(row[:], src.rearrange("(a h) -> a h", a=1).broadcast_to([P, src.shape[0]])) \
                    .then_inc(self.params_in, 16)
            for k in range(1, T.D // P):
                win(k)
            for s in range(2, 6):
                sp.wait_ge(self.cols_done, s - 1)
                section(s)
                if s == 3:
                    KH = T.DI // P // 2
                    sp.wait_ge(self.win_low, T.D // P)
                    for k in range(KH):
                        sp.dma_start(self.wo_stage[k], T.woutT[k * P:(k + 1) * P, :]).then_inc(self.wout_in, 16)
                    sp.dma_start(A.Wo[:], T.woutT[KH * P:, :].rearrange("(k p) n -> p k n", p=P)) \
                        .then_inc(self.wout_in, 16)

    def gpsimd(self, pool, rstd):
        nc, T, A = self.nc, self.T, self.A
        step = self.const_step
        nc.gpsimd.memset(A.ident[:], 0.0).then_inc(step, 1)
        nc.gpsimd.memset(A.triu[:], 1.0).then_inc(step, 1)
        nc.gpsimd.memset(T.neg_half[:], -0.5).then_inc(step, 1)
        nc.gpsimd.memset(A.ones[:], 1.0).then_inc(step, 1)
        pool.wait_ge(step, 4)
        nc.gpsimd.affine_select(out=A.ident[:], in_=A.ident[:], compare_op=ALU.not_equal, fill=1.0,
                                base=0, pattern=[[-1, P]], channel_multiplier=1).then_inc(step, 1)
        nc.gpsimd.affine_select(out=A.triu[:], in_=A.triu[:], compare_op=ALU.is_ge, fill=0.0,
                                base=0, pattern=[[1, P]], channel_multiplier=-1).then_inc(step, 1)
        nc.gpsimd.memset(T.wtop[:], 0.0).then_inc(step, 1)
        for b in range(2):
            nc.gpsimd.memset(A.tail[b][:], 0.0).then_inc(step, 1)
        rstd()
        pool.wait_ge(self.win_low, 3)
        nc.gpsimd.memset(A.raw[:, :, 0:3], 0.0).then_inc(step, 1)
        pool.wait_ge(self.win_low, 4)
        for b in range(2):
            nc.gpsimd.memset(A.S[b][:], 0.0).then_inc(step, 1)
        pool.wait_ge(self.params_in, 16 * self.SMALL)
        pool.wait_ge(self.wout_in, 16 * (len(self.wo_stage) + 1))
        for k, w in enumerate(self.wo_stage + [A.Wo[:, k, :] for k in range(T.DI // P - len(self.wo_stage))]):
            nc.gpsimd.tensor_scalar(w, w, A.normw[:, k:k + 1], None, ALU.mult).then_inc(self.wout_scaled, 1)

    def scalar(self, act, evac_ln):
        nc, T, A = self.nc, self.T, self.A
        act.wait_ge(self.c_in, 16)
        nc.scalar.activation(A.sc[:], A.cT[:], ACT.Silu).then_inc(self.silu_c_done, 1)
        for k in range(T.D // P):
            if k == T.D // P - 1:
                act.wait_ge(self.cols_read, 2)
                evac_ln()
            act.wait_ge(self.win_in[k], 16 * len(self.stage[k]))
            for buf, n0, n1 in self.stage[k]:
                last = nc.scalar.activation(A.Whi[:, k, n0:n1], buf, ACT.Copy)
            last.then_inc(self.win_high, 1)
        act.wait_ge(self.params_in, 16 * self.SMALL)
        nc.scalar.activation(A.negA[:], A.negA[:], ACT.Exp).then_inc(self.a_done, 1)
        act.wait_ge(self.win_low, T.D // P)
        act.wait_ge(self.const_step, 10)

    def scalar_turn0(self, act):
        for k, w in enumerate(self.wo_stage):
            act.wait_ge(self.wout_scaled, k + 1)
            self.nc.scalar.activation(self.A.Wohi[:, k, :], w, ACT.Copy).then_inc(self.wout_high, 1)

    def vector(self, dve, normalise, split_h):
        nc, T, A = self.nc, self.T, self.A

        def low(k):
            dve.wait_ge(self.win_high, k + 1)
            for buf, n0, n1 in self.stage[k]:
                last = nc.vector.tensor_tensor(A.Wlo[:, k, n0:n1], buf, A.Whi[:, k, n0:n1].bitcast(F32), ALU.subtract)
            last.then_inc(self.win_low, 1)

        self.vectors(dve, 0)
        low(0)
        normalise()
        low(1)
        self.vectors(dve, 1)
        low(2)
        split_h()
        low(3)
        dve.wait_ge(self.a_done, 1)
        nc.vector.tensor_scalar(A.negA[:], A.negA[:], -1.0, None, ALU.mult).then_inc(self.a_ready, 1)
        dve.wait_ge(self.a_ready, 1)
        dve.wait_ge(self.const_step, 10)

    def vectors(self, dve, s):
        i = (0, 1, 3, 4).index(s)
        dve.wait_ge(self.cols_done, s + 1)
        self.nc.vector.tensor_scalar(self.T.modc[:, i], self.cols[s], float(i % 2), None, ALU.add) \
            .then_inc(self.cols_read, 1)

    def gate(self, dve, s):
        nc, g, i = self.nc, self.gates[s], (2, 5).index(s)
        t = self.A.gtmp[i]
        dve.wait_ge(self.cols_done, s + 1)
        nc.vector.tensor_scalar(t[:], self.cols[s], 0.0, 2.0, ALU.is_ge, ALU.mult).then_inc(self.gate_step, 1)
        dve.wait_ge(self.gate_step, 4 * i + 1)
        nc.vector.tensor_scalar(t[:], t[:], -1.0, None, ALU.add).then_inc(self.gate_step, 1)
        dve.wait_ge(self.gate_step, 4 * i + 2)
        nc.vector.tensor_tensor(g[:], self.cols[s], t[:], ALU.mult).then_inc(self.gate_step, 1)
        dve.wait_ge(self.gate_step, 4 * i + 3)
        nc.vector.scalar_tensor_tensor(g[:], g[:], FLOOR, t[:], ALU.max, ALU.mult).then_inc(self.gate_step, 1)
        dve.wait_ge(self.gate_step, 4 * i + 4)

    def vector_turn0(self, dve, part):
        nc, T, A = self.nc, self.T, self.A
        if part == 0:
            self.gate(dve, 2)
            self.vectors(dve, 3)
            for b in range(2):
                spread_gate(nc, dve, A.gsp[b], A.gate1c[:, :, b], self.spread_done)
            return
        self.vectors(dve, 4)
        self.gate(dve, 5)
        dve.wait_ge(self.params_in, 16 * self.SMALL)
        nc.vector.tensor_tensor(T.gate2c[:], T.gate2c[:], A.sdown[:].unsqueeze(2).broadcast_to([P, T.D // P, 2]),
                                ALU.mult).then_inc(self.gate_step, 1)
        for b in range(2):
            dve.wait_ge(self.rows_done, b + 1)
            nc.vector.tensor_copy(T.gate_row[b][:], A.psum[5 + b][:]).then_inc(self.rows_read, 1)
        for k, w in enumerate(self.wo_stage):
            dve.wait_ge(self.wout_high, k + 1)
            nc.vector.tensor_tensor(A.Wolo[:, k, :], w, A.Wohi[:, k, :].bitcast(F32), ALU.subtract) \
                .then_inc(self.wout_low, 1)
        dve.wait_ge(self.const_step, 12)
        dve.wait_ge(self.wout_low, len(self.wo_stage))

    def tensor(self, pe, transpose_ln):
        pe.wait_ge(self.silu_c_done, 1)
        self.section(pe, 0)
        self.section(pe, 1)
        pe.wait_ge(self.const_step, 6)
        transpose_ln()
        pe.wait_ge(self.win_low, self.T.D // P)

    def section(self, pe, s):
        KD = self.T.D // P
        pe.wait_ge(self.mod_in[s], 16)
        for k in range(KD):
            for q in range(KD):
                mm = self.nc.tensor.matmul(self.cols[s][:, k, :], self.wm[s][:, q, k * P:(k + 1) * P],
                                           self.A.sc[:, q, :], start=(q == 0), stop=(q == KD - 1))
        mm.then_inc(self.cols_done, 1)

    def tensor_turn0(self, pe, part):
        nc, T, A = self.nc, self.T, self.A
        KD = T.D // P
        if part == 0:
            pe.wait_ge(self.cols_read, 2)
            self.section(pe, 2)
            self.section(pe, 3)
            return
        self.section(pe, 4)
        pe.wait_ge(self.gate_step, 4)
        self.section(pe, 5)
        for b in range(2):
            pe.wait_ge(self.spread_done, b + 1)
            pe.wait_ge(self.cols_read, 3 + b)
            for k in range(KD):
                mm = nc.tensor.matmul(A.psum[5 + b][:, k * P:(k + 1) * P], A.gsp[b][:, k, :], A.ident[:],
                                      start=True, stop=True)
            mm.then_inc(self.rows_done, 1)
        pe.wait_ge(self.gate_step, 9)
        pe.wait_ge(self.rows_read, 2)
        pe.wait_ge(self.const_step, 12)


def mixer_stage(nc, T, A):
    D, DI, H, HD = T.D, T.DI, T.H, T.HD
    KD, KI = D // P, DI // P
    KH = KI // 2
    MX = T.CD // P
    SC, NC = T.SC, T.SC // P
    N = 2 * T.S // SC
    HH = H // 2
    W = HH * HD
    SP_STEPS = 17
    T_USES, A_USES = 12, 18
    X0 = DI + H
    ZQ = T.ZQ
    Z = DI - ZQ
    with ExitStack() as ctx:
        sem = lambda name: ctx.enter_context(nc.semaphore(name))
        setup = Setup(nc, T, A, sem)
        resid_in, cs_out = sem("resid_in"), sem("cs_out")
        wq_in, wq_out, widened, measured = (sem(s) for s in ("wq_in", "wq_out", "widened", "measured"))
        ghi_done, glo_done = sem("ghi_done"), sem("glo_done")
        x_in, cs_in, x1_out = ([sem(f"{s}{c}") for c in range(NC)] for s in ("x_in", "cs_in", "x1_out"))
        cs_done, G_done = sem("cs_done"), sem("G_done")
        a_filled, a_emptied = sem("a_filled"), sem("a_emptied")
        t_filled, t_emptied = sem("t_filled"), sem("t_emptied")
        yoff_done, ydiag_done, state_done = sem("yoff_done"), sem("ydiag_done"), sem("state_done")
        silu_done, siluq_done, e3_done, edt_done, decay_done, sq_done = (
            sem(s) for s in ("silu_done", "siluq_done", "e3_done", "edt_done", "decay_done", "sq_done"))
        stats_step, normed, split, conv_step, softplus_step, sums_step = (
            sem(s) for s in ("stats_step", "normed", "split", "conv_step", "softplus_step", "sums_step"))
        tail_step, diff_done, G_masked, M_done, Xdec_done = (
            sem(s) for s in ("tail_step", "diff_done", "G_masked", "M_done", "Xdec_done"))
        yoff_read, ydiag_read, S_step = sem("yoff_read"), sem("ydiag_read"), sem("S_step")
        rstd_step, XD_done, y_summed, gated, rs_step, out_step = (
            sem(s) for s in ("rstd_step", "XD_done", "y_summed", "gated", "rs_step", "out_step"))

        accs, tps = A.psum[0:2], A.psum[2:4]
        small, yoff, ydiag, state = A.psum[4:8]
        x_d, x1_d = T.x, T.x1
        hT = (A.hThi, A.hTlo)
        h32 = A.XD[:, :].rearrange("p (k t) -> p k t", k=KD)
        Win = (A.Whi, A.Wlo)
        gT, Wo = (A.gThi, A.gTlo), (A.Wohi, A.Wolo)
        PARTS = ((0, 0), (0, 1), (1, 0))

        A_ORDER = [("zdt", 0), ("zdt", 1)] + [("m", m) for m in range(9)] + [("out", 0)] + \
                  [("m", m) for m in range(9, MX)] + [("z", j) for j in range(4)] + [("out", 1)]
        T_ORDER = [("x", 0, 0), ("x", 0, 1), ("x", 0, 2), ("x", 1, 0), ("x", 1, 1), ("x", 1, 2),
                   ("g", 0, 0), ("g", 0, 1), ("g", 1, 0), ("g", 1, 1), ("ln", 0), ("ln", 1)]

        def a_slot(n, key):
            if n == 0:
                return [k for k in A_ORDER if k[0] != "out"].index(key), 0
            order = A_ORDER if n != N else [k for k in A_ORDER if k[0] == "out"]
            return order.index(key), -2

        def a_wait(eng, sem_, n, key, back):
            r, off = a_slot(n, key)
            wait(eng, sem_, n, A_USES, off + r + back)
            return accs[r % 2]

        def t_slot(n, key):
            if n == -1:
                return key[1], 0, 0
            if n == 0:
                return key[1], 2, 0
            order = T_ORDER if not (isinstance(n, int) and n >= N - 1) else [k for k in T_ORDER if k[0] != "ln"]
            return order.index(key), -8 - (2 if n == N else 0), n

        def t_wait(eng, sem_, n, key, back):
            r, off, m = t_slot(n, key)
            wait(eng, sem_, m, T_USES, off + r + back)
            return tps[(r + off) % 2]

        block = ctx.enter_context(nc.Block())

        def turns(engine, prologue, turn):
            prologue()
            for n in range(3):
                turn(n, n % 2)
            pairs = (N - 1 - 3) // 2
            with engine.Fori(0, pairs) as i:
                turn((i, 2, 3), 1)
                turn((i, 2, 4), 0)
            for n in range(3 + 2 * pairs, N + 1):
                turn(n, n % 2)

        def has_own(n):
            return not (isinstance(n, int) and n == N)

        assert T.wq.shape[0] // P == 2 * N + 1

        def wq_rows(t, n, s):
            return t[bass.ds(count(n, 2 * P, s * P), P), :]

        def has_before(n):
            return not (isinstance(n, int) and n == 0)

        def has_next(n):
            return not (isinstance(n, int) and n >= N - 1)

        @block.sync
        def _(sp):
            def rows(t, b, n, c):
                return t[b][bass.ds(start_token(n, SC) + c * P, P), :]

            def load_x(n, b):
                if n != 0:
                    r, off, m = t_slot(-1 if n == 1 else before(before(n)), ("ln", 1))
                    wait_apart(sp, t_filled, m, T_USES, off + r + 1)
                for c in range(NC):
                    sp.dma_start(A.xl[c][:], rows(x_d, b, n, c)).then_inc(x_in[c], 16)

            def prologue():
                setup.sync(sp, lambda: load_x(0, 0))

            def load_wq(n, s):
                wait_apart(sp, measured, n, 4, 2 * s)
                wait_apart(sp, wq_out, n, 32, 16 * s)
                sp.dma_start(A.wst[:].bitcast(I32), wq_rows(T.wq, n, s)).then_inc(wq_in, 16)

            def store_wq(n, s):
                wait_apart(sp, widened, n, 2, s + 1)
                sp.dma_start(wq_rows(T.wf, n, s), A.wst[:]).then_inc(wq_out, 16)

            def load_resid(u, b, c):
                if c:
                    wait_apart(sp, x1_out[0], u, 16, 16)
                else:
                    wait_apart(sp, x1_out[NC - 1], u, 16, 0)
                if u == 0 and c == 0:
                    sp.wait_ge(setup.wout_low, KI // 2)
                sp.dma_start(A.xr[:], rows(x_d, 1 - b, u, c)).then_inc(resid_in, 16)

            def turn(n, b):
                u = before(n)
                if has_next(n):
                    load_x(after(n), 1 - b)
                if has_before(n):
                    load_resid(u, b, 0)
                load_wq(n, 0)
                if has_own(n):
                    wait_apart(sp, sums_step, n, 3, 3)
                    for c in range(NC):
                        wait_apart(sp, cs_in[c], u, 16, 16)
                    sp.dma_start(T.cs_d.rearrange("c h l -> (c h) l"), A.csT[:]).then_inc(cs_out, 16)
                    wait_apart(sp, cs_out, n, 16, 16)
                if n == 0:
                    sp.wait_ge(setup.cols_done, 6)
                for c in range(NC):
                    if has_own(n):
                        wait_apart(sp, ydiag_done, u, 2 * NC, 2 * (c + 1))
                        sp.dma_start(A.L[c][:].rearrange("p h l -> p (h l)"),
                                     T.cs_d[c].rearrange("h l -> (h l)").rearrange("(a x) -> a x", a=1)
                                     .broadcast_to([P, H * P])).then_inc(cs_in[c], 16)
                    if c == 0:
                        store_wq(n, 0)
                    elif has_own(n):
                        load_wq(n, 1)
                    if has_before(n):
                        wait_apart(sp, out_step, u, 2 * NC, 2 * (c + 1))
                        sp.dma_start(rows(x1_d, 1 - b, u, c), A.xr[:]).then_inc(x1_out[c], 16)
                        if c == 0:
                            load_resid(u, b, 1)
                if has_own(n):
                    store_wq(n, 1)

            turns(sp, prologue, turn)
            for c in range(NC):
                sp.wait_ge(x1_out[c], N * 16)
            sp.wait_ge(wq_out, (2 * N + 1) * 16)

        @block.gpsimd
        def _(pool):
            def rstd(n):
                for c in range(NC):
                    wait(pool, stats_step, n, 2 * NC, 2 * (c + 1))
                    wait_apart(pool, normed, before(n), NC, c + 1)
                    nc.gpsimd.tensor_scalar(A.rstd[:, c:c + 1], A.mv[c][:, 1:2], 1.0, EPS, ALU.mult, ALU.add) \
                        .then_inc(rstd_step, 1)
                    wait(pool, rstd_step, n, 2 * NC, 2 * c + 1)
                    nc.gpsimd.tensor_tensor(A.rstd[:, c:c + 1], A.rstd[:, c:c + 1], T.neg_half[:], ALU.pow) \
                        .then_inc(rstd_step, 1)

            def times_D(n, u, c):
                t_wait(pool, t_emptied, n, ("x", c, 1), 1)
                wait(pool, sq_done, u, NC, c)
                if c == 0 and has_own(n):
                    wait(pool, split, n, 2 * NC, 2 * NC)
                nc.gpsimd.tensor_tensor(A.XD[:].rearrange("p (h d) -> p h d", h=H),
                                        A.X[:].rearrange("p (h d) -> p h d", h=H),
                                        A.Drow[:].unsqueeze(2).broadcast_to([P, H, HD]), ALU.mult).then_inc(XD_done, 1)

            def gate(n, u, b, c):
                wait(pool, yoff_read, u, 2 * NC, 2 * c + 2)
                wait(pool, ydiag_read, u, 2 * NC, 2 * c + 2)
                nc.gpsimd.tensor_tensor(A.yt[:], A.yt[:], A.XD[:], ALU.add).then_inc(y_summed, 1)
                wait(pool, y_summed, u, NC, c + 1)
                a_wait(pool, a_emptied, u, ("z", 2 * c + 1), 1)
                nc.gpsimd.tensor_tensor(A.yt[:, 0:Z], A.yt[:, 0:Z], A.siluz[:, c, :], ALU.mult)
                wait(pool, siluq_done, u, 1, 1)
                nc.gpsimd.tensor_tensor(A.yt[:, Z:], A.yt[:, Z:], A.zdt[1 - b][:, c, 0:ZQ], ALU.mult).then_inc(gated, 1)

            def inv_rms(n, u, c):
                if u != 0:
                    r, off = a_slot(u, ("out", c))
                    wait_apart(pool, a_emptied, u, A_USES, off + r + 1)
                wait_apart(pool, sq_done, u, NC, c + 1)
                nc.gpsimd.tensor_scalar(A.rs[:, c:c + 1], A.ssq[:, c:c + 1], 1.0 / DI, EPS, ALU.mult, ALU.add) \
                    .then_inc(rs_step, 1)
                wait(pool, rs_step, u, 2 * NC, 2 * c + 1)
                nc.gpsimd.tensor_tensor(A.rs[:, c:c + 1], A.rs[:, c:c + 1], T.neg_half[:], ALU.pow).then_inc(rs_step, 1)

            def residual(n, u, b, c):
                a_wait(pool, a_emptied, n, ("out", c), 1)
                nc.gpsimd.tensor_tensor(A.ob[:], A.ob[:], T.gate_row[1 - b][:], ALU.mult).then_inc(out_step, 1)
                wait(pool, out_step, u, 2 * NC, 2 * c + 1)
                wait(pool, resid_in, u, NC * 16, (c + 1) * 16)
                nc.gpsimd.tensor_tensor(A.xr[:], A.ob[:], A.xr[:], ALU.add).then_inc(out_step, 1)

            def turn(n, b):
                u = before(n)
                own, bef, nxt = has_own(n), has_before(n), has_next(n)
                if bef:
                    times_D(n, u, 0)
                    gate(n, u, b, 0)
                    inv_rms(n, u, 0)
                    times_D(n, u, 1)
                if nxt:
                    rstd(after(n))
                if bef:
                    residual(n, u, b, 0)
                    gate(n, u, b, 1)
                    inv_rms(n, u, 1)
                    residual(n, u, b, 1)

            turns(pool, lambda: setup.gpsimd(pool, lambda: rstd(0)), turn)

        @block.scalar
        def _(act):
            def evac_ln(n, b, turn_n):
                for j in range(2):
                    ps = t_wait(act, t_filled, turn_n, ("ln", j), 1)
                    if j == 0 and turn_n != -1:
                        wait(act, sq_done, before(turn_n), NC, NC)
                    for q in range(2):
                        k = 2 * j + q
                        last = nc.scalar.activation(h32[:, k, :], ps[:, q * SC:(q + 1) * SC], ACT.Identity,
                                                    bias=T.modc[:, 0, k, b:b + 1], scale=T.modc[:, 1, k, b:b + 1])
                    last.then_inc(t_emptied, 1)

            def widen(n, s):
                wait(act, wq_in, n, 32, 16 * (s + 1))
                nc.scalar.activation(A.wst[:], A.wst[:].bitcast(I32), ACT.Copy, bias=-ZERO_POINT) \
                    .then_inc(widened, 1)

            def evac_tile(n, b, m):
                ps = a_wait(act, a_filled, n, ("m", m), 1)
                wait(act, tail_step, n, 2, 0)
                wait(act, yoff_done, before(n), 2 * NC, 0)
                nc.scalar.activation(A.raw[:, m, 3:3 + SC], ps[:, 0:SC], ACT.Copy)
                nc.scalar.activation(A.xc[b][:, m, :], ps[:, 0:SC], ACT.Identity, bias=A.bconv[:, m:m + 1],
                                     scale=A.wconv[:, m, 3:4]).then_inc(a_emptied, 1)

            def silu_tile(n, b, m):
                wait(act, conv_step, n, 3 * MX, 3 * (m + 1))
                x = A.xc[b][:, m, :]
                nc.scalar.activation(x, x, ACT.Silu).then_inc(silu_done, 1)

            def silu_z(n, j):
                ps = a_wait(act, a_filled, n, ("z", j), 1)
                c, f = divmod(j, 2)
                e = min((f + 1) * W, Z)
                wait(act, gated, n, NC, c + 1 - NC)
                nc.scalar.activation(A.siluz[:, c, f * W:e], ps[:, 0:e - f * W], ACT.Silu).then_inc(a_emptied, 1)

            def evac_zdt(n, b, c):
                ps = a_wait(act, a_filled, n, ("zdt", c), 1)
                if c == 0:
                    wait(act, gated, before(n), NC, 0)
                    wait(act, softplus_step, before(n), SP_STEPS, 0)
                nc.scalar.activation(A.zdt[b][:, c, :], ps[:, 0:ZQ + H], ACT.Copy).then_inc(a_emptied, 1)

            def silu_q(n, b):
                a_wait(act, a_emptied, n, ("zdt", 1), 1)
                z = A.zdt[b][:, :, 0:ZQ]
                nc.scalar.activation(z, z, ACT.Silu).then_inc(siluq_done, 1)

            def evac_x(n, u, c):
                for f in range(2):
                    ps = t_wait(act, t_filled, n, ("x", c, f), 1)
                    if f == 0:
                        wait(act, ydiag_done, u, 2 * NC, 2 * c)
                        wait(act, state_done, u, 2 * NC, 2 * c)
                        wait(act, Xdec_done, u, NC, c)
                        wait(act, XD_done, u, NC, c)
                    nc.scalar.activation(A.X[:, f * W:(f + 1) * W], ps[:, 0:W], ACT.Copy).then_inc(t_emptied, 1)

            def evac_B(n, u, c):
                ps = t_wait(act, t_filled, n, ("x", c, 2), 1)
                wait(act, state_done, u, 2 * NC, 2 * c)
                nc.scalar.activation(A.Btok[:], ps[:, 0:P], ACT.Copy).then_inc(t_emptied, 1)

            def evac_g(n, u, c):
                ps = t_wait(act, t_filled, n, ("g", c, 0), 1)
                if c:
                    a_wait(act, a_filled, n, ("out", 0), 1)
                elif u != 0:
                    a_wait(act, a_filled, u, ("out", 1), 1)
                nc.scalar.activation(A.gThi[:, :, :].rearrange("p k t -> p (k t)"), ps[:, 0:W], ACT.Copy) \
                    .then_inc(ghi_done, 1)
                ps = t_wait(act, t_filled, n, ("g", c, 1), 1)
                wait(act, glo_done, u, NC, c + 1)
                nc.scalar.activation(A.gT[:, :, :].rearrange("p k t -> p (k t)"), ps[:, 0:W], ACT.Copy) \
                    .then_inc(t_emptied, 2)

            def exp_sums(u):
                wait(act, sums_step, u, 3, 3)
                wait(act, S_step, u, 4 * NC, 0)
                wait(act, Xdec_done, u, NC, 0)
                wait(act, yoff_read, u, 2 * NC, 0)
                nc.scalar.activation(A.e3[:], A.s3[:], ACT.Exp).then_inc(e3_done, 1)

            def exp_decay(u, c, f):
                wait(act, diff_done, u, 2 * NC, 2 * c + f + 1)
                x = A.L[c][:, f * HH:(f + 1) * HH, :]
                nc.scalar.activation(x, x, ACT.Exp).then_inc(decay_done, 1)

            def exp_dt(n):
                wait(act, softplus_step, n, SP_STEPS, 2)
                nc.scalar.activation(A.sp[1][:], A.sp[1][:], ACT.Exp).then_inc(edt_done, 1)

            def square(u, c):
                wait(act, gated, u, NC, c + 1)
                wait(act, rs_step, u, 2 * NC, 2 * c + 2 - 2 * NC)
                nc.scalar.activation(A.XD[:], A.yt[:], ACT.Square, accum_out=A.ssq[:, c:c + 1]).then_inc(sq_done, 1)

            def scale_out(n, u, c):
                ps = a_wait(act, a_filled, n, ("out", c), 1)
                wait(act, rs_step, u, 2 * NC, 2 * c + 2)
                wait(act, out_step, u, 2 * NC, 2 * c)
                nc.scalar.activation(A.ob[:], ps[:], ACT.Identity, scale=A.rs[:, c:c + 1]).then_inc(a_emptied, 1)

            def turn(n, b):
                u = before(n)
                own, bef, nxt = has_own(n), has_before(n), has_next(n)
                if own:
                    evac_zdt(n, b, 0)
                if bef:
                    evac_x(n, u, 0)
                if own:
                    evac_zdt(n, b, 1)
                if bef:
                    evac_B(n, u, 0)
                if own:
                    evac_tile(n, b, 0)
                    exp_dt(n)
                    evac_tile(n, b, 1)
                    evac_tile(n, b, 2)
                    evac_tile(n, b, 3)
                    evac_tile(n, b, 4)
                if bef:
                    evac_x(n, u, 1)
                if own:
                    evac_tile(n, b, 5)
                if bef:
                    evac_B(n, u, 1)
                if own:
                    evac_tile(n, b, 6)
                if bef:
                    square(u, 0)
                    evac_g(n, u, 0)
                if own:
                    evac_tile(n, b, 7)
                    evac_tile(n, b, 8)
                widen(n, 0)
                if own:
                    silu_tile(n, b, 0)
                    silu_q(n, b)
                    silu_tile(n, b, 1)
                    silu_tile(n, b, 2)
                if bef:
                    scale_out(n, u, 0)
                if own:
                    silu_tile(n, b, 3)
                    silu_tile(n, b, 4)
                    evac_tile(n, b, 9)
                    silu_tile(n, b, 5)
                if n == 0:
                    setup.scalar_turn0(act)
                if own:
                    silu_z(n, 0)
                    silu_tile(n, b, 6)
                    silu_z(n, 1)
                if bef:
                    square(u, 1)
                    evac_g(n, u, 1)
                if own:
                    silu_z(n, 2)
                    silu_tile(n, b, 7)
                    silu_z(n, 3)
                if nxt:
                    evac_ln(after(n), 1 - b, n)
                if own:
                    widen(n, 1)
                    silu_tile(n, b, 8)
                    silu_tile(n, b, 9)
                    exp_sums(n)
                    exp_decay(n, 0, 0)
                    exp_decay(n, 0, 1)
                    exp_decay(n, 1, 0)
                    exp_decay(n, 1, 1)
                if bef:
                    scale_out(n, u, 1)

            turns(act, lambda: setup.scalar(act, lambda: evac_ln(0, 0, -1)), turn)

        @block.vector
        def _(dve):
            def stats(n, c):
                wait(dve, x_in[c], n, 16, 16)
                wait(dve, rstd_step, n, 2 * NC, 2 * c + 2 - 2 * NC)
                wait(dve, normed, before(n), NC, c + 1)
                wait(dve, stats_step, n, 2 * NC, 2 * c + 2 - 2 * NC)
                nc.vector.bn_stats(A.bst[c][:], A.xl[c][:]).then_inc(stats_step, 1)
                wait_apart(dve, stats_step, n, 2 * NC, 2 * c + 1)
                nc.vector.bn_aggr(A.mv[c][:], A.bst[c][:]).then_inc(stats_step, 1)

            def norm(n, turn_n, c):
                wait(dve, rstd_step, n, 2 * NC, 2 * c + 2)
                nc.vector.tensor_scalar(A.xl[c][:], A.xl[c][:], A.mv[c][:, 0:1], A.rstd[:, c:c + 1],
                                        ALU.subtract, ALU.mult).then_inc(normed, 1)

            def split_h(n, turn_n, c):
                t_wait(dve, t_emptied, turn_n, ("ln", 1), 1)
                if turn_n != -1:
                    a_wait(dve, a_filled, turn_n, ("z", 3), 1)
                wait(dve, split, n, 2 * NC, 2 * c)
                s = slice(c * P, (c + 1) * P)
                h = h32[:, :, s]
                nc.vector.tensor_copy(A.hThi[:, :, s], h).then_inc(split, 1)
                wait(dve, split, n, 2 * NC, 2 * c + 1)
                nc.vector.tensor_tensor(A.hTlo[:, :, s], h, A.hThi[:, :, s].bitcast(F32),
                                        ALU.subtract).then_inc(split, 1)

            def conv(n, b, m):
                a_wait(dve, a_emptied, n, ("m", m), 1)
                for j in range(3):
                    if j:
                        wait(dve, conv_step, n, 3 * MX, 3 * m + j)
                    nc.vector.scalar_tensor_tensor(A.xc[b][:, m, :], A.raw[:, m, j:j + SC], A.wconv[:, m, j:j + 1],
                                                   A.xc[b][:, m, :], ALU.mult, ALU.add).then_inc(conv_step, 1)

            def tails(n, b):
                wait(dve, conv_step, n, 3 * MX, 3 * MX)
                wait(dve, tail_step, n, 2, 0)
                nc.vector.tensor_copy(A.tail[b][:], A.raw[:, :, SC:SC + 3]).then_inc(tail_step, 1)
                nc.vector.tensor_copy(A.raw[:, :, 0:3], A.tail[1 - b][:]).then_inc(tail_step, 1)

            sp0, sp1, sp2, sp3, sp4, sp5 = A.sp

            def dt_first(n, b):
                a_wait(dve, a_emptied, n, ("zdt", 1), 1)
                wait(dve, softplus_step, n, SP_STEPS, 0)
                nc.vector.tensor_tensor(sp0[:], A.zdt[b][:, :, ZQ:ZQ + H],
                                        A.dtb[:].unsqueeze(1).broadcast_to([P, NC, H]), ALU.add) \
                    .then_inc(softplus_step, 1)
                wait(dve, softplus_step, n, SP_STEPS, 1)
                nc.vector.scalar_tensor_tensor(sp1[:], sp0[:], -1.0, sp0[:], ALU.mult, ALU.min) \
                    .then_inc(softplus_step, 1)

            def softplus(n):
                wait(dve, edt_done, n, 1, 1)
                step = [2]

                def did(ins):
                    ins.then_inc(softplus_step, 1)
                    step[0] += 1
                    wait(dve, softplus_step, n, SP_STEPS, step[0])

                did(nc.vector.tensor_scalar(sp2[:], sp1[:], 2.0, None, ALU.add))
                did(nc.vector.reciprocal(sp2[:], sp2[:]))
                did(nc.vector.tensor_tensor(sp3[:], sp1[:], sp2[:], ALU.mult))
                did(nc.vector.tensor_tensor(sp4[:], sp3[:], sp3[:], ALU.mult))
                did(nc.vector.tensor_scalar(sp5[:], sp4[:], 1.0 / 15.0, None, ALU.mult))
                for k in (13, 11, 9, 7, 5, 3):
                    did(nc.vector.scalar_tensor_tensor(sp5[:], sp5[:], 1.0 / k, sp4[:], ALU.add, ALU.mult))
                did(nc.vector.scalar_tensor_tensor(sp5[:], sp5[:], 1.0, sp3[:], ALU.add, ALU.mult))
                did(nc.vector.tensor_scalar(sp0[:], sp0[:], 0.0, None, ALU.max))
                did(nc.vector.scalar_tensor_tensor(sp5[:], sp5[:], 2.0, sp0[:], ALU.mult, ALU.add))
                nc.vector.tensor_tensor(A.a[:], sp5[:], A.negA[:].unsqueeze(1).broadcast_to([P, NC, H]),
                                        ALU.mult).then_inc(softplus_step, 1)

            def sums(n):
                wait(dve, cs_done, n, 1, 1)
                wait(dve, e3_done, n, 1, 0)
                wait(dve, cs_out, n, 16, 0)
                wait(dve, diff_done, n, 2 * NC, 0)
                nc.vector.tensor_copy(A.s3[:, 0:2 * NC * H], small[:, 0:2 * NC * H]).then_inc(sums_step, 1)
                wait(dve, sums_step, n, 3, 1)
                nc.vector.tensor_tensor(A.s3[:, 2 * NC * H:3 * NC * H], A.s3[:, NC * H:2 * NC * H],
                                        A.s3[:, 0:NC * H], ALU.subtract).then_inc(sums_step, 1)
                nc.vector.tensor_copy(A.csT[:], small[0:NC * H, 2 * P:3 * P]).then_inc(sums_step, 1)

            def diff(u, c, f):
                if f == 0:
                    wait(dve, cs_in[c], u, 16, 16)
                    wait(dve, sums_step, u, 3, 3)
                for h in range(f * HH, (f + 1) * HH):
                    last = nc.vector.tensor_scalar(A.L[c][:, h, :], A.L[c][:, h, :], A.s3[:, c * H + h:c * H + h + 1],
                                                   0.0, ALU.subtract, ALU.min)
                last.then_inc(diff_done, 1)

            def mask_G(u):
                wait(dve, G_done, u, 1, 1)
                wait(dve, M_done, u, 2 * NC, 0)
                nc.vector.tensor_tensor(A.Gm[:], small[:, 0:NC * P].rearrange("p (c l) -> p c l", c=NC),
                                        A.triu[:].unsqueeze(1).broadcast_to([P, NC, P]), ALU.mult).then_inc(G_masked, 1)

            def scores(u, c, f):
                if c == 0 and f == 0:
                    wait(dve, G_masked, u, 1, 1)
                wait(dve, decay_done, u, 2 * NC, 2 * c + f + 1)
                x = A.L[c][:, f * HH:(f + 1) * HH, :]
                nc.vector.tensor_tensor(x, x, A.Gm[:, c, :].unsqueeze(1).broadcast_to([P, HH, P]), ALU.mult) \
                    .then_inc(M_done, 1)

            def e3(kind, c, f):
                o = kind * NC * H + c * H + f * HH
                return A.e3[:, o:o + HH].unsqueeze(2).broadcast_to([P, HH, HD])

            def heads(x, f):
                return x[:, f * W:(f + 1) * W].rearrange("p (h d) -> p h d", h=HH)

            def decay_X(n, u, c):
                t_wait(dve, t_emptied, n, ("x", c, 1), 1)
                wait(dve, e3_done, u, 1, 1)
                wait(dve, ydiag_done, u, 2 * NC, 2 * c + 2)
                wait(dve, XD_done, u, NC, c + 1)
                o = 2 * NC * H + c * H
                nc.vector.tensor_tensor(A.X[:].rearrange("p (h d) -> p h d", h=H),
                                        A.X[:].rearrange("p (h d) -> p h d", h=H),
                                        A.e3[:, o:o + H].unsqueeze(2).broadcast_to([P, H, HD]),
                                        ALU.mult).then_inc(Xdec_done, 1)

            def read_yoff(n, u, b, c, f):
                wait(dve, yoff_done, u, 2 * NC, 2 * c + f + 1)
                if f == 0:
                    if c:
                        t_wait(dve, t_filled, n, ("g", 0, 1), 1)
                    elif u != 0:
                        t_wait(dve, t_filled, u, ("g", 1, 1), 1)
                    wait(dve, sq_done, u, NC, c)
                    wait(dve, e3_done, u, 1, 1)
                nc.vector.tensor_tensor(heads(A.yt, f), yoff[:, 0:W].rearrange("p (h d) -> p h d", h=HH), e3(0, c, f),
                                        ALU.mult).then_inc(yoff_read, 1)
                nc.vector.tensor_tensor(heads(A.S[1 - b], f), heads(A.S[1 - b], f), e3(1, c, f),
                                        ALU.mult).then_inc(S_step, 1)

            def read_ydiag(u, c, f):
                wait(dve, ydiag_done, u, 2 * NC, 2 * c + f + 1)
                wait(dve, XD_done, u, NC, c + 1)
                nc.vector.tensor_tensor(A.XD[:, f * W:(f + 1) * W], ydiag[:, 0:W], A.XD[:, f * W:(f + 1) * W],
                                        ALU.add).then_inc(ydiag_read, 1)

            def read_state(u, b, c, f):
                wait(dve, state_done, u, 2 * NC, 2 * c + f + 1)
                wait(dve, S_step, u, 4 * NC, 4 * c + 2)
                s = A.S[1 - b][:, f * W:(f + 1) * W]
                nc.vector.tensor_tensor(s, state[:, 0:W], s, ALU.add).then_inc(S_step, 1)

            def low_g(n, u, c):
                wait(dve, ghi_done, u, NC, c + 1)
                ps = t_wait(dve, t_filled, n, ("g", c, 0), 1)
                nc.vector.tensor_tensor(A.gTlo[:, :, :].rearrange("p k t -> p (k t)"), ps[:, 0:W],
                                        A.gThi[:, :, :].rearrange("p k t -> p (k t)").bitcast(F32),
                                        ALU.subtract).then_inc(glo_done, 1)

            def measure(n, s):
                wait(dve, widened, n, 2, s + 1)
                wait(dve, measured, n, 4, 2 * s)
                nc.vector.tensor_reduce(A.wm1[:], A.wst[:], AX_X, ALU.max, apply_absolute_value=True) \
                    .then_inc(measured, 1)
                wait(dve, measured, n, 4, 2 * s + 1)
                nc.vector.tensor_tensor(T.wtop[:], T.wtop[:], A.wm1[:], ALU.max).then_inc(measured, 1)

            def normalise():
                for c in range(NC):
                    stats(0, c)
                for c in range(NC):
                    norm(0, -1, c)

            def prologue():
                setup.vector(dve, normalise, lambda: [split_h(0, -1, c) for c in range(NC)])

            def turn(n, b):
                u = before(n)
                own, bef, nxt = has_own(n), has_before(n), has_next(n)
                if bef:
                    mask_G(u)
                    scores(u, 0, 0)
                    read_yoff(n, u, b, 0, 0)
                    scores(u, 0, 1)
                if own:
                    dt_first(n, b)
                if bef:
                    scores(u, 1, 0)
                    scores(u, 1, 1)
                    read_ydiag(u, 0, 0)
                    read_yoff(n, u, b, 0, 1)
                if own:
                    conv(n, b, 0)
                if bef:
                    read_ydiag(u, 0, 1)
                    decay_X(n, u, 0)
                if own:
                    conv(n, b, 1)
                if bef:
                    read_state(u, b, 0, 0)
                if own:
                    conv(n, b, 2)
                if bef:
                    read_state(u, b, 0, 1)
                if own:
                    softplus(n)
                    conv(n, b, 3)
                if n == 0:
                    setup.vector_turn0(dve, 0)
                if own:
                    sums(n)
                if bef:
                    low_g(n, u, 0)
                    read_yoff(n, u, b, 1, 0)
                if own:
                    conv(n, b, 4)
                    conv(n, b, 5)
                if bef:
                    read_ydiag(u, 1, 0)
                measure(n, 0)
                if nxt:
                    stats(after(n), 0)
                    stats(after(n), 1)
                if own:
                    conv(n, b, 6)
                if bef:
                    read_yoff(n, u, b, 1, 1)
                    read_ydiag(u, 1, 1)
                    decay_X(n, u, 1)
                if nxt:
                    norm(after(n), n, 0)
                    norm(after(n), n, 1)
                if own:
                    conv(n, b, 7)
                if bef:
                    read_state(u, b, 1, 0)
                if own:
                    conv(n, b, 8)
                if bef:
                    read_state(u, b, 1, 1)
                    low_g(n, u, 1)
                if own:
                    conv(n, b, 9)
                    tails(n, b)
                if n == 0:
                    setup.vector_turn0(dve, 1)
                if own:
                    diff(n, 0, 0)
                    diff(n, 0, 1)
                    diff(n, 1, 0)
                    diff(n, 1, 1)
                if nxt:
                    split_h(after(n), n, 0)
                    split_h(after(n), n, 1)
                if own:
                    measure(n, 1)

            turns(dve, prologue, turn)

        @block.tensor
        def _(pe):
            def transpose_ln(n, turn_n):
                for j in range(2):
                    ps = t_wait(pe, t_emptied, turn_n, ("ln", j), -1)
                    for c in range(NC):
                        if j == 0:
                            wait(pe, normed, n, NC, c + 1)
                        for q in range(2):
                            k = 2 * j + q
                            mm = nc.tensor.transpose(ps[:, q * SC + c * P:q * SC + (c + 1) * P],
                                                     A.xl[c][:, k * P:(k + 1) * P], A.ident[:])
                    mm.then_inc(t_filled, 1)

            def product(out, pairs, parts):
                last = len(pairs) * len(parts) - 1
                i = 0
                for wp, ap in parts:
                    for lhs, rhs in pairs:
                        mm = nc.tensor.matmul(out, lhs(wp, ap), rhs(wp, ap), start=(i == 0), stop=(i == last))
                        i += 1
                return mm

            def project_zdt(n, c):
                if c == 0:
                    wait(pe, split, n, 2 * NC, 2 * NC)
                ps = a_wait(pe, a_emptied, n, ("zdt", c), -1)
                s = slice(c * P, (c + 1) * P)
                mm = product(ps[:, 0:ZQ + H],
                             [(lambda w, a, k=k: hT[a][:, k, s], lambda w, a, k=k: Win[w][:, k, Z:Z + ZQ + H])
                              for k in range(KD)], PARTS)
                mm.then_inc(a_filled, 1)

            def project_tile(n, m):
                ps = a_wait(pe, a_emptied, n, ("m", m), -1)
                o = X0 + m * P
                mm = product(ps[:, 0:SC],
                             [(lambda w, a, k=k: Win[w][:, k, o:o + P], lambda w, a, k=k: hT[a][:, k, :])
                              for k in range(KD)], PARTS)
                mm.then_inc(a_filled, 1)

            def project_z(n, j):
                ps = a_wait(pe, a_emptied, n, ("z", j), -1)
                c, f = divmod(j, 2)
                s = slice(c * P, (c + 1) * P)
                o, e = f * W, min((f + 1) * W, Z)
                mm = product(ps[:, 0:e - o],
                             [(lambda w, a, k=k: hT[a][:, k, s], lambda w, a, k=k: Win[w][:, k, o:e])
                              for k in range(KD)], PARTS)
                mm.then_inc(a_filled, 1)

            def scores_G(n, u, b):
                wait(pe, silu_done, u, MX, MX)
                wait(pe, sums_step, n, 3, 0)
                for c in range(NC):
                    s = slice(c * P, (c + 1) * P)
                    mm = nc.tensor.matmul(small[:, c * P:(c + 1) * P], A.xc[1 - b][:, MX - 2, s],
                                          A.xc[1 - b][:, MX - 1, s], start=True, stop=True)
                mm.then_inc(G_done, 1)

            def cumulate(n):
                wait(pe, softplus_step, n, SP_STEPS, SP_STEPS)
                wait(pe, G_masked, n, 1, 0)
                a = A.a[:, :, :].rearrange("p c h -> p (c h)")
                nc.tensor.matmul(small[:, 0:NC * H], A.triu[:], a, start=True, stop=True)
                nc.tensor.matmul(small[:, NC * H:2 * NC * H], A.ones[:], a, start=True, stop=True)
                mm = nc.tensor.matmul(small[0:NC * H, 2 * P:3 * P], a, A.triu[:], start=True, stop=True)
                mm.then_inc(cs_done, 1)

            def transpose_x(n, u, b, c):
                s = slice(c * P, (c + 1) * P)
                for f in range(2):
                    ps = t_wait(pe, t_emptied, n, ("x", c, f), -1)
                    for q in range(4):
                        mm = nc.tensor.transpose(ps[:, q * P:(q + 1) * P], A.xc[1 - b][:, 4 * f + q, s], A.ident[:])
                    mm.then_inc(t_filled, 1)

            def transpose_B(n, u, b, c):
                s = slice(c * P, (c + 1) * P)
                ps = t_wait(pe, t_emptied, n, ("x", c, 2), -1)
                nc.tensor.transpose(ps[:, 0:P], A.xc[1 - b][:, MX - 2, s], A.ident[:]).then_inc(t_filled, 1)

            def y_off(u, b, c, f):
                s = slice(c * P, (c + 1) * P)
                wait(pe, yoff_read, u, 2 * NC, 2 * c + f)
                if c:
                    wait(pe, S_step, u, 4 * NC, 4 * c)
                else:
                    wait(pe, S_step, before(u), 4 * NC, 0)
                nc.tensor.matmul(yoff[:, 0:W], A.xc[1 - b][:, MX - 1, s], A.S[1 - b][:, f * W:(f + 1) * W],
                                 start=True, stop=True).then_inc(yoff_done, 1)

            def y_diag(n, u, c, f):
                wait(pe, M_done, u, 2 * NC, 2 * c + f + 1)
                t_wait(pe, t_emptied, n, ("x", c, f), 1)
                wait(pe, ydiag_read, u, 2 * NC, 2 * c + f)
                for h in range(HH):
                    g = f * HH + h
                    mm = nc.tensor.matmul(ydiag[:, h * HD:(h + 1) * HD], A.L[c][:, g, :],
                                          A.X[:, g * HD:(g + 1) * HD], start=True, stop=True)
                mm.then_inc(ydiag_done, 1)

            def states(n, u, c, f):
                wait(pe, Xdec_done, u, NC, c + 1)
                t_wait(pe, t_emptied, n, ("x", c, 2), 1)
                if f:
                    wait(pe, S_step, u, 4 * NC, 4 * c + 3)
                else:
                    wait(pe, S_step, u, 4 * NC, 4 * c)
                nc.tensor.matmul(state[:, 0:W], A.Btok[:], A.X[:, f * W:(f + 1) * W],
                                 start=True, stop=True).then_inc(state_done, 1)

            def transpose_g(n, u, c):
                wait(pe, gated, u, NC, c + 1)
                for f in range(2):
                    ps = t_wait(pe, t_emptied, n, ("g", c, f), -1)
                    for q in range(4):
                        k = 4 * f + q
                        mm = nc.tensor.transpose(ps[:, q * P:(q + 1) * P], A.yt[:, k * P:(k + 1) * P], A.ident[:])
                    mm.then_inc(t_filled, 1)

            def project_out(n, u, c):
                t_wait(pe, t_emptied, n, ("g", c, 1), 1)
                wait(pe, glo_done, u, NC, c + 1)
                if n == 1:
                    pe.wait_ge(setup.wout_scaled, KI)
                    pe.wait_ge(setup.wout_low, KH)
                ps = a_wait(pe, a_emptied, n, ("out", c), -1)
                for k in range(KH):
                    for i, (wp, gp) in enumerate(PARTS):
                        nc.tensor.matmul(ps[:], gT[gp][:, k, :], Wo[wp][:, k, :], start=(k == 0 and i == 0), stop=False)
                for k in range(KI - KH):
                    mm = nc.tensor.matmul(ps[:], A.gT[:, k, :], A.Wo[:, k, :], start=False, stop=(k == KI - KH - 1))
                mm.then_inc(a_filled, 1)

            def turn(n, b):
                u = before(n)
                own, bef, nxt = has_own(n), has_before(n), has_next(n)
                if bef:
                    scores_G(n, u, b)
                    y_off(u, b, 0, 0)
                if own:
                    project_zdt(n, 0)
                if bef:
                    transpose_x(n, u, b, 0)
                if own:
                    project_zdt(n, 1)
                if bef:
                    transpose_B(n, u, b, 0)
                    y_off(u, b, 0, 1)
                if own:
                    project_tile(n, 0)
                if bef:
                    y_diag(n, u, 0, 0)
                if own:
                    project_tile(n, 1)
                if bef:
                    y_diag(n, u, 0, 1)
                if own:
                    project_tile(n, 2)
                    project_tile(n, 3)
                if n == 0:
                    setup.tensor_turn0(pe, 0)
                if bef:
                    states(n, u, 0, 0)
                if own:
                    project_tile(n, 4)
                if bef:
                    states(n, u, 0, 1)
                    transpose_x(n, u, b, 1)
                if own:
                    project_tile(n, 5)
                if bef:
                    transpose_B(n, u, b, 1)
                    y_off(u, b, 1, 0)
                if own:
                    project_tile(n, 6)
                    cumulate(n)
                if bef:
                    y_diag(n, u, 1, 0)
                    transpose_g(n, u, 0)
                if own:
                    project_tile(n, 7)
                    project_tile(n, 8)
                if bef:
                    project_out(n, u, 0)
                    y_off(u, b, 1, 1)
                    y_diag(n, u, 1, 1)
                if own:
                    project_tile(n, 9)
                if n == 0:
                    setup.tensor_turn0(pe, 1)
                if own:
                    project_z(n, 0)
                if bef:
                    states(n, u, 1, 0)
                if own:
                    project_z(n, 1)
                if bef:
                    states(n, u, 1, 1)
                    transpose_g(n, u, 1)
                if own:
                    project_z(n, 2)
                    project_z(n, 3)
                if nxt:
                    transpose_ln(after(n), n)
                if bef:
                    project_out(n, u, 1)

            turns(pe, lambda: setup.tensor(pe, lambda: transpose_ln(0, -1)), turn)


def feed_forward_stage(nc, T, B):
    D, HID = T.D, T.HID
    KD, KH = D // P, HID // P
    SC = T.SC2
    NC = SC // P
    N = 2 * T.S // SC
    with ExitStack() as ctx:
        sem = lambda name: ctx.enter_context(nc.semaphore(name))
        resid_in = sem("ff_resid_in")
        x_in, out_sent = ([sem(f"{s}{c}") for c in range(NC)] for s in ("ff_x_in", "ff_out_sent"))
        t_filled, t_emptied = sem("ff_t_filled"), sem("ff_t_emptied")
        gate_done, up_done, down_done, gate_read, hid_step = (
            sem(s) for s in ("gate_done", "up_done", "down_done", "gate_read", "hid_step"))
        stats_step, rstd_step, normed, split, down_read, summed = (
            sem(s) for s in ("ff_stats_step", "ff_rstd_step", "ff_normed", "ff_split", "down_read", "summed"))
        flag_step, flag_turned = sem("flag_step"), sem("flag_turned")
        rows_spread, rows_done, rows_read = sem("ff_rows_spread"), sem("ff_rows_done"), sem("ff_rows_read")
        tps, gates, ups, downs = B.psum[0:2], B.psum[2:4], B.psum[4:6], B.psum[6:8]
        HID_GROUPS = ((0, 1), (1, 3), (3, 7), (7, KH))
        DOWN_GROUPS = ((0, KH // 2), (KH // 2, KH))
        hid_w_in = [sem(f"hid_w_in{g}") for g in range(len(HID_GROUPS))]
        down_w_in = [sem(f"down_w_in{g}") for g in range(len(DOWN_GROUPS))]
        w_rows = T.wf.shape[0] // 3
        w_flat = [T.wf[j * w_rows:(j + 1) * w_rows, :].rearrange("a b -> (a b)") for j in range(3)]
        wg_d, wu_d = (w.rearrange("(k p n) -> p k n", p=P, n=HID) for w in w_flat[0:2])
        wd_d = w_flat[2].rearrange("(k p n) -> p k n", p=P, n=D)
        LN_AT = {7: range(0, KD // 2), 8: range(KD // 2, KD)}
        block = ctx.enter_context(nc.Block())

        def turns(engine, prologue, turn):
            prologue()
            turn(0, 0)
            pairs = (N - 2) // 2
            with engine.Fori(0, pairs) as i:
                turn((i, 2, 1), 1)
                turn((i, 2, 2), 0)
            for n in range(1 + 2 * pairs, N):
                turn(n, n % 2)

        def has_next(n):
            return not (isinstance(n, int) and n == N - 1)

        @block.sync
        def _(sp):
            def rows(t, b, n, c):
                return t[b][bass.ds(start_token(n, SC) + c * P, P), :]

            def load_x(n, b):
                for c in range(NC):
                    wait_apart(sp, normed, before(n), NC, c + 1)
                    sp.dma_start(B.xl[c][:], rows(T.x1, b, n, c)).then_inc(x_in[c], 16)

            def turn(n, b):
                if has_next(n):
                    load_x(after(n), 1 - b)
                for c in range(NC):
                    wait_apart(sp, out_sent[c], n, 16, 0)
                    sp.dma_start(B.xr[c][:], rows(T.x1, b, n, c)).then_inc(resid_in, 16)
                for c in range(NC):
                    wait_apart(sp, summed, n, NC, c + 1)
                    sp.dma_start(rows(T.out, b, n, c), B.xr[c][:]).then_inc(out_sent[c], 16)

            turns(sp, lambda: load_x(0, 0), turn)
            for c in range(NC):
                sp.wait_ge(out_sent[c], N * 16)

        @block.gpsimd
        def _(pool):
            def rstd(n):
                for c in range(NC):
                    wait(pool, stats_step, n, 2 * NC, 2 * (c + 1))
                    wait_apart(pool, normed, before(n), NC, c + 1)
                    nc.gpsimd.tensor_scalar(B.rstd[:, c:c + 1], B.mv[c][:, 1:2], 1.0, EPS, ALU.mult, ALU.add) \
                        .then_inc(rstd_step, 1)
                    wait(pool, rstd_step, n, 2 * NC, 2 * c + 1)
                    nc.gpsimd.tensor_tensor(B.rstd[:, c:c + 1], B.rstd[:, c:c + 1], T.neg_half[:], ALU.pow) \
                        .then_inc(rstd_step, 1)

            def turn(n, b):
                if has_next(n):
                    rstd(after(n))
                for c in range(NC):
                    wait(pool, down_read, n, NC, c + 1)
                    wait(pool, resid_in, n, NC * 16, NC * 16)
                    nc.gpsimd.tensor_tensor(B.xr[c][:], B.ob[c % 2][:], B.xr[c][:], ALU.add).then_inc(summed, 1)

            turns(pool, lambda: rstd(0), turn)

        @block.scalar
        def _(act):
            def evac_ln(n, b, tiles):
                for k in tiles:
                    wait(act, t_filled, n, KD, k + 1)
                    if k == 0:
                        wait(act, split, n, 2 * KD, 0)
                    nc.scalar.activation(B.h32[:, k, :], tps[k % 2][:], ACT.Identity, bias=T.modc[:, 2, k, b:b + 1],
                                         scale=T.modc[:, 3, k, b:b + 1]).then_inc(t_emptied, 1)

            def turn(n, b):
                for m in range(KH):
                    wait(act, gate_done, n, KH, m + 1)
                    wait(act, hid_step, n, 3 * KH, 3 * (m - 2) + 1)
                    nc.scalar.activation(B.sg[m % 2][:], gates[m % 2][:], ACT.Silu, scale=T.sgate[:, m:m + 1]) \
                        .then_inc(gate_read, 1)
                    if m in LN_AT and has_next(n):
                        evac_ln(after(n), 1 - b, LN_AT[m])

            def prologue():
                for g, (m0, m1) in enumerate(HID_GROUPS):
                    s = slice(m0 * P, m1 * P)
                    for w, src in ((B.Wg, wg_d), (B.Wu, wu_d)):
                        act.dma_start(w[:, :, s].bitcast(F32), src[:, :, s]).then_inc(hid_w_in[g], 16)
                for g, (m0, m1) in enumerate(DOWN_GROUPS):
                    act.dma_start(B.Wd[:, m0:m1, :].bitcast(F32), wd_d[:, m0:m1, :]).then_inc(down_w_in[g], 16)
                evac_ln(0, 0, range(KD))

            turns(act, prologue, turn)

        @block.vector
        def _(dve):
            def stats(n, c):
                wait(dve, x_in[c], n, 16, 16)
                wait(dve, rstd_step, n, 2 * NC, 2 * c + 2 - 2 * NC)
                wait(dve, normed, before(n), NC, c + 1)
                wait(dve, stats_step, n, 2 * NC, 2 * c + 2 - 2 * NC)
                nc.vector.bn_stats(B.bst[c][:], B.xl[c][:]).then_inc(stats_step, 1)
                wait_apart(dve, stats_step, n, 2 * NC, 2 * c + 1)
                nc.vector.bn_aggr(B.mv[c][:], B.bst[c][:]).then_inc(stats_step, 1)

            def norm(n, c):
                wait(dve, rstd_step, n, 2 * NC, 2 * c + 2)
                wait(dve, t_filled, n, KD, 0)
                nc.vector.tensor_scalar(B.hn[c][:], B.xl[c][:], B.mv[c][:, 0:1], B.rstd[:, c:c + 1],
                                        ALU.subtract, ALU.mult).then_inc(normed, 1)

            def split_h(n):
                for k in range(KD):
                    wait(dve, t_emptied, n, KD, k + 1)
                    if k == 0:
                        wait(dve, up_done, n, KH, 0)
                        wait(dve, split, n, 2 * KD, 0)
                    nc.vector.tensor_copy(B.hThi[:, k, :], B.h32[:, k, :]).then_inc(split, 1)
                    wait(dve, split, n, 2 * KD, 2 * k + 1)
                    nc.vector.tensor_tensor(B.hTlo[:, k, :], B.h32[:, k, :], B.hThi[:, k, :].bitcast(F32),
                                            ALU.subtract).then_inc(split, 1)

            def hidden(n, m):
                wait(dve, gate_read, n, KH, m + 1)
                wait(dve, up_done, n, KH, m + 1)
                wait(dve, hid_step, n, 3 * KH, 3 * (m - 1))
                if m == 0:
                    wait(dve, down_done, n, NC, 0)
                nc.vector.scalar_tensor_tensor(B.hid[m % 2][:], ups[m % 2][:], T.sup[:, m:m + 1], B.sg[m % 2][:],
                                               ALU.mult, ALU.mult).then_inc(hid_step, 1)
                wait(dve, hid_step, n, 3 * KH, 3 * m + 1)
                nc.vector.tensor_copy(B.hidhi[:, m, :], B.hid[m % 2][:]).then_inc(hid_step, 1)
                wait(dve, hid_step, n, 3 * KH, 3 * m + 2)
                nc.vector.tensor_tensor(B.hidlo[:, m, :], B.hid[m % 2][:], B.hidhi[:, m, :].bitcast(F32),
                                        ALU.subtract).then_inc(hid_step, 1)

            def prologue():
                for b in range(2):
                    spread_gate(nc, dve, B.hid[b][:].rearrange("p (k j) -> p k j", k=KD), T.gate2c[:, :, b],
                                rows_spread)
                dve.wait_ge(flag_turned, 1)
                nc.vector.tensor_reduce(B.top1[:], gates[0][0:1, 0:P], AX_X, ALU.max).then_inc(flag_step, 1)
                dve.wait_ge(flag_step, 1)
                nc.vector.tensor_scalar(B.flag[:], B.top1[:], EXACT_INT, None, ALU.is_gt).then_inc(flag_step, 1)
                for c in range(NC):
                    stats(0, c)
                for c in range(NC):
                    norm(0, c)
                for b in range(2):
                    dve.wait_ge(rows_done, b + 1)
                    nc.vector.tensor_copy(B.gate_row[b][:], downs[b][:]).then_inc(rows_read, 1)
                split_h(0)
                dve.wait_ge(rows_read, 2)

            def turn(n, b):
                for m in range(KH):
                    hidden(n, m)
                    if has_next(n) and 1 <= m <= NC:
                        stats(after(n), m - 1)
                        if m == NC:
                            for c in range(NC):
                                norm(after(n), c)
                if has_next(n):
                    split_h(after(n))
                for c in range(NC):
                    wait(dve, down_done, n, NC, c + 1)
                    wait(dve, summed, n, NC, c - 1)
                    nc.vector.tensor_tensor(B.ob[c % 2][:], downs[c % 2][:], B.gate_row[b][:], ALU.mult) \
                        .then_inc(down_read, 1)

            turns(dve, prologue, turn)

        @block.tensor
        def _(pe):
            def transpose_ln(n, tiles):
                for k in tiles:
                    wait(pe, t_emptied, n, KD, k - 1)
                    if k == 0:
                        wait(pe, normed, n, NC, NC)
                    for c in range(NC):
                        mm = nc.tensor.transpose(tps[k % 2][:, c * P:(c + 1) * P], B.hn[c][:, k * P:(k + 1) * P],
                                                 B.ident[:])
                    mm.then_inc(t_filled, 1)

            def program(dt):

                def project(ps, W, m):
                    for k in range(KD):
                        for a, h in enumerate((B.hThi, B.hTlo)):
                            mm = nc.tensor.matmul(ps[:], W[:, k, m * P:(m + 1) * P].bitcast(dt),
                                                  h[:, k, :].bitcast(dt),
                                                  start=(k == 0 and a == 0), stop=(k == KD - 1 and a == 1))
                    return mm

                def turn(n, b):
                    wait(pe, split, n, 2 * KD, 2 * KD)
                    for m in range(KH):
                        if n == 0:
                            for g, (m0, m1) in enumerate(HID_GROUPS):
                                if m == m0:
                                    pe.wait_ge(hid_w_in[g], 32)
                        wait(pe, gate_read, n, KH, m - 1)
                        project(gates[m % 2], B.Wg, m).then_inc(gate_done, 1)
                        wait(pe, hid_step, n, 3 * KH, 3 * (m - 2) + 1)
                        project(ups[m % 2], B.Wu, m).then_inc(up_done, 1)
                        if m in LN_AT and has_next(n):
                            transpose_ln(after(n), LN_AT[m])
                    if n == 0:
                        for g in range(len(DOWN_GROUPS)):
                            pe.wait_ge(down_w_in[g], 16)
                        pe.wait_ge(rows_read, 2)
                    for c in range(NC):
                        wait(pe, down_read, n, NC, c - 1)
                        s = slice(c * P, (c + 1) * P)
                        for m in range(KH):
                            if c == 0:
                                wait(pe, hid_step, n, 3 * KH, 3 * (m + 1))
                            for a, h in enumerate((B.hidhi, B.hidlo)):
                                mm = nc.tensor.matmul(downs[c % 2][:], h[:, m, s].bitcast(dt), B.Wd[:, m, :].bitcast(dt),
                                                      start=(m == 0 and a == 0), stop=(m == KH - 1 and a == 1))
                        mm.then_inc(down_done, 1)

                turns(pe, lambda: transpose_ln(0, range(KD)), turn)

            nc.tensor.transpose(gates[0][0:1, 0:P], T.wtop[:], B.ident[:]).then_inc(flag_turned, 1)
            for b in range(2):
                pe.wait_ge(rows_spread, b + 1)
                for k in range(KD):
                    mm = nc.tensor.matmul(downs[b][:, k * P:(k + 1) * P], B.hid[b][:, k * P:(k + 1) * P], B.ident[:],
                                          start=True, stop=True)
                mm.then_inc(rows_done, 1)
            pe.wait_ge(flag_step, 2)
            wide = pe.value_load(B.flag[0:1, 0:1], min_val=0, max_val=1)
            with pe.If(wide == 0):
                program(FR)
            with pe.Else():
                program(F32)


def adaln_block(nc, T):
    T.D, T.DI, T.CD, T.H, T.HD, T.S, T.HID = 512, 1024, 1280, 16, 64, 2048, 1408
    T.NIN = T.DI + T.CD + T.H
    T.SC, T.SC2 = 256, 512
    T.ZQ = 256
    KD, KI, MX, KH = T.D // P, T.DI // P, T.CD // P, T.HID // P
    NC = T.SC // P
    T.x1 = nc.dram_tensor("x1_scratch", [2, T.S, T.D], F32, kind="Internal").ap()
    T.wf = nc.dram_tensor("widened_scratch", list(T.wq.shape), F32, kind="Internal").ap()
    T.cs_d = nc.dram_tensor("sums_scratch", [NC, T.H, P], F32, kind="Internal").ap()
    with ExitStack() as outer:
        def sb(ctx, name, shape, dt=F32):
            return ctx.enter_context(nc.sbuf_tensor(name, shape, dt))

        psum = [outer.enter_context(nc.psum_tensor(f"bank{i}", [P, 512], F32)) for i in range(8)]
        T.modc = sb(outer, "modc", [P, 4, KD, 2])
        T.neg_half = sb(outer, "neg_half", [P, 1])
        T.gate2c, T.wtop = sb(outer, "gate2_cols", [P, KD, 2]), sb(outer, "wtop", [P, 1])
        T.sgate, T.sup = sb(outer, "sgate", [P, KH]), sb(outer, "sup", [P, KH])
        ident = sb(outer, "ident", [P, P])

        with ExitStack() as ctx:
            A = Tensors()
            A.psum, A.ident = psum, ident
            T.gate_row = [sb(ctx, f"gate_row{b}", [P, T.D]) for b in range(2)]
            A.triu, A.ones = sb(ctx, "triu", [P, P]), sb(ctx, "ones", [P, P])
            A.Whi, A.Wlo = sb(ctx, "W_in_high", [P, KD, T.NIN], FR), sb(ctx, "W_in_low", [P, KD, T.NIN], FR)
            A.Wohi, A.Wolo = (sb(ctx, s, [P, KI // 2, T.D], FR) for s in ("W_out_high", "W_out_low"))
            A.Wo = sb(ctx, "W_out", [P, KI - KI // 2, T.D])
            A.cT, A.sc = sb(ctx, "cT", [P, KD, 2]), sb(ctx, "silu_c", [P, KD, 2])
            A.wconv, A.bconv = sb(ctx, "wconv", [P, MX, 4]), sb(ctx, "bconv", [P, MX])
            A.normw, A.sdown = sb(ctx, "normw", [P, KI]), sb(ctx, "sdown", [P, KD])
            A.gate1c = sb(ctx, "gate1_cols", [P, KD, 2])
            A.gtmp = [sb(ctx, f"gate_sign{i}", [P, KD, 2]) for i in range(2)]
            A.wst, A.wm1 = sb(ctx, "wq_rows", [P, 512]), sb(ctx, "wmax", [P, 1])
            A.dtb, A.negA, A.Drow = sb(ctx, "dt_bias", [P, T.H]), sb(ctx, "negA", [P, T.H]), sb(ctx, "Drow", [P, T.H])
            A.xl = [sb(ctx, f"x_tile{c}", [P, T.D]) for c in range(NC)]
            A.xr = sb(ctx, "x_resid", [P, T.D])
            A.ob = sb(ctx, "branch", [P, T.D])
            A.bst = [sb(ctx, f"bn_stats{c}", [P, 6]) for c in range(NC)]
            A.mv = [sb(ctx, f"mean_var{c}", [P, 2]) for c in range(NC)]
            A.rstd, A.rs, A.ssq = (sb(ctx, s, [P, NC]) for s in ("rstd", "inv_rms", "square_sum"))
            A.hThi, A.hTlo = sb(ctx, "h_high", [P, KD, T.SC], FR), sb(ctx, "h_low", [P, KD, T.SC], FR)
            A.raw = sb(ctx, "conv_in", [P, MX, 3 + T.SC])
            A.tail = [sb(ctx, f"conv_tail{b}", [P, MX, 3]) for b in range(2)]
            A.xc = [sb(ctx, f"xBC{b}", [P, MX, T.SC]) for b in range(2)]
            A.siluz = sb(ctx, "silu_z", [P, NC, T.DI - T.ZQ])
            A.zdt = [sb(ctx, f"z_dt{b}", [P, NC, T.ZQ + T.H]) for b in range(2)]
            A.sp = [sb(ctx, f"softplus{j}", [P, NC, T.H]) for j in range(6)]
            A.a = sb(ctx, "dtA", [P, NC, T.H])
            A.s3, A.e3 = sb(ctx, "sums", [P, 3 * NC * T.H]), sb(ctx, "exp_sums", [P, 3 * NC * T.H])
            A.csT = sb(ctx, "sumsT", [NC * T.H, P])
            A.L = [sb(ctx, f"decay{c}", [P, T.H, P]) for c in range(NC)]
            A.Gm = sb(ctx, "G_masked", [P, NC, P])
            A.X, A.XD = sb(ctx, "X", [P, T.DI]), sb(ctx, "X_D", [P, T.DI])
            A.Btok = sb(ctx, "B_rows", [P, P])
            A.yt = sb(ctx, "y", [P, T.DI])
            A.gThi, A.gTlo = (sb(ctx, s, [P, KI // 2, P], FR) for s in ("gT_high", "gT_low"))
            A.gT = sb(ctx, "gT", [P, KI - KI // 2, P])
            A.S = [sb(ctx, f"state{b}", [P, T.DI]) for b in range(2)]
            A.gsp = [A.X[:, b * T.D:(b + 1) * T.D].rearrange("p (k j) -> p k j", k=KD) for b in range(2)]
            mixer_stage(nc, T, A)

        with ExitStack() as ctx:
            B = Tensors()
            NC2 = T.SC2 // P
            B.psum, B.ident = psum, ident
            B.Wg, B.Wu = sb(ctx, "W_gate", [P, KD, T.HID], FR), sb(ctx, "W_up", [P, KD, T.HID], FR)
            B.Wd = sb(ctx, "W_down", [P, KH, T.D], FR)
            B.top1 = sb(ctx, "top1", [1, 1])
            B.gate_row = [sb(ctx, f"gate2_row{b}", [P, T.D]) for b in range(2)]
            B.flag = sb(ctx, "wide_flag", [1, 1], I32)
            B.xl = [sb(ctx, f"ff_x_tile{c}", [P, T.D]) for c in range(NC2)]
            B.xr = [sb(ctx, f"ff_x_resid{c}", [P, T.D]) for c in range(NC2)]
            B.hn = [sb(ctx, f"ff_normed{c}", [P, T.D]) for c in range(NC2)]
            B.ob = [sb(ctx, f"ff_branch{c}", [P, T.D]) for c in range(2)]
            B.bst = [sb(ctx, f"ff_bn_stats{c}", [P, 6]) for c in range(NC2)]
            B.mv = [sb(ctx, f"ff_mean_var{c}", [P, 2]) for c in range(NC2)]
            B.rstd = sb(ctx, "ff_rstd", [P, NC2])
            B.h32 = sb(ctx, "ff_h", [P, KD, T.SC2])
            B.hThi, B.hTlo = sb(ctx, "ff_h_high", [P, KD, T.SC2], FR), sb(ctx, "ff_h_low", [P, KD, T.SC2], FR)
            B.sg = [sb(ctx, f"silu_gate{j}", [P, T.SC2]) for j in range(2)]
            B.hid = [sb(ctx, f"hidden{j}", [P, T.SC2]) for j in range(2)]
            B.hidhi, B.hidlo = (sb(ctx, s, [P, KH, T.SC2], FR) for s in ("hidden_high", "hidden_low"))
            feed_forward_stage(nc, T, B)


def kernel(**inputs):
    import numpy as np
    import concourse.bacc as bacc
    from concourse.bass_utils import run_bass_kernel_spmd

    nc = bacc.Bacc("TRN2", target_bir_lowering=False, num_devices=1)
    arrays = {}

    def put(name, a):
        a = np.ascontiguousarray(a)
        arrays[name] = a
        return nc.dram_tensor(name, a.shape, mybir.dt.from_np(a.dtype), kind="ExternalInput").ap()

    T = Tensors()
    T.x = put("x", inputs["L0_attn_u"])
    w_in = np.asarray(inputs["L0_attn_W_in"]).T
    h = np.asarray(inputs["L0_attn_dt_bias"]).shape[0]
    di = np.asarray(inputs["L0_attn_norm_w"]).shape[0]
    T.winT = put("W_inT", np.concatenate([w_in[:, :di], w_in[:, -h:], w_in[:, di:-h]], axis=1))
    T.woutT = put("W_outT", np.asarray(inputs["L0_attn_W_out"]).T)
    T.wconv = put("W_conv", inputs["L0_attn_W_conv"])
    T.bconv = put("b_conv", inputs["L0_attn_b_conv"])
    T.dtb = put("dt_bias_in", inputs["L0_attn_dt_bias"])
    T.alog = put("A_log", inputs["L0_attn_A_log"])
    T.Dp = put("Dp", inputs["L0_attn_Dp"])
    T.normw = put("norm_w", inputs["L0_attn_norm_w"])
    wq = [np.ascontiguousarray(np.asarray(inputs[f"L0_ffn_wq_{w}"]).T).reshape(-1, 512) for w in ("gate", "up", "down")]
    T.wq = put("wqT", np.concatenate(wq, axis=0))
    T.sgate_in = put("s_gate", inputs["L0_ffn_s_gate"])
    T.sup_in = put("s_up", inputs["L0_ffn_s_up"])
    T.sdown = put("s_down", inputs["L0_ffn_s_down"])
    T.cT = put("cT_in", np.asarray(inputs["L0_c"]).T)
    T.wmod = put("w_mod", inputs["L0_wmod"])
    T.out = nc.dram_tensor("out", inputs["L0_attn_u"].shape, F32, kind="ExternalOutput").ap()
    adaln_block(nc, T)
    r = run_bass_kernel_spmd(nc, [arrays], core_ids=[0])
    return r.results[0]["out"]
```
